# Optimizing a Trainium2 kernel written in Bass

```python
import numpy as np
import jax
import jax.numpy as jnp

def _softmax(x, axis=-1):
    return jax.nn.softmax(x, axis=axis)

def _gelu(x):
    return jax.nn.gelu(x, approximate=True)

def _silu(x):
    return jax.nn.silu(x)

def _sigmoid(x):
    return jax.nn.sigmoid(x)

def _layernorm(x, axis=-1, eps=1e-05):
    m = jnp.mean(x, axis=axis, keepdims=True)
    v = jnp.var(x, axis=axis, keepdims=True)
    return (x - m) / jnp.sqrt(v + eps)

def _scatter_add(tgt, idx, src, axis=0):
    return tgt.at[idx].add(src)

def _segment_sum(src, seg, n):
    return jax.ops.segment_sum(src, seg, n)
kernel_name = 'mk_decoder_postln_d1_seqx_r4_33bc7c'

def setup_inputs(seed: int=0):
    np.random.seed(seed)
    _w = jnp.asarray

    def _rec_inputs():
        import jax
        import jax.numpy as jnp
        _rk = jax.random.key(seed)
        x = -0.0002928 + 1 * jax.random.normal(jax.random.fold_in(_rk, 1), (16, 256, 256), jnp.float32)
        _lenS = 256 - jax.random.randint(jax.random.fold_in(_rk, 7), (16,), 0, max(1, 256 // 4) + 1, jnp.int32)
        _lenS2 = 77 - jax.random.randint(jax.random.fold_in(_rk, 8), (16,), 0, max(1, 77 // 4) + 1, jnp.int32)
        _ctx_2048P = jax.random.normal(jax.random.fold_in(_rk, 11), (16, 16, 512), jnp.float32)
        _ctx_2048c = jax.random.dirichlet(jax.random.fold_in(_rk, 511), 0.3 * jnp.ones((16,), jnp.float32), (16, 77))
        _ctx_2048t = jnp.einsum('bsk,bkd->bsd', _ctx_2048c, _ctx_2048P)
        _ctx_2048t = _ctx_2048t * jax.lax.rsqrt(jnp.mean(jnp.square(_ctx_2048t)) + 1e-12) * 0.953939
        ctx_2048 = -0.000514642 + 1.00011 * (_ctx_2048t + 0.3 * jax.random.normal(jax.random.fold_in(_rk, 611), (16, 77, 512), jnp.float32))
        return (x, ctx_2048)
    x, ctx_2048 = _rec_inputs()

    def _L0_attn_setup():
        import jax, jax.numpy as jnp
        import numpy as np
        B, N, C, H, W = (2, 512, 256, 16, 8)
        HD = C // H
        SCALE = HD ** (-0.5)

        def band_mask(n, w):
            i = jnp.arange(n)[:, None]
            j = jnp.arange(n)[None, :]
            lo = jnp.where(i <= w, 0, i - w)
            hi = jnp.where(n - i <= w, n - 1, i + w)
            return (j >= lo) & (j <= hi)
        key = jax.random.key(seed)
        k1, k2, k3 = jax.random.split(key, 3)
        x = jax.random.normal(k1, (B, N, C), dtype=jnp.float32)
        Wqkv = jax.random.normal(k2, (C, 3 * C), dtype=jnp.float32) * C ** (-0.5)
        Wproj = jax.random.normal(k3, (C, C), dtype=jnp.float32) * C ** (-0.5)
        bproj = jnp.zeros((C,), dtype=jnp.float32)
        return {'x': x, 'Wqkv': Wqkv, 'Wproj': Wproj, 'bproj': bproj}
    _L0_attn_all = _L0_attn_setup()
    _L0_attn_in = {k: v for k, v in _L0_attn_all.items() if k in ('Wqkv', 'Wproj', 'bproj')}
    del _L0_attn_all

    def _L0_xattn_setup():
        import jax, jax.numpy as jnp
        import numpy as np
        NUM_HEADS = 16
        key = jax.random.key(seed)
        ks = jax.random.split(key, 5)
        dim = 256
        B, N, N_c = (4, 256, 64)
        x = jax.random.normal(ks[0], (B, N, dim), dtype=jnp.float32)
        context = jax.random.normal(ks[1], (B, N_c, 2 * dim), dtype=jnp.float32)
        w_qkv = jax.random.normal(ks[2], (3 * dim, dim), dtype=jnp.float32) * 0.02
        w_proj = jax.random.normal(ks[3], (dim, dim), dtype=jnp.float32) * 0.02
        b_proj = jax.random.normal(ks[4], (dim,), dtype=jnp.float32) * 0.02
        return {'x': x, 'context': context, 'w_qkv': w_qkv, 'w_proj': w_proj, 'b_proj': b_proj}
    _L0_xattn_all = _L0_xattn_setup()
    _L0_xattn_in = {k: v for k, v in _L0_xattn_all.items() if k in ('w_qkv', 'w_proj', 'b_proj')}
    del _L0_xattn_all

    def _L0_ffn_setup():
        import jax, jax.numpy as jnp
        import numpy as np
        TOP_K = 2
        NUM_EXPERTS = 8
        B, T, H, F = (4, 512, 256, 1024)
        key = jax.random.key(seed)
        ks = jax.random.split(key, 6)
        s_in = 1.0 / np.sqrt(H)
        s_ff = 1.0 / np.sqrt(F)
        return {'x': jax.random.normal(ks[0], (B, T, H), dtype=jnp.float32), 'router_w': jax.random.normal(ks[1], (NUM_EXPERTS, H), dtype=jnp.float32) * s_in, 'router_b': jax.random.normal(ks[2], (NUM_EXPERTS,), dtype=jnp.float32) * 0.01, 'gate_w': jax.random.normal(ks[3], (NUM_EXPERTS, F, H), dtype=jnp.float32) * s_in, 'up_w': jax.random.normal(ks[4], (NUM_EXPERTS, F, H), dtype=jnp.float32) * s_in, 'down_w': jax.random.normal(ks[5], (NUM_EXPERTS, H, F), dtype=jnp.float32) * s_ff}
    _L0_ffn_all = _L0_ffn_setup()
    _L0_ffn_in = {k: v for k, v in _L0_ffn_all.items() if k in ('router_w', 'router_b', 'gate_w', 'up_w', 'down_w')}
    del _L0_ffn_all
    return {'x': x, 'ctx_2048': ctx_2048, 'L0_attn_Wqkv': _L0_attn_in['Wqkv'], 'L0_attn_Wproj': _L0_attn_in['Wproj'], 'L0_attn_bproj': _L0_attn_in['bproj'], 'L0_xattn_w_qkv': _L0_xattn_in['w_qkv'], 'L0_xattn_w_proj': _L0_xattn_in['w_proj'], 'L0_xattn_b_proj': _L0_xattn_in['b_proj'], 'L0_ffn_router_w': _L0_ffn_in['router_w'], 'L0_ffn_router_b': _L0_ffn_in['router_b'], 'L0_ffn_gate_w': _L0_ffn_in['gate_w'], 'L0_ffn_up_w': _L0_ffn_in['up_w'], 'L0_ffn_down_w': _L0_ffn_in['down_w']}

def reference(x, ctx_2048, L0_attn_Wqkv, L0_attn_Wproj, L0_attn_bproj, L0_xattn_w_qkv, L0_xattn_w_proj, L0_xattn_b_proj, L0_ffn_router_w, L0_ffn_router_b, L0_ffn_gate_w, L0_ffn_up_w, L0_ffn_down_w):
    import jax
    import jax.numpy as jnp

    def _L0_attn_ref(x, Wqkv, Wproj, bproj):
        import jax, jax.numpy as jnp
        import numpy as np
        B, N, C, H, W = (2, 512, 256, 16, 8)
        HD = C // H
        SCALE = HD ** (-0.5)

        def band_mask(n, w):
            i = jnp.arange(n)[:, None]
            j = jnp.arange(n)[None, :]
            lo = jnp.where(i <= w, 0, i - w)
            hi = jnp.where(n - i <= w, n - 1, i + w)
            return (j >= lo) & (j <= hi)
        b, n, c = x.shape
        qkv = (x @ Wqkv).reshape(b, n, 3, H, HD)
        qkv = jnp.transpose(qkv, (2, 0, 3, 1, 4))
        q, k, v = (qkv[0], qkv[1], qkv[2])
        attn = jnp.einsum('bhqd,bhkd->bhqk', q, k) * SCALE
        mask = band_mask(n, W)
        attn = jnp.where(mask[None, None], attn, jnp.float32(-1000000000.0))
        attn = jax.nn.softmax(attn, axis=-1)
        out = jnp.einsum('bhqk,bhkd->bhqd', attn, v)
        out = jnp.transpose(out, (0, 2, 1, 3)).reshape(b, n, c)
        return out @ Wproj + bproj

    def _L0_xattn_ref(x, context, w_qkv, w_proj, b_proj):
        import jax, jax.numpy as jnp
        import numpy as np
        NUM_HEADS = 16
        B, N, C = x.shape
        H = NUM_HEADS
        D = C // H
        scale = D ** (-0.5)
        qkv = (x @ w_qkv.T).reshape(B, N, 3, H, D).transpose(2, 0, 3, 1, 4)
        q, k, v = (qkv[0], qkv[1], qkv[2])
        N_c = context.shape[1]
        kv = context.reshape(B, N_c, 2, H, D).transpose(2, 0, 3, 1, 4)
        extra_k, extra_v = (kv[0], kv[1])
        k = jnp.concatenate([extra_k, k], axis=2)
        v = jnp.concatenate([extra_v, v], axis=2)
        dtype = q.dtype
        attn = jnp.einsum('bhnd,bhmd->bhnm', q * scale, k).astype(jnp.float32)
        attn = jax.nn.softmax(attn, axis=-1).astype(dtype)
        out = jnp.einsum('bhnm,bhmd->bhnd', attn, v)
        out = out.transpose(0, 2, 1, 3).reshape(B, N, C)
        return out @ w_proj.T + b_proj

    def _L0_ffn_ref(x, router_w, router_b, gate_w, up_w, down_w):
        import jax, jax.numpy as jnp
        import numpy as np
        TOP_K = 2
        NUM_EXPERTS = 8
        B, T, H, F = (4, 512, 256, 1024)
        logits = jnp.einsum('bth,eh->bte', x, router_w) + router_b
        topv, topi = jax.lax.top_k(logits, TOP_K)
        gates = jax.nn.softmax(topv, axis=-1)

        def body(acc, inputs):
            e, gw, uw, dw = inputs
            w = jnp.sum(gates * (topi == e), axis=-1)
            h = jax.nn.silu(jnp.einsum('bth,fh->btf', x, gw)) * jnp.einsum('bth,fh->btf', x, uw)
            y = jnp.einsum('btf,hf->bth', h, dw)
            return (acc + y * w[..., None], None)
        init = jnp.zeros_like(x)
        xs = (jnp.arange(NUM_EXPERTS), gate_w, up_w, down_w)
        out, _ = jax.lax.scan(body, init, xs)
        return out
    x = _layernorm(x + _L0_attn_ref(x, L0_attn_Wqkv, L0_attn_Wproj, L0_attn_bproj), axis=-1)
    x = _layernorm(x + _L0_xattn_ref(x, ctx_2048, L0_xattn_w_qkv, L0_xattn_w_proj, L0_xattn_b_proj), axis=-1)
    x = _layernorm(x + _L0_ffn_ref(x, L0_ffn_router_w, L0_ffn_router_b, L0_ffn_gate_w, L0_ffn_up_w, L0_ffn_down_w), axis=-1)
    return x

_drawn_inputs = setup_inputs


def setup_inputs(seed=0):
    import zlib

    import numpy as np

    out = dict(_drawn_inputs(seed))
    spreads = {'L0_attn_bproj': (0.0, 0.1)}
    factors = {}
    for name, (base, spread) in spreads.items():
        noise = np.random.default_rng([zlib.crc32(name.encode()), seed]).standard_normal(out[name].shape)
        drawn = base * np.exp(spread * noise) if base else spread * noise
        out[name] = jnp.asarray(drawn.astype(out[name].dtype))
    for name, factor in factors.items():
        out[name] = (out[name] * factor).astype(out[name].dtype)
    return out
```

```python
import concourse.bass as bass
from concourse import mybir
from contextlib import ExitStack

B, N, C, H, D = 16, 256, 256, 16, 16
NCTX = 77
BAND = 8
P = 128
TT = N // P
KT = C // P
WIN = P + BAND
W0 = [0, N - WIN]
NK = N + NCTX
EPS = 1e-5
SCALE = float(D) ** -0.5
NE, F = 8, 1024
FM = F // P
TM = 384
TMT = TM // P
NTILE = (2 * B * N + NE * (TM - 1)) // TM
CAP = B * N + TM
SPARE = NE * CAP
NSPARE = NTILE - 2 * B * N // TM
NSLOT = SPARE + NSPARE * TM
LEVELS = (B * N + TM - 1) // TM
NTOK = B * N // P
UNITS, HU = 4, 4
MASKED = -1e30
QSPLIT = [0, 0, 0, 1, 1, 2]
KSPLIT = [0, 1, 2, 0, 1, 0]
ROWS = len(QSPLIT) * D
SIZES = [P, P, TT * WIN, NE, NE * LEVELS, NE * NE, NTILE * NE, NE]
IDENT, UPPER, MASK, EXPERT, LEVEL, LOWER, TILE, REGION, NCONST = [sum(SIZES[:i]) for i in range(9)]


class Step:

    def __init__(self, s, par, half, low, high):
        self.s, self.par, self.half, self.low, self.high = s, par, half, low, high

    def since(self, n):
        return self.low >= n

    def before(self, n):
        return self.high < n


def steps(eng, body, total=B, front=4, back=2, chain=None, per_pair=0):
    for s in range(front):
        body(Step(s, s % 2, s // 2, s, s))
    pairs = (total - front - back) // 2
    start = chain.at if chain else 0
    with eng.Fori(0, pairs) as i:
        if chain:
            chain.at, chain.inside = i * per_pair + start, 0
        for par in range(2):
            body(Step(i * 2 + (front + par), par, i + front // 2, front + par, total - back - 2 + par))
        if chain:
            assert chain.inside == per_pair, chain.inside
    if chain:
        chain.at, chain.inside = start + pairs * per_pair, None
    for s in range(total - back, total):
        body(Step(s, s % 2, s // 2, s, s))


def alone(eng):
    eng.nop(nofuse=True)


class Chain:

    def __init__(self, eng, sem):
        self.eng, self.sem, self.at, self.inside = eng, sem, 0, None

    def link(self, ins, apart=False):
        self.at = self.at + 1
        if self.inside is not None:
            self.inside += 1
        ins.then_inc(self.sem, 1)
        self.eng.wait_ge(self.sem, self.at)
        if apart:
            alone(self.eng)


def project_first(nc, hbm):
    fp32, bf16 = mybir.dt.float32, mybir.dt.bfloat16
    ALU = mybir.AluOpType
    ctx = ExitStack()
    with ctx:
        def sb(name, shape, dt=fp32):
            return ctx.enter_context(nc.sbuf_tensor(name, shape, dt))

        def sem(name):
            return ctx.enter_context(nc.semaphore(name))

        w = sb("a_w", [P, KT, 3 * C])
        xT = sb("a_xT", [P, 2, KT, N])
        cT = sb("a_cT", [P, 2, KT, NCTX])
        res = sb("a_res", [P, 2, 2, KT * N])
        planes = sb("a_planes", [P, 2, 2, 3, KT * N], bf16)
        cres = sb("a_cres", [P, 2, KT * NCTX])
        cplanes = sb("a_cplanes", [P, 2, 3, KT * NCTX], bf16)
        va = sb("a_va", [P, 2, TT, H, 2 * D])
        ps = [[ctx.enter_context(nc.psum_tensor(f"a_ps{a}{b}", [P, 512], fp32)) for b in range(3)]
              for a in range(2)]
        weights_loaded = sem("a_weights_loaded")
        x_loaded = [sem(f"a_x_loaded{i}") for i in range(2)]
        ones_set = sem("a_ones_set")
        q_filled, k_filled, v_filled = sem("a_q_filled"), sem("a_k_filled"), sem("a_v_filled")
        high_ready = sem("a_high_ready")
        v_ready = sem("a_v_ready")
        res_ready = sem("a_res_ready")
        planes_ready = sem("a_planes_ready")
        pool_seq = sem("a_pool_seq")
        stored = [sem(f"a_stored{i}") for i in range(2)]
        block = ctx.enter_context(nc.Block())

        @block.sync
        def _(sp):
            sp.dma_start(w[:], hbm["wqkv"].rearrange("(k p) n -> p k n", p=P)).then_inc(weights_loaded, 16)

            def load(st):
                if st.since(2):
                    sp.wait_ge(v_filled, st.s - 1)
                    sp.wait_ge(planes_ready, st.s * 2 - 2)
                sp.dma_start(xT[:, st.par], hbm["xT"][bass.ds(st.s, 1)].rearrange("a (k p) t -> p (a k) t", p=P)
                             ).then_inc(x_loaded[st.par], 16)
                sp.dma_start(cT[:, st.par], hbm["ctxT"][bass.ds(st.s, 1), 0:C].rearrange(
                    "a (k p) t -> p (a k) t", p=P)).then_inc(x_loaded[st.par], 16)

            steps(sp, load)

        @block.tensor
        def _(pe):
            pe.wait_ge(weights_loaded, 16)

            def project(st):
                pe.wait_ge(x_loaded[st.par], st.half * 32 + 32)
                if st.since(2):
                    pe.wait_ge(res_ready, st.s * 2 - 2)
                    pe.wait_ge(v_ready, st.s - 1)
                for b, filled in ((0, q_filled), (1, k_filled)):
                    for m in range(KT):
                        for k in range(KT):
                            last = nc.tensor.matmul(ps[st.par][b][:, m * N:(m + 1) * N],
                                                    w[:, k, b * C + m * P:b * C + (m + 1) * P],
                                                    xT[:, st.par, k], start=(k == 0), stop=(k == KT - 1))
                    last.then_inc(filled, 1)
                for t in range(TT):
                    for k in range(KT):
                        last = nc.tensor.matmul(ps[st.par][2][:, t * C:(t + 1) * C],
                                                xT[:, st.par, k, t * P:(t + 1) * P], w[:, k, 2 * C:],
                                                start=(k == 0), stop=(k == KT - 1))
                last.then_inc(v_filled, 1)

            steps(pe, project)

        @block.scalar
        def _(act):
            act.wait_ge(ones_set, 1)

            def high(st):
                if st.since(2):
                    act.wait_ge(stored[st.par], st.half * 64)
                act.wait_ge(q_filled, st.s + 1)
                nc.scalar.copy(planes[:, st.par, 0, 0], ps[st.par][0][:]).then_inc(high_ready, 1)
                act.wait_ge(k_filled, st.s + 1)
                nc.scalar.copy(planes[:, st.par, 1, 0], ps[st.par][1][:]).then_inc(high_ready, 1)
                act.wait_ge(v_filled, st.s + 1)
                nc.scalar.copy(va[:, st.par, :, :, 0:D],
                               ps[st.par][2][:].rearrange("p (t h d) -> p t h d", t=TT, h=H)).then_inc(v_ready, 1)

            steps(act, high)

        @block.vector
        def _(dve):
            nc.vector.memset(va[:, :, :, :, D:], 1.0).then_inc(ones_set, 1)

            def residue(st):
                for b in range(2):
                    dve.wait_ge(high_ready, st.s * 2 + (b + 1))
                    if st.since(2):
                        dve.wait_ge(planes_ready, st.s * 2 - 2)
                    nc.vector.tensor_tensor(res[:, st.par, b], ps[st.par][b][:], planes[:, st.par, b, 0],
                                            ALU.subtract).then_inc(res_ready, 1)

            steps(dve, residue)

        @block.gpsimd
        def _(pool):
            chain = Chain(pool, pool_seq)

            def low(st):
                pool.wait_ge(x_loaded[st.par], st.half * 32 + 32)
                if st.since(2):
                    pool.wait_ge(stored[st.par], st.half * 64)
                alone(pool)
                c = cT[:, st.par].rearrange("p k t -> p (k t)")
                chain.link(nc.gpsimd.tensor_copy(cplanes[:, st.par, 0], c))
                chain.link(nc.gpsimd.tensor_tensor(cres[:, st.par], c, cplanes[:, st.par, 0], ALU.subtract),
                           apart=True)
                chain.link(nc.gpsimd.tensor_copy(cplanes[:, st.par, 1], cres[:, st.par]))
                nc.gpsimd.tensor_tensor(cplanes[:, st.par, 2], cres[:, st.par], cplanes[:, st.par, 1],
                                        ALU.subtract).then_inc(planes_ready, 1)
                for b in range(2):
                    pool.wait_ge(res_ready, st.s * 2 + (b + 1))
                    alone(pool)
                    chain.link(nc.gpsimd.tensor_copy(planes[:, st.par, b, 1], res[:, st.par, b]))
                    last = nc.gpsimd.tensor_tensor(planes[:, st.par, b, 2], res[:, st.par, b],
                                                   planes[:, st.par, b, 1], ALU.subtract)
                last.then_inc(planes_ready, 1)
                pool.wait_ge(planes_ready, st.s * 2 + 2)
                pool.wait_ge(v_ready, st.s + 1)
                for b, name in ((0, "q1"), (1, "k1")):
                    pool.dma_start(hbm[name][bass.ds(st.s, 1)].rearrange("a l (m p) t -> p (a l) m t", p=P),
                                   planes[:, st.par, b].rearrange("p l (m t) -> p l m t", m=KT)
                                   ).then_inc(stored[st.par], 16)
                pool.dma_start(hbm["k2"][bass.ds(st.s, 1), :, :, N:].rearrange("a l (m p) t -> p (a l) m t", p=P),
                               cplanes[:, st.par].rearrange("p l (m t) -> p l m t", m=KT)
                               ).then_inc(stored[st.par], 16)
                pool.dma_start(hbm["v1"][bass.ds(st.s, 1)].rearrange("a (t p) n -> p (a t) n", p=P),
                               va[:, st.par].rearrange("p t h d -> p t (h d)")).then_inc(stored[st.par], 16)

            steps(pool, low, chain=chain, per_pair=10)
            for par in range(2):
                pool.wait_ge(stored[par], 64 * B // 2)


def attention(nc, hbm, kept, cross):
    fp32, bf16, i32, u32 = mybir.dt.float32, mybir.dt.bfloat16, mybir.dt.int32, mybir.dt.uint32
    ALU, ACT, AX = mybir.AluOpType, mybir.ActivationFunctionType, mybir.AxisListType
    u = "c_" if cross else "b_"
    keys = NK if cross else N
    qd, kd, vd = (hbm[n + ("2" if cross else "1")] for n in "qkv")
    x_in, x_out = (hbm["x1"], hbm["x2"]) if cross else (hbm["x"], hbm["x1"])
    wide = TT * N if cross else TT * WIN
    tiles = H * TT if cross else H
    share = [11, 11, 10] if cross else [6, 5, 5]
    chunks = 3 if cross else 2
    ctx = ExitStack()
    with ctx:
        def sb(name, shape, dt=fp32):
            return ctx.enter_context(nc.sbuf_tensor(u + name, shape, dt))

        def sem(name):
            return ctx.enter_context(nc.semaphore(u + name))

        def bank(name):
            return ctx.enter_context(nc.psum_tensor(u + name, [P, 512], fp32))

        qs = sb("qs", [ROWS + 3, 2, H, N], bf16)
        ks = sb("ks", [ROWS + 3, 2, H, keys], bf16)
        va = sb("va", [P, 2, chunks, H, 2 * D])
        resid = sb("resid", [P, 2, TT, C])
        pm = sb("pm", [P, 2, HU, wide])
        pt = sb("pt", [NCTX, 2, HU, N]) if cross else None
        nm = sb("nm", [P, 2, H, TT])
        nmr = sb("nmr", [P, 2, TT, H])
        nmp = sb("nmp", [P, 2, TT, 3, H], bf16)
        nmT = sb("nmT", [3 * H, 2, N], bf16)
        den = sb("den", [P, N])
        rden = sb("rden", [P, N])
        on = sb("on", [P, UNITS, N])
        wp = sb("wp", [P, UNITS, C])
        y = sb("y", [P, 2, TT, C])
        stats = sb("stats", [P, TT, 6])
        mv = sb("mv", [P, 2, TT, 2])
        lnv = sb("lnv", [P, 2, TT])
        rstd = sb("rstd", [P, 2, TT])
        newton = sb("newton", [P, 2, TT])
        eps = sb("eps", [P, 1])
        xn = sb("xn", [P, 2, TT, C])
        xnT = sb("xnT", [P, KT, N])
        const = sb("const", [P, NCONST])
        identb = sb("identb", [P, P], bf16)
        maskb = sb("maskb", [P, TT, WIN], bf16)
        ident = const[:, IDENT:IDENT + P]
        if cross:
            rw = sb("rw", [P, KT, NE])
            rb = sb("rb", [P, TT, NE])
            trib = sb("trib", [P, P], bf16)
            onesb = sb("onesb", [P, P], bf16)
            iota4 = sb("iota4", [P, 2 * TT, NE])
            logit = sb("logit", [P, TT, NE])
            top = sb("top", [P, TT, 8])
            topi = sb("topi", [P, TT, 8], u32)
            idxf = sb("idxf", [P, TT, 2])
            hot = sb("hot", [P, TT * 2, NE])
            hotb = sb("hotb", [P, TT, NE], bf16)
            gap = sb("gap", [P, TT])
            egap = sb("egap", [P, TT])
            oneg = sb("oneg", [P, TT])
            gate = sb("gate", [P, 2, TT])
            place = sb("place", [P, TT, NE])
            pick = sb("pick", [P, TT * 2, NE])
            slotf = sb("slotf", [P, TT * 2])
            slot = sb("slot", [P, 2, TT * 2], u32)
            base = kept["count"]
        else:
            w = sb("w", [P, KT, 3 * C])
            res = sb("res", [P, 2, KT * N])
            planes = sb("planes", [P, 2, 3, KT * N], bf16)
            vo = sb("vo", [P, TT, H, 2 * D])
        st_bank = [bank(f"st{i}") for i in range(2)]
        tl_bank = bank("tl")
        sm_bank = [bank(f"sm{i}") for i in range(2)]
        pv_bank = bank("pv")
        m0, m1 = bank("m0"), bank("m1")

        const_loaded, weights_loaded = sem("const_loaded"), sem("weights_loaded")
        zeroed, setup_done = sem("zeroed"), sem("setup_done")
        qk_loaded = [[sem(f"qk_loaded{a}{b}") for b in range(UNITS)] for a in range(2)]
        nm_loaded = [sem(f"nm_loaded{i}") for i in range(2)]
        rest_loaded = [sem(f"rest_loaded{i}") for i in range(2)]
        sm_filled, sm_drained = sem("sm_filled"), sem("sm_drained")
        st_filled, st_drained = sem("st_filled"), sem("st_drained")
        tl_filled, tl_drained = sem("tl_filled"), sem("tl_drained")
        pv_filled, pv_drained = sem("pv_filled"), sem("pv_drained")
        nmp_ready, nm_filled, nm_drained = sem("nmp_ready"), sem("nm_filled"), sem("nm_drained")
        op_filled, op_drained = sem("op_filled"), sem("op_drained")
        stats_ready, rstd_ready, xn_ready = sem("stats_ready"), sem("rstd_ready"), sem("xn_ready")
        tr_filled, tr_drained = sem("tr_filled"), sem("tr_drained")
        dve_seq, act_seq, pool_seq = sem("dve_seq"), sem("act_seq"), sem("pool_seq")
        x_stored = [sem(f"x_stored{i}") for i in range(2)]
        if cross:
            lg_filled, lg_drained = sem("lg_filled"), sem("lg_drained")
            hot_ready, rk_filled, rk_drained = sem("hot_ready"), sem("rk_filled"), sem("rk_drained")
            gap_ready, egap_ready = sem("gap_ready"), sem("egap_ready")
            slot_ready = sem("slot_ready")
            scattered = [sem(f"scattered{i}") for i in range(2)]
        else:
            q_filled, k_filled, v_filled = sem("q_filled"), sem("k_filled"), sem("v_filled")
            high_ready, res_ready = sem("high_ready"), sem("res_ready")
            v_drained, planes_ready = sem("v_drained"), sem("planes_ready")
            p_stored = sem("p_stored")
        block = ctx.enter_context(nc.Block())

        def tail(body, st):
            if st.since(1):
                body(Step(st.s - 1, 1 - st.par, st.half - (1 - st.par), st.low - 1, st.high - 1))

        @block.sync
        def _(sp):
            sp.dma_start(const[:], hbm["const"]).then_inc(const_loaded, 16)
            sp.wait_ge(zeroed, 1)
            for j in range(HU):
                sp.dma_start(wp[32 * j:32 * j + D], hbm["wp2" if cross else "wp1"].rearrange(
                    "(a j d) n -> j d a n", j=HU, d=D)[j]).then_inc(weights_loaded, 16)
            sp.dma_start(wp[D:D + 1, 0], hbm["bp2" if cross else "bp1"]).then_inc(weights_loaded, 16)
            if cross:
                sp.dma_start(rw[:], hbm["rw"].rearrange("(k p) e -> p k e", p=P)).then_inc(weights_loaded, 16)
                for t in range(TT):
                    sp.dma_start(rb[:, t], hbm["rb"].to_broadcast([P, NE])).then_inc(weights_loaded, 16)
            else:
                sp.dma_start(w[:], hbm["wx"].rearrange("(k p) n -> p k n", p=P)).then_inc(weights_loaded, 16)

            def load_qk(s, par, g):
                hs = slice(g * HU, g * HU + HU)
                for split, dst, src in ((QSPLIT, qs, qd), (KSPLIT, ks, kd)):
                    for r, pl in enumerate(split):
                        sp.dma_start(dst[r * D:r * D + D, par, hs],
                                     src[bass.ds(s, 1), pl, g * HU * D:(g + 1) * HU * D].rearrange(
                                         "a (h d) t -> d (a h) t", h=HU)).then_inc(qk_loaded[par][g], 16)

            def load_rest(s, par):
                sp.dma_start(va[:, par, 0:TT].rearrange("p t h d -> p t (h d)"),
                             vd[bass.ds(s, 1)].rearrange("a (t p) n -> p (a t) n", p=P)).then_inc(rest_loaded[par], 16)
                sp.dma_start(resid[:, par], x_in[bass.ds(s, 1)].rearrange("a (t p) n -> p (a t) n", p=P)
                             ).then_inc(rest_loaded[par], 16)
                if cross:
                    sp.dma_start(va[0:NCTX, par, TT, :, 0:D], hbm["ctx"][bass.ds(s, 1), :, C:].rearrange(
                        "a p (h d) -> p (a h) d", h=H)).then_inc(rest_loaded[par], 16)

            def load_nm(st):
                sp.wait_ge(nm_drained, st.s + 1)
                for pl in range(3):
                    sp.dma_start(qs[ROWS + pl:ROWS + pl + 1, st.par], nmT[pl * H:pl * H + H, st.par]
                                 ).then_inc(nm_loaded[st.par], 16)

            sp.wait_ge(setup_done, 2)
            for s in range(2):
                for g in range(UNITS):
                    load_qk(s, s, g)
                load_rest(s, s)
            load_nm(Step(0, 0, 0, 0, 0))

            def store_x(st):
                sp.wait_ge(xn_ready, st.s + 1)
                sp.dma_start(x_out[bass.ds(st.s, 1)].rearrange("a (t p) n -> p (a t) n", p=P), xn[:, st.par]
                             ).then_inc(x_stored[st.par], 16)

            def store_projected(st):
                sp.wait_ge(planes_ready, st.s * 2 + 2)
                for b, name in ((0, "q2"), (1, "k2")):
                    sp.dma_start(hbm[name][bass.ds(st.s, 1), :, :, 0:N].rearrange(
                        "a l (m p) t -> p (a l) m t", p=P), planes[:, b].rearrange(
                        "p l (m t) -> p l m t", m=KT)).then_inc(p_stored, 16)
                sp.wait_ge(v_drained, st.s + 1)
                alone(sp)
                sp.dma_start(hbm["v2"][bass.ds(st.s, 1)].rearrange("a (t p) n -> p (a t) n", p=P),
                             vo[:].rearrange("p t h d -> p t (h d)")).then_inc(p_stored, 16)

            def step(st):
                for g in range(UNITS):
                    if st.before(B - 2):
                        if cross:
                            sp.wait_ge(tl_filled, st.s * (H // 2) + (g + 1) * (HU // 2))
                        else:
                            sp.wait_ge(st_filled, st.s * H + (g + 1) * HU)
                        load_qk(st.s + 2, st.par, g)
                    if g == 0:
                        tail(store_x, st)
                if st.before(B - 1):
                    load_nm(Step(st.s + 1, 1 - st.par, st.half + st.par, st.low + 1, st.high + 1))
                if not cross:
                    tail(store_projected, st)
                if st.before(B - 2):
                    sp.wait_ge(pv_filled, st.s * UNITS + UNITS)
                    alone(sp)
                    sp.wait_ge(op_drained, st.s + 1)
                    alone(sp)
                    load_rest(st.s + 2, st.par)

            steps(sp, step)
            last = Step(B - 1, 1, B // 2 - 1, B - 1, B - 1)
            store_x(last)
            if not cross:
                store_projected(last)
                sp.wait_ge(p_stored, 48 * B)
            for par in range(2):
                sp.wait_ge(x_stored[par], 16 * B // 2)

        @block.tensor
        def _(pe):
            pe.wait_ge(weights_loaded, (HU + 1 + (1 + TT if cross else 1)) * 16)
            pe.wait_ge(setup_done, 3)

            def maxima(st, part):
                first = sum(share[:part])
                for n in range(first, first + share[part]):
                    h, t = (n // TT, n % TT) if cross else (n, 0)
                    if n == first or (h % HU == 0 and t == 0):
                        pe.wait_ge(qk_loaded[st.par][h // HU], (st.half + 1) * 2 * len(QSPLIT) * 16)
                    if st.since(1) or n >= 2:
                        pe.wait_ge(sm_drained, st.s * tiles + (n - 1))
                    out = sm_bank[n % 2]
                    if cross:
                        last = nc.tensor.matmul(out[:, 0:NK], qs[0:ROWS, st.par, h, t * P:(t + 1) * P],
                                                ks[0:ROWS, st.par, h], start=True, stop=True)
                    else:
                        nc.tensor.matmul(out[:, 0:TT * WIN], identb[:], maskb[:], start=True, stop=False,
                                         skip_group_check=True)
                        for t in range(TT):
                            last = nc.tensor.matmul(
                                out[:, t * WIN:(t + 1) * WIN], qs[0:ROWS, st.par, h, t * P:(t + 1) * P],
                                ks[0:ROWS, st.par, h, W0[t]:W0[t] + WIN], start=False, stop=(t == TT - 1),
                                skip_group_check=True)
                    last.then_inc(sm_filled, 1)

            def scores(st, pair):
                if pair == 0:
                    pe.wait_ge(nm_loaded[st.par], st.half * 48 + 48)
                for e in range(2):
                    h = pair * 2 + e
                    if st.since(1) or h >= 2:
                        pe.wait_ge(st_drained, st.s * H + (h - 1))
                    out = st_bank[e]
                    if cross:
                        for c in range(TT):
                            last = nc.tensor.matmul(out[:, c * N:(c + 1) * N], ks[:, st.par, h, c * P:(c + 1) * P],
                                                    qs[:, st.par, h], start=True, stop=True)
                    else:
                        nc.tensor.matmul(out[:, 0:TT * WIN], identb[:], maskb[:], start=True, stop=False,
                                         skip_group_check=True)
                        for c in range(TT):
                            last = nc.tensor.matmul(
                                out[:, c * WIN:(c + 1) * WIN], ks[:, st.par, h, c * P:(c + 1) * P],
                                qs[:, st.par, h, W0[c]:W0[c] + WIN], start=False, stop=(c == TT - 1),
                                skip_group_check=True)
                    last.then_inc(st_filled, 1)
                if cross:
                    if st.since(1) or pair >= 1:
                        pe.wait_ge(tl_drained, st.s * (H // 2) + pair)
                    for e in range(2):
                        last = nc.tensor.matmul(tl_bank[0:NCTX, e * N:(e + 1) * N],
                                                ks[:, st.par, pair * 2 + e, N:], qs[:, st.par, pair * 2 + e],
                                                start=True, stop=True)
                    last.then_inc(tl_filled, 1)

            def weigh(st, g):
                if g == 0:
                    pe.wait_ge(rest_loaded[st.par], (st.half + 1) * (3 if cross else 2) * 16)
                pe.wait_ge(st_drained, st.s * H + (g + 1) * HU)
                if cross:
                    pe.wait_ge(tl_drained, st.s * (H // 2) + (g + 1) * (HU // 2))
                if st.since(1) or g >= 1:
                    pe.wait_ge(pv_drained, st.s * UNITS + g)
                for c in range(chunks):
                    for j in range(HU):
                        kc = NCTX if c == TT else P
                        lhsT = va[0:kc, st.par, c, g * HU + j]
                        if c == TT:
                            cols, rhs = slice(0, N), pt[:, g % 2, j]
                        elif cross:
                            cols, rhs = slice(0, N), pm[:, g % 2, j, c * N:(c + 1) * N]
                        else:
                            cols, rhs = slice(W0[c], W0[c] + WIN), pm[:, g % 2, j, c * WIN:(c + 1) * WIN]
                        last = nc.tensor.matmul(pv_bank[32 * j:32 * j + 32, cols], lhsT, rhs, start=(c == 0),
                                                stop=(c == chunks - 1), skip_group_check=True)
                last.then_inc(pv_filled, 1)

            def turn_maxima(st):
                pe.wait_ge(nmp_ready, st.s + 1)
                if st.since(2):
                    pe.wait_ge(rk_drained if cross else res_ready, st.s - 1 if cross else st.s * 2 - 2)
                alone(pe)
                out = m1[0:3 * H, 0:N // 2].bitcast(bf16)
                for t in range(TT):
                    last = nc.tensor.transpose(out[:, t * P:(t + 1) * P],
                                               nmp[:, st.par, t].rearrange("p l h -> p (l h)"), identb[:])
                last.then_inc(nm_filled, 1)

            def project(st):
                pe.wait_ge(pv_drained, st.s * UNITS + UNITS)
                if st.since(1):
                    pe.wait_ge(lg_drained if cross else v_drained, st.s)
                for t in range(TT):
                    for g in range(UNITS):
                        last = nc.tensor.matmul(m0[:, t * C:(t + 1) * C], on[:, g, t * P:(t + 1) * P], wp[:, g],
                                                start=(g == 0), stop=(g == UNITS - 1))
                last.then_inc(op_filled, 1)

            def turn_x(st):
                pe.wait_ge(xn_ready, st.s + 1)
                if st.before(B - 1):
                    pe.wait_ge(nm_drained, st.s + 2)
                else:
                    pe.wait_ge(nm_drained, B)
                for k in range(KT):
                    for t in range(TT):
                        last = nc.tensor.transpose(m1[:, k * N + t * P:k * N + (t + 1) * P],
                                                   xn[:, st.par, t, k * P:(k + 1) * P], ident)
                last.then_inc(tr_filled, 1)

            def project_next(st):
                pe.wait_ge(tr_drained, st.s + 1)
                pe.wait_ge(op_drained, st.s + 1)
                for b, out, filled in ((0, m0, q_filled), (1, m1, k_filled)):
                    for m in range(KT):
                        for k in range(KT):
                            last = nc.tensor.matmul(out[:, m * N:(m + 1) * N],
                                                    w[:, k, b * C + m * P:b * C + (m + 1) * P], xnT[:, k],
                                                    start=(k == 0), stop=(k == KT - 1))
                    last.then_inc(filled, 1)
                pe.wait_ge(res_ready, st.s * 2 + 1)
                for t in range(TT):
                    for k in range(KT):
                        last = nc.tensor.matmul(m0[:, t * C:(t + 1) * C], xnT[:, k, t * P:(t + 1) * P],
                                                w[:, k, 2 * C:], start=(k == 0), stop=(k == KT - 1))
                last.then_inc(v_filled, 1)

            def logits(st):
                pe.wait_ge(tr_drained, st.s + 1)
                pe.wait_ge(op_drained, st.s + 1)
                for t in range(TT):
                    for k in range(KT):
                        last = nc.tensor.matmul(m0[:, t * NE:(t + 1) * NE], xnT[:, k, t * P:(t + 1) * P], rw[:, k],
                                                start=(k == 0), stop=(k == KT - 1))
                last.then_inc(lg_filled, 1)

            def ranks(st):
                pe.wait_ge(hot_ready, st.s + 1)
                nc.tensor.matmul(m1[:, 0:NE], trib[:], hotb[:, 0], start=True, stop=True)
                nc.tensor.matmul(m1[:, NE:2 * NE], onesb[:], hotb[:, 0], start=True, stop=False)
                nc.tensor.matmul(m1[:, NE:2 * NE], trib[:], hotb[:, 1], start=False, stop=True)
                nc.tensor.matmul(m1[:, 2 * NE:3 * NE], onesb[:], hotb[:, 0], start=True, stop=False)
                nc.tensor.matmul(m1[:, 2 * NE:3 * NE], onesb[:], hotb[:, 1], start=False, stop=True
                                 ).then_inc(rk_filled, 1)

            first = Step(0, 0, 0, 0, 0)
            for part in range(3):
                maxima(first, part)
            turn_maxima(first)

            def step(st):
                nxt = Step(st.s + 1, 1 - st.par, st.half + st.par, st.low + 1, st.high + 1)
                for g in range(UNITS):
                    scores(st, 2 * g)
                    scores(st, 2 * g + 1)
                    if g >= 1:
                        weigh(st, g - 1)
                    if g < 3 and st.before(B - 1):
                        maxima(nxt, g)
                    if g == 1:
                        tail(turn_x, st)
                    if g == 2:
                        tail(logits if cross else project_next, st)
                    if g == 3:
                        if cross:
                            tail(ranks, st)
                        if st.before(B - 1):
                            turn_maxima(nxt)
                weigh(st, UNITS - 1)
                project(st)

            steps(pe, step)
            last = Step(B - 1, 1, B // 2 - 1, B - 1, B - 1)
            turn_x(last)
            if cross:
                logits(last)
                ranks(last)
            else:
                project_next(last)

        @block.scalar
        def _(act):
            chain = Chain(act, act_seq)
            nc.scalar.preload_act_table_set("natural_log_exp_and_others")
            act.wait_ge(setup_done, 3)

            def probabilities(st, pair):
                g = pair // 2
                if pair % 2 == 0 and (st.since(1) or g >= 2):
                    act.wait_ge(pv_filled, st.s * UNITS + (g - 1))
                for e in range(2):
                    h = pair * 2 + e
                    act.wait_ge(st_filled, st.s * H + (h + 1))
                    nc.scalar.activation(pm[:, g % 2, h % HU], st_bank[e][:, 0:wide], ACT.Exp,
                                         scale=SCALE).then_inc(st_drained, 1)
                if cross:
                    act.wait_ge(tl_filled, st.s * (H // 2) + (pair + 1))
                    nc.scalar.activation(pt[:, g % 2, pair % 2 * 2:pair % 2 * 2 + 2], tl_bank[0:NCTX].rearrange(
                        "p (e t) -> p e t", e=2), ACT.Exp, scale=SCALE).then_inc(tl_drained, 1)

            def drain_maxima(st):
                act.wait_ge(nm_filled, st.s + 1)
                if st.since(2):
                    act.wait_ge(nm_loaded[st.par], st.half * 48)
                nc.scalar.copy(nmT[:, st.par], m1[0:3 * H, 0:N // 2].bitcast(bf16)).then_inc(nm_drained, 1)

            def drain_x(st):
                act.wait_ge(tr_filled, st.s + 1)
                if st.since(1):
                    act.wait_ge(lg_filled if cross else v_filled, st.s)
                nc.scalar.copy(xnT[:].rearrange("p k t -> p (k t)"), m1[:]).then_inc(tr_drained, 1)

            def high(st):
                if st.since(1):
                    act.wait_ge(p_stored, st.s * 48)
                act.wait_ge(q_filled, st.s + 1)
                nc.scalar.copy(planes[:, 0, 0], m0[:]).then_inc(high_ready, 1)
                act.wait_ge(k_filled, st.s + 1)
                nc.scalar.copy(planes[:, 1, 0], m1[:]).then_inc(high_ready, 1)
                act.wait_ge(v_filled, st.s + 1)
                nc.scalar.copy(vo[:, :, :, 0:D], m0[:].rearrange("p (t h d) -> p t h d", t=TT, h=H)
                               ).then_inc(v_drained, 1)

            def gates(st):
                act.wait_ge(gap_ready, st.s + 1)
                nc.scalar.activation(egap[:], gap[:], ACT.Exp).then_inc(egap_ready, 1)

            def spread(st):
                act.wait_ge(stats_ready, st.s + 1)
                chain.link(nc.scalar.activation(lnv[:, st.par], mv[:, st.par, :, 1], ACT.Ln, bias=eps[:]))
                nc.scalar.activation(rstd[:, st.par], lnv[:, st.par], ACT.Exp, scale=-0.5).then_inc(rstd_ready, 1)

            drain_maxima(Step(0, 0, 0, 0, 0))

            def step(st):
                for pair in range(H // 2):
                    probabilities(st, pair)
                    if pair == 3:
                        tail(drain_x, st)
                    if pair == 5:
                        if cross:
                            tail(gates, st)
                        else:
                            tail(high, st)
                if st.before(B - 1):
                    drain_maxima(Step(st.s + 1, 1 - st.par, st.half + st.par, st.low + 1, st.high + 1))
                spread(st)

            steps(act, step, chain=chain, per_pair=2)
            last = Step(B - 1, 1, B // 2 - 1, B - 1, B - 1)
            drain_x(last)
            if cross:
                gates(last)
            else:
                high(last)

        @block.vector
        def _(dve):
            chain = Chain(dve, dve_seq)
            nc.vector.memset(ks[ROWS:ROWS + 3], 1.0).then_inc(setup_done, 1)
            nc.vector.memset(va[:, :, :, :, D:], 1.0).then_inc(setup_done, 1)
            dve.wait_ge(const_loaded, 16)
            nc.vector.tensor_copy(identb[:], const[:, IDENT:IDENT + P])
            nc.vector.tensor_copy(maskb[:].rearrange("p t n -> p (t n)"), const[:, MASK:MASK + TT * WIN])
            if cross:
                nc.vector.memset(base[:], 0.0)
                nc.vector.memset(onesb[:], 1.0)
                nc.vector.tensor_copy(trib[:], const[:, UPPER:UPPER + P])
                for i in range(2 * TT):
                    nc.vector.tensor_copy(iota4[:, i], const[:, EXPERT:EXPERT + NE])
            else:
                nc.vector.memset(vo[:, :, :, D:], 1.0)
            nc.vector.memset(eps[:], EPS).then_inc(setup_done, 1)

            def maxima(st, part):
                first = sum(share[:part])
                if part == 0 and st.since(2):
                    dve.wait_ge(nmp_ready, st.s - 1)
                for n in range(first, first + share[part]):
                    dve.wait_ge(sm_filled, st.s * tiles + (n + 1))
                    if cross:
                        h, t = n // TT, n % TT
                        nc.vector.reduce_max(nm[:, st.par, h, t:t + 1], sm_bank[n % 2][:, 0:NK], AX.X,
                                             negate=True).then_inc(sm_drained, 1)
                    else:
                        nc.vector.reduce_max(nm[:, st.par, n], sm_bank[n % 2][:, 0:TT * WIN].rearrange(
                            "p (t n) -> p t n", t=TT), AX.X, negate=True).then_inc(sm_drained, 1)

            swap = [i % D + D for i in range(2 * D)]

            def normalize(st, g):
                dve.wait_ge(pv_filled, st.s * UNITS + (g + 1))
                alone(dve)
                chain.link(nc.vector.stream_shuffle(den[:], pv_bank[:, 0:N], swap))
                chain.link(nc.vector.reciprocal(rden[:], den[:]))
                if g == 0 and st.since(1):
                    dve.wait_ge(op_filled, st.s)
                nc.vector.tensor_tensor(on[:, g], pv_bank[:, 0:N], rden[:], ALU.mult).then_inc(pv_drained, 1)

            def residual(st):
                dve.wait_ge(op_filled, st.s + 1)
                dve.wait_ge(rest_loaded[st.par], (st.half + 1) * (3 if cross else 2) * 16)
                nc.vector.tensor_tensor(y[:, st.par].rearrange("p t n -> p (t n)"), m0[:],
                                        resid[:, st.par].rearrange("p t n -> p (t n)"), ALU.add
                                        ).then_inc(op_drained, 1)
                dve.wait_ge(op_drained, st.s + 1)
                for t in range(TT):
                    last = nc.vector.bn_stats(stats[:, t], y[:, st.par, t])
                chain.link(last, apart=True)
                for t in range(TT):
                    last = nc.vector.bn_aggr(mv[:, st.par, t], stats[:, t])
                last.then_inc(stats_ready, 1)

            def norm(st):
                dve.wait_ge(rstd_ready, st.s + 1)
                r, t1, var = rstd[:, st.par], newton[:, st.par], mv[:, st.par, :, 1]
                chain.link(nc.vector.tensor_tensor(t1, r, r, ALU.mult))
                chain.link(nc.vector.scalar_tensor_tensor(t1, var, EPS, t1, ALU.add, ALU.mult))
                chain.link(nc.vector.tensor_scalar(t1, t1, -0.5, 1.5, ALU.mult, ALU.add))
                chain.link(nc.vector.tensor_tensor(t1, t1, r, ALU.mult))
                if st.since(2):
                    dve.wait_ge(x_stored[st.par], st.half * 16)
                    dve.wait_ge(tr_filled, st.s - 1)
                    if cross:
                        dve.wait_ge(scattered[st.par], st.half * 64)
                for t in range(TT):
                    last = nc.vector.tensor_scalar(xn[:, st.par, t], y[:, st.par, t], mv[:, st.par, t, 0:1],
                                                   newton[:, st.par, t:t + 1], ALU.subtract, ALU.mult)
                last.then_inc(xn_ready, 1)

            def residue(st):
                for b, out in ((0, m0), (1, m1)):
                    dve.wait_ge(high_ready, st.s * 2 + (b + 1))
                    if st.since(1):
                        dve.wait_ge(planes_ready, st.s * 2)
                    nc.vector.tensor_tensor(res[:, b], out[:], planes[:, b, 0], ALU.subtract
                                            ).then_inc(res_ready, 1)

            def choose(st):
                dve.wait_ge(lg_filled, st.s + 1)
                nc.vector.tensor_tensor(logit[:].rearrange("p t e -> p (t e)"), m0[:, 0:TT * NE],
                                        rb[:].rearrange("p t e -> p (t e)"), ALU.add).then_inc(lg_drained, 1)
                dve.wait_ge(lg_drained, st.s + 1)
                alone(dve)
                for t in range(TT):
                    last = nc.vector.max(top[:, t], logit[:, t])
                chain.link(last, apart=True)
                for t in range(TT):
                    last = nc.vector.max_index(topi[:, t], top[:, t], logit[:, t])
                chain.link(last)
                nc.vector.tensor_tensor(gap[:], top[:, :, 1], top[:, :, 0], ALU.subtract).then_inc(gap_ready, 1)
                chain.link(nc.vector.tensor_copy(idxf[:], topi[:, :, 0:2]))
                chain.link(nc.vector.tensor_tensor(
                    hot[:], iota4[:], idxf[:].rearrange("p t k -> p (t k)").unsqueeze(2).to_broadcast([P, 2 * TT, NE]),
                    ALU.is_equal))
                hv = hot[:].rearrange("p (t k) e -> p t k e", t=TT)
                nc.vector.tensor_tensor(hotb[:], hv[:, :, 0], hv[:, :, 1], ALU.add).then_inc(hot_ready, 1)
                dve.wait_ge(egap_ready, st.s + 1)
                chain.link(nc.vector.tensor_scalar(oneg[:], egap[:], 1.0, None, ALU.add))
                chain.link(nc.vector.reciprocal(gate[:, 0], oneg[:]))
                chain.link(nc.vector.tensor_tensor(gate[:, 1], egap[:], gate[:, 0], ALU.mult))
                nc.vector.tensor_copy(kept["gate"][:, bass.ds(st.s * 2 * TT, 2 * TT)],
                                      gate[:].rearrange("p k t -> p (k t)"))

            def assign(st):
                dve.wait_ge(rk_filled, st.s + 1)
                if st.since(1):
                    dve.wait_ge(rk_drained, st.s)
                ecap = const[:, REGION:REGION + NE]
                chain.link(nc.vector.tensor_tensor(
                    place[:], m1[:, 0:TT * NE].rearrange("p (t e) -> p t e", t=TT),
                    base[:].unsqueeze(1).to_broadcast([P, TT, NE]), ALU.add))
                nc.vector.tensor_tensor(base[:], m1[:, TT * NE:(TT + 1) * NE], base[:], ALU.add).then_inc(rk_drained, 1)
                chain.link(nc.vector.tensor_tensor(place[:], place[:], ecap.unsqueeze(1).to_broadcast([P, TT, NE]),
                                                   ALU.add))
                for t in range(TT):
                    last = nc.vector.tensor_tensor(pick[:, 2 * t:2 * t + 2], hot[:, 2 * t:2 * t + 2],
                                                   place[:, t:t + 1].to_broadcast([P, 2, NE]), ALU.mult)
                chain.link(last)
                chain.link(nc.vector.reduce_sum(slotf[:], pick[:], AX.X))
                if st.since(2):
                    dve.wait_ge(scattered[st.par], st.half * 64)
                nc.vector.tensor_copy(kept["slot"][:, bass.ds(st.s * 2 * TT, 2 * TT)], slotf[:])
                nc.vector.tensor_copy(slot[:, st.par], slotf[:]).then_inc(slot_ready, 1)

            first = Step(0, 0, 0, 0, 0)
            for part in range(3):
                maxima(first, part)

            def step(st):
                nxt = Step(st.s + 1, 1 - st.par, st.half + st.par, st.low + 1, st.high + 1)
                for g in range(UNITS):
                    if g >= 1:
                        normalize(st, g - 1)
                    if g < 3 and st.before(B - 1):
                        maxima(nxt, g)
                    if g == 0:
                        tail(norm, st)
                    if g == 2:
                        tail(choose if cross else residue, st)
                    if g == 3 and cross:
                        tail(assign, st)
                normalize(st, UNITS - 1)
                residual(st)

            steps(dve, step, chain=chain, per_pair=2 * (8 + 1 + 4 + (7 + 4 if cross else 0)))
            last = Step(B - 1, 1, B // 2 - 1, B - 1, B - 1)
            norm(last)
            if cross:
                choose(last)
                assign(last)
            else:
                residue(last)

        @block.gpsimd
        def _(pool):
            chain = Chain(pool, pool_seq)
            nc.gpsimd.memset(wp[:], 0.0).then_inc(zeroed, 1)

            def split_maxima(st):
                pool.wait_ge(sm_drained, st.s * tiles + tiles)
                if st.since(2):
                    pool.wait_ge(nm_filled, st.s - 1)
                alone(pool)
                v = nm[:, st.par].rearrange("p h t -> p t h")
                chain.link(nc.gpsimd.tensor_copy(nmp[:, st.par, :, 0], v))
                chain.link(nc.gpsimd.tensor_tensor(nmr[:, st.par], v, nmp[:, st.par, :, 0], ALU.subtract), apart=True)
                chain.link(nc.gpsimd.tensor_copy(nmp[:, st.par, :, 1], nmr[:, st.par]))
                nc.gpsimd.tensor_tensor(nmp[:, st.par, :, 2], nmr[:, st.par], nmp[:, st.par, :, 1],
                                        ALU.subtract).then_inc(nmp_ready, 1)

            def low(st):
                for b in range(2):
                    pool.wait_ge(res_ready, st.s * 2 + (b + 1))
                    if st.since(1) and b == 0:
                        pool.wait_ge(p_stored, st.s * 48)
                    alone(pool)
                    chain.link(nc.gpsimd.tensor_copy(planes[:, b, 1], res[:, b]))
                    nc.gpsimd.tensor_tensor(planes[:, b, 2], res[:, b], planes[:, b, 1], ALU.subtract
                                            ).then_inc(planes_ready, 1)

            def scatter(st):
                pool.wait_ge(slot_ready, st.s + 1)
                alone(pool)
                for t in range(TT):
                    for k in range(2):
                        pool.indirect_dma_start(
                            out=hbm["xs"], out_offset=bass.IndirectOffsetOnAxis(
                                ap=slot[:, st.par, 2 * t + k:2 * t + k + 1], axis=0),
                            in_=xn[:, st.par, t], in_offset=None).then_inc(scattered[st.par], 16)

            split_maxima(Step(0, 0, 0, 0, 0))

            def step(st):
                if st.before(B - 1):
                    split_maxima(Step(st.s + 1, 1 - st.par, st.half + st.par, st.low + 1, st.high + 1))
                tail(scatter if cross else low, st)

            steps(pool, step, chain=chain, per_pair=6 if cross else 10)
            last = Step(B - 1, 1, B // 2 - 1, B - 1, B - 1)
            if cross:
                scatter(last)
                for par in range(2):
                    pool.wait_ge(scattered[par], 64 * B // 2)
            else:
                low(last)


def experts(nc, hbm, kept):
    fp32, i32 = mybir.dt.float32, mybir.dt.int32
    ALU, ACT, AX = mybir.AluOpType, mybir.ActivationFunctionType, mybir.AxisListType
    ctx = ExitStack()
    with ctx:
        def sb(name, shape, dt=fp32):
            return ctx.enter_context(nc.sbuf_tensor("e_" + name, shape, dt))

        def sem(name):
            return ctx.enter_context(nc.semaphore("e_" + name))

        def bank(name):
            return ctx.enter_context(nc.psum_tensor("e_" + name, [P, 512], fp32))

        const = sb("const", [P, NCONST])
        zeros = sb("zeros", [P, TMT, C])
        wg, wu = sb("wg", [P, 2, KT, F]), sb("wu", [P, 2, KT, F])
        wd = sb("wd", [P, 2, FM, C])
        xs = sb("xs", [P, 2, TMT, C])
        xT = sb("xT", [P, 2, KT, TM])
        silu = sb("silu", [P, 2, TM])
        hT = sb("hT", [P, 2, FM, TM])
        y = sb("y", [P, 2, TMT, C])
        over = sb("over", [P, NE, LEVELS])
        tiles = sb("tiles", [P, NE])
        below = sb("below", [P, NE, NE])
        ends = sb("ends", [P, NE])
        skip = kept["skip"]
        past = sb("past", [1, NTILE, NE])
        past2 = sb("past2", [1, NTILE, NE])
        expf = sb("expf", [1, NTILE])
        rowf = sb("rowf", [1, NTILE])
        expert_of = sb("expert_of", [1, NTILE], i32)
        row_of = sb("row_of", [1, NTILE], i32)
        tail_of = sb("tail_of", [1, NE], i32)
        tailf = sb("tailf", [1, NE])
        g_bank = [bank(f"g{i}") for i in range(2)]
        u_bank = [bank(f"u{i}") for i in range(2)]
        y_bank = [bank(f"y{i}") for i in range(2)]
        t_bank = [bank(f"t{i}") for i in range(2)]
        const_loaded, map_ready, padded = sem("const_loaded"), sem("map_ready"), sem("padded")
        zeros_set = sem("zeros_set")
        w_loaded = [sem(f"w_loaded{i}") for i in range(2)]
        xs_loaded = [sem(f"xs_loaded{i}") for i in range(2)]
        t_filled, t_drained = sem("t_filled"), sem("t_drained")
        gu_filled, g_drained, h_ready = sem("gu_filled"), sem("g_drained"), sem("h_ready")
        y_filled, y_ready = sem("y_filled"), sem("y_ready")
        y_stored = [sem(f"y_stored{i}") for i in range(2)]
        dve_seq = sem("dve_seq")
        block = ctx.enter_context(nc.Block())

        def slots(name, row):
            return hbm[name][bass.ds(row, TM)].rearrange("(t p) n -> p t n", p=P)

        @block.sync
        def _(sp):
            sp.dma_start(const[:], hbm["const"]).then_inc(const_loaded, 16)
            sp.wait_ge(map_ready, 1)
            sp.wait_ge(zeros_set, 1)
            for e in range(NE):
                row = sp.value_load(tail_of[0:1, e:e + 1], min_val=0, max_val=SPARE - TM)
                sp.dma_start(slots("xs", row), zeros[:]).then_inc(padded, 16)
            for n in range(NSPARE):
                sp.dma_start(slots("xs", SPARE + n * TM), zeros[:]).then_inc(padded, 16)
            sp.wait_ge(padded, (NE + NSPARE) * 16)

            def row(st):
                return sp.value_load(row_of[0:1, bass.ds(st.s, 1)], min_val=0, max_val=NSLOT - TM)

            def store(st):
                sp.wait_ge(y_ready, st.s + 1)
                alone(sp)
                sp.dma_start(slots("ys", st.s * TM), y[:, st.par]).then_inc(y_stored[st.par], 16)

            def load(st):
                if st.since(2):
                    sp.wait_ge(t_filled, st.s - 1)
                sp.dma_start(xs[:, st.par], slots("xs", row(st))).then_inc(xs_loaded[st.par], 16)
                e = sp.value_load(expert_of[0:1, bass.ds(st.s, 1)], min_val=0, max_val=NE - 1)
                if st.since(2):
                    sp.wait_ge(y_filled, st.s - 1)
                for name, dst in (("wg", wg), ("wu", wu), ("wd", wd)):
                    sp.dma_start(dst[:, st.par].rearrange("p k n -> p (k n)"), hbm[name][bass.ds(e, 1)].rearrange(
                        "a p n -> p (a n)")).then_inc(w_loaded[st.par], 16)
                if st.since(2):
                    store(Step(st.s - 2, st.par, st.half - 1, st.low - 2, st.high - 2))

            steps(sp, load, total=NTILE, front=2, back=1)
            for s in range(NTILE - 2, NTILE):
                store(Step(s, s % 2, s // 2, s, s))
            for par in range(2):
                sp.wait_ge(y_stored[par], ((NTILE + 1 - par) // 2) * 16)

        @block.tensor
        def _(pe):
            pe.wait_ge(const_loaded, 16)

            def turn(st):
                pe.wait_ge(xs_loaded[st.par], st.half * 16 + 16)
                if st.since(1):
                    pe.wait_ge(t_drained, st.s)
                for k in range(KT):
                    for t in range(TMT):
                        last = nc.tensor.transpose(t_bank[k][:, t * P:(t + 1) * P],
                                                   xs[:, st.par, t, k * P:(k + 1) * P], const[:, IDENT:IDENT + P])
                last.then_inc(t_filled, 1)

            turn(Step(0, 0, 0, 0, 0))

            def tile(st):
                pe.wait_ge(t_drained, st.s + 1)
                pe.wait_ge(w_loaded[st.par], st.half * 48 + 48)
                for m in range(FM):
                    if st.since(1) or m >= 2:
                        pe.wait_ge(h_ready, st.s * FM + (m - 1))
                    for out, wt in ((g_bank, wg), (u_bank, wu)):
                        for k in range(KT):
                            last = nc.tensor.matmul(out[m % 2][:, 0:TM], wt[:, st.par, k, m * P:(m + 1) * P],
                                                    xT[:, st.par, k], start=(k == 0), stop=(k == KT - 1))
                    last.then_inc(gu_filled, 1)
                if st.before(NTILE - 1):
                    turn(Step(st.s + 1, 1 - st.par, st.half + st.par, st.low + 1, st.high + 1))
                pe.wait_ge(h_ready, st.s * FM + FM)
                if st.since(1):
                    pe.wait_ge(y_ready, st.s)
                for t in range(TMT):
                    for m in range(FM):
                        last = nc.tensor.matmul(y_bank[t // 2][:, t % 2 * C:(t % 2 + 1) * C],
                                                hT[:, st.par, m, t * P:(t + 1) * P], wd[:, st.par, m],
                                                start=(m == 0), stop=(m == FM - 1))
                last.then_inc(y_filled, 1)

            steps(pe, tile, total=NTILE, front=2, back=1)

        @block.scalar
        def _(act):
            def gates(st):
                for m in range(FM):
                    act.wait_ge(gu_filled, st.s * FM + (m + 1))
                    if st.since(1) or m >= 2:
                        act.wait_ge(h_ready, st.s * FM + (m - 1))
                    nc.scalar.activation(silu[:, m % 2], g_bank[m % 2][:, 0:TM], ACT.Silu).then_inc(g_drained, 1)

            steps(act, gates, total=NTILE, front=2, back=1)

        @block.vector
        def _(dve):
            chain = Chain(dve, dve_seq)
            count = kept["count"][:]
            nc.vector.memset(zeros[:], 0.0).then_inc(zeros_set, 1)
            dve.wait_ge(const_loaded, 16)

            def table(at, *shape):
                n = 1
                for x in shape:
                    n *= x
                v = const[:, at:at + n]
                return v.rearrange("p (a b) -> p a b", b=shape[-1]) if len(shape) == 2 else v

            chain.link(nc.vector.tensor_tensor(over[:], count.unsqueeze(2).to_broadcast([P, NE, LEVELS]),
                                               table(LEVEL, NE, LEVELS), ALU.is_gt))
            chain.link(nc.vector.reduce_sum(tiles[:], over[:], AX.X))
            chain.link(nc.vector.tensor_tensor(below[:], tiles[:].unsqueeze(1).to_broadcast([P, NE, NE]),
                                               table(LOWER, NE, NE), ALU.mult))
            chain.link(nc.vector.reduce_sum(ends[:], below[:], AX.X))
            chain.link(nc.vector.tensor_scalar(skip[:], tiles[:], -float(TM), float(CAP), ALU.mult, ALU.add))
            chain.link(nc.vector.tensor_tensor(past[:], table(TILE, NTILE, NE)[0:1],
                                               ends[0:1].unsqueeze(1).to_broadcast([1, NTILE, NE]), ALU.is_ge))
            chain.link(nc.vector.reduce_sum(expf[:], past[:], AX.X))
            chain.link(nc.vector.tensor_tensor(past2[:], past[:],
                                               skip[0:1].unsqueeze(1).to_broadcast([1, NTILE, NE]), ALU.mult))
            chain.link(nc.vector.reduce_sum(rowf[:], past2[:], AX.X))
            chain.link(nc.vector.tensor_scalar(expf[:], expf[:], float(NE - 1), None, ALU.min))
            chain.link(nc.vector.tensor_copy(expert_of[:], expf[:]))
            chain.link(nc.vector.scalar_tensor_tensor(rowf[:], table(TILE, NTILE, NE)[0:1, :, 0], float(TM), rowf[:],
                                                      ALU.mult, ALU.add))
            chain.link(nc.vector.tensor_copy(row_of[:], rowf[:]))
            chain.link(nc.vector.tensor_tensor(tailf[:], kept["count"][0:1], table(REGION, NE)[0:1], ALU.add))
            nc.vector.tensor_copy(tail_of[:], tailf[:]).then_inc(map_ready, 1)

            def drain_turned(st):
                dve.wait_ge(t_filled, st.s + 1)
                if st.since(2):
                    dve.wait_ge(gu_filled, st.s * FM - FM)
                for k in range(KT):
                    last = nc.vector.tensor_copy(xT[:, st.par, k], t_bank[k][:, 0:TM])
                last.then_inc(t_drained, 1)

            drain_turned(Step(0, 0, 0, 0, 0))

            def tile(st):
                if st.since(2):
                    dve.wait_ge(y_filled, st.s - 1)
                for m in range(FM):
                    dve.wait_ge(g_drained, st.s * FM + (m + 1))
                    nc.vector.tensor_tensor(hT[:, st.par, m], u_bank[m % 2][:, 0:TM], silu[:, m % 2], ALU.mult
                                            ).then_inc(h_ready, 1)
                if st.before(NTILE - 1):
                    drain_turned(Step(st.s + 1, 1 - st.par, st.half + st.par, st.low + 1, st.high + 1))
                dve.wait_ge(y_filled, st.s + 1)
                if st.since(2):
                    dve.wait_ge(y_stored[st.par], st.half * 16)
                nc.vector.tensor_copy(y[:, st.par, 0:2].rearrange("p t n -> p (t n)"), y_bank[0][:])
                nc.vector.tensor_copy(y[:, st.par, 2], y_bank[1][:, 0:C]).then_inc(y_ready, 1)

            steps(dve, tile, total=NTILE, front=2, back=1)


def combine(nc, hbm, kept):
    fp32, u32 = mybir.dt.float32, mybir.dt.uint32
    ALU, ACT = mybir.AluOpType, mybir.ActivationFunctionType
    ctx = ExitStack()
    with ctx:
        def sb(name, shape, dt=fp32):
            return ctx.enter_context(nc.sbuf_tensor("o_" + name, shape, dt))

        def sem(name):
            return ctx.enter_context(nc.semaphore("o_" + name))

        x = sb("x", [P, 2, TT, C])
        picked = sb("picked", [P, 2, TT, 2, C])
        region = sb("region", [P, NE])
        behind = sb("behind", [P, B * TT * 2, NE - 1])
        gaps = sb("gaps", [P, B * TT * 2])
        yslot = sb("yslot", [P, B * TT * 2])
        slot = sb("slot", [P, 2, TT * 2], u32)
        gate = sb("gate", [P, 2, 2, TT])
        y = sb("y", [P, 2, TT, C])
        out = sb("out", [P, 2, TT, C])
        stats = sb("stats", [P, TT, 6])
        mv = sb("mv", [P, 2, TT, 2])
        lnv = sb("lnv", [P, 2, TT])
        rstd = sb("rstd", [P, 2, TT])
        newton = sb("newton", [P, 2, TT])
        eps = sb("eps", [P, 1])
        eps_set, region_loaded = sem("eps_set"), sem("region_loaded")
        x_loaded = [sem(f"x_loaded{i}") for i in range(2)]
        gathered = [sem(f"gathered{i}") for i in range(2)]
        slot_ready, sum_ready, stats_ready = sem("slot_ready"), sem("sum_ready"), sem("stats_ready")
        rstd_ready, out_ready = sem("rstd_ready"), sem("out_ready")
        stored = [sem(f"stored{i}") for i in range(2)]
        dve_seq, act_seq = sem("dve_seq"), sem("act_seq")
        block = ctx.enter_context(nc.Block())

        def rows(name, st):
            return hbm[name][bass.ds(st.s, 1)].rearrange("a (t p) n -> p (a t) n", p=P)

        @block.sync
        def _(sp):
            sp.dma_start(region[:], hbm["const"][:, REGION:REGION + NE]).then_inc(region_loaded, 16)

            def step(st):
                if st.since(2):
                    sp.wait_ge(sum_ready, st.s - 1)
                sp.dma_start(x[:, st.par], rows("x2", st)).then_inc(x_loaded[st.par], 16)
                if st.since(2):
                    before = Step(st.s - 2, st.par, st.half - 1, st.low - 2, st.high - 2)
                    sp.wait_ge(out_ready, st.s - 1)
                    sp.dma_start(rows("out", before), out[:, st.par]).then_inc(stored[st.par], 16)

            steps(sp, step)
            for s in range(B - 2, B):
                sp.wait_ge(out_ready, s + 1)
                sp.dma_start(rows("out", Step(s, s % 2, s // 2, s, s)), out[:, s % 2]).then_inc(stored[s % 2], 16)
            for par in range(2):
                sp.wait_ge(stored[par], 16 * B // 2)

        @block.gpsimd
        def _(pool):
            def gather(st):
                pool.wait_ge(slot_ready, st.s + 1)
                if st.since(2):
                    pool.wait_ge(sum_ready, st.s - 1)
                alone(pool)
                for t in range(TT):
                    for k in range(2):
                        pool.indirect_dma_start(
                            out=picked[:, st.par, t, k], out_offset=None, in_=hbm["ys"],
                            in_offset=bass.IndirectOffsetOnAxis(ap=slot[:, st.par, 2 * t + k:2 * t + k + 1], axis=0),
                        ).then_inc(gathered[st.par], 16)

            steps(pool, gather)

        @block.scalar
        def _(act):
            chain = Chain(act, act_seq)
            nc.scalar.preload_act_table_set("natural_log_exp_and_others")
            act.wait_ge(eps_set, 1)

            def spread(st):
                act.wait_ge(stats_ready, st.s + 1)
                chain.link(nc.scalar.activation(lnv[:, st.par], mv[:, st.par, :, 1], ACT.Ln, bias=eps[:]))
                nc.scalar.activation(rstd[:, st.par], lnv[:, st.par], ACT.Exp, scale=-0.5).then_inc(rstd_ready, 1)

            steps(act, spread, chain=chain, per_pair=2)

        @block.vector
        def _(dve):
            chain = Chain(dve, dve_seq)
            nc.vector.memset(eps[:], EPS).then_inc(eps_set, 1)
            n = B * TT * 2
            dve.wait_ge(region_loaded, 16)
            chain.link(nc.vector.tensor_tensor(
                behind[:], kept["slot"][:].unsqueeze(2).to_broadcast([P, n, NE - 1]),
                region[:, 1:].unsqueeze(1).to_broadcast([P, n, NE - 1]), ALU.is_ge))
            chain.link(nc.vector.tensor_tensor(
                behind[:], behind[:], kept["skip"][:, 0:NE - 1].unsqueeze(1).to_broadcast([P, n, NE - 1]), ALU.mult))
            chain.link(nc.vector.reduce_sum(gaps[:], behind[:], mybir.AxisListType.X))
            chain.link(nc.vector.tensor_tensor(yslot[:], kept["slot"][:], gaps[:], ALU.subtract))

            def address(st):
                nc.vector.tensor_copy(gate[:, st.par].rearrange("p k t -> p (k t)"),
                                      kept["gate"][:, bass.ds(st.s * 2 * TT, 2 * TT)])
                if st.since(2):
                    dve.wait_ge(gathered[st.par], st.half * 64)
                nc.vector.tensor_copy(slot[:, st.par], yslot[:, bass.ds(st.s * 2 * TT, 2 * TT)]
                                      ).then_inc(slot_ready, 1)

            def add(st):
                dve.wait_ge(x_loaded[st.par], st.half * 16 + 16)
                dve.wait_ge(gathered[st.par], st.half * 64 + 64)
                dve.wait_ge(slot_ready, st.s + 1)
                if st.since(2):
                    dve.wait_ge(out_ready, st.s - 1)
                for t in range(TT):
                    last = nc.vector.scalar_tensor_tensor(y[:, st.par, t], picked[:, st.par, t, 0],
                                                          gate[:, st.par, 0, t:t + 1], x[:, st.par, t],
                                                          ALU.mult, ALU.add)
                chain.link(last)
                for t in range(TT):
                    last = nc.vector.scalar_tensor_tensor(y[:, st.par, t], picked[:, st.par, t, 1],
                                                          gate[:, st.par, 1, t:t + 1], y[:, st.par, t],
                                                          ALU.mult, ALU.add)
                last.then_inc(sum_ready, 1)
                dve.wait_ge(sum_ready, st.s + 1)
                for t in range(TT):
                    last = nc.vector.bn_stats(stats[:, t], y[:, st.par, t])
                chain.link(last, apart=True)
                for t in range(TT):
                    last = nc.vector.bn_aggr(mv[:, st.par, t], stats[:, t])
                last.then_inc(stats_ready, 1)

            def norm(st):
                dve.wait_ge(rstd_ready, st.s + 1)
                r, t1, var = rstd[:, st.par], newton[:, st.par], mv[:, st.par, :, 1]
                chain.link(nc.vector.tensor_tensor(t1, r, r, ALU.mult))
                chain.link(nc.vector.scalar_tensor_tensor(t1, var, EPS, t1, ALU.add, ALU.mult))
                chain.link(nc.vector.tensor_scalar(t1, t1, -0.5, 1.5, ALU.mult, ALU.add))
                chain.link(nc.vector.tensor_tensor(t1, t1, r, ALU.mult))
                if st.since(2):
                    dve.wait_ge(stored[st.par], st.half * 16)
                for t in range(TT):
                    last = nc.vector.tensor_scalar(out[:, st.par, t], y[:, st.par, t], mv[:, st.par, t, 0:1],
                                                   newton[:, st.par, t:t + 1], ALU.subtract, ALU.mult)
                last.then_inc(out_ready, 1)

            address(Step(0, 0, 0, 0, 0))

            def step(st):
                if st.before(B - 1):
                    address(Step(st.s + 1, 1 - st.par, st.half + st.par, st.low + 1, st.high + 1))
                add(st)
                if st.since(1):
                    norm(Step(st.s - 1, 1 - st.par, st.half - (1 - st.par), st.low - 1, st.high - 1))

            steps(dve, step, chain=chain, per_pair=12)
            norm(Step(B - 1, 1, B // 2 - 1, B - 1, B - 1))


def program(nc, hbm):
    fp32, bf16 = mybir.dt.float32, mybir.dt.bfloat16

    def scratch(name, shape, dt=fp32):
        hbm[name] = nc.dram_tensor("scratch_" + name, shape, dt, kind="Internal").ap()

    scratch("q1", [B, 3, C, N], bf16)
    scratch("k1", [B, 3, C, N], bf16)
    scratch("v1", [B, N, H * 2 * D])
    scratch("q2", [B, 3, C, N], bf16)
    scratch("k2", [B, 3, C, NK], bf16)
    scratch("v2", [B, N, H * 2 * D])
    scratch("x1", [B, N, C])
    scratch("x2", [B, N, C])
    scratch("xs", [NSLOT, C])
    scratch("ys", [NTILE * TM, C])
    with ExitStack() as ctx:
        kept = {
            "slot": ctx.enter_context(nc.sbuf_tensor("slots", [P, B * TT * 2], fp32)),
            "gate": ctx.enter_context(nc.sbuf_tensor("gates", [P, B * TT * 2], fp32)),
            "skip": ctx.enter_context(nc.sbuf_tensor("skips", [P, NE], fp32)),
            "count": ctx.enter_context(nc.sbuf_tensor("counts", [P, NE], fp32)),
        }
        project_first(nc, hbm)
        attention(nc, hbm, kept, cross=False)
        attention(nc, hbm, kept, cross=True)
        experts(nc, hbm, kept)
        combine(nc, hbm, kept)


def constants():
    import numpy as np
    p = np.arange(P)[:, None]
    out = np.zeros((P, NCONST), np.float32)
    out[:, IDENT:IDENT + P] = p == np.arange(P)
    out[:, UPPER:UPPER + P] = p < np.arange(P)
    for t in range(TT):
        apart = np.abs(t * P + p - (W0[t] + np.arange(WIN)))
        out[:, MASK + t * WIN:MASK + (t + 1) * WIN] = np.where(apart <= BAND, 0.0, MASKED)
    out[:, EXPERT:EXPERT + NE] = np.arange(NE)
    out[:, LEVEL:LEVEL + NE * LEVELS] = np.tile(np.arange(LEVELS) * TM, NE)
    out[:, LOWER:LOWER + NE * NE] = (np.arange(NE)[:, None] >= np.arange(NE)).reshape(-1)
    out[:, TILE:TILE + NTILE * NE] = np.repeat(np.arange(NTILE), NE)
    out[:, REGION:REGION + NE] = np.arange(NE) * CAP
    return out


def kernel(x, ctx_2048, L0_attn_Wqkv, L0_attn_Wproj, L0_attn_bproj, L0_xattn_w_qkv, L0_xattn_w_proj,
           L0_xattn_b_proj, L0_ffn_router_w, L0_ffn_router_b, L0_ffn_gate_w, L0_ffn_up_w, L0_ffn_down_w):
    import numpy as np
    import concourse.bacc as bacc
    from concourse.bass_utils import run_bass_kernel_spmd

    def lay(a, *order):
        return np.ascontiguousarray(np.transpose(np.asarray(a), order))

    def up(a):
        a = np.asarray(a).reshape(NE, F, KT, P)
        return np.ascontiguousarray(a.transpose(0, 3, 2, 1).reshape(NE, P, KT * F))

    def down(a):
        a = np.asarray(a).reshape(NE, C, FM, P)
        return np.ascontiguousarray(a.transpose(0, 3, 2, 1).reshape(NE, P, FM * C))

    arrays = {
        "x": np.ascontiguousarray(x), "xT": lay(x, 0, 2, 1),
        "ctx": np.ascontiguousarray(ctx_2048), "ctxT": lay(ctx_2048, 0, 2, 1),
        "wqkv": np.ascontiguousarray(L0_attn_Wqkv), "wp1": np.ascontiguousarray(L0_attn_Wproj),
        "bp1": np.asarray(L0_attn_bproj).reshape(1, C),
        "wx": lay(L0_xattn_w_qkv, 1, 0), "wp2": lay(L0_xattn_w_proj, 1, 0),
        "bp2": np.asarray(L0_xattn_b_proj).reshape(1, C),
        "rw": lay(L0_ffn_router_w, 1, 0), "rb": np.asarray(L0_ffn_router_b).reshape(1, NE),
        "wg": up(L0_ffn_gate_w), "wu": up(L0_ffn_up_w), "wd": down(L0_ffn_down_w),
        "const": constants(),
    }
    nc = bacc.Bacc("TRN2", target_bir_lowering=False, num_devices=1)
    hbm = {n: nc.dram_tensor("in_" + n, a.shape, mybir.dt.from_np(a.dtype), kind="ExternalInput").ap()
           for n, a in arrays.items()}
    hbm["out"] = nc.dram_tensor("out_x", [B, N, C], mybir.dt.float32, kind="ExternalOutput").ap()
    program(nc, hbm)
    r = run_bass_kernel_spmd(nc, [{"in_" + n: a for n, a in arrays.items()}], core_ids=[0])
    return r.results[0]["out_x"]
```

```python
import concourse.bass as bass
from concourse import mybir
from contextlib import ExitStack

B, N, C, H, D = 16, 256, 256, 16, 16
NCTX = 77
BAND = 8
P = 128
TT = N // P
KT = C // P
WIN = P + BAND
W0 = [0, N - WIN]
NK = N + NCTX
EPS = 1e-5
SCALE = float(D) ** -0.5
NE, F = 8, 1024
FM = F // P
TM = 384
TMT = TM // P
WDQ = 4
NTILE = (2 * B * N + NE * (TM - 1)) // TM
CAP = B * N + TM
SPARE = NE * CAP
NSPARE = NTILE - 2 * B * N // TM
NSLOT = SPARE + NSPARE * TM
LEVELS = (B * N + TM - 1) // TM
NTOK = B * N // P
UNITS, HU = 4, 4
MASKED = -1e30
PLANES = {"q": [(0, 3), (0, 2), (0, 1)], "k": [(0, 3), (1, 3), (2, 3)]}
ROWS = 6 * D
HALVES = 2
SIZES = [P, P, TT * WIN, NE, NE * LEVELS, NE * NE, NTILE * NE, NE]
IDENT, UPPER, MASK, EXPERT, LEVEL, LOWER, TILE, REGION, NCONST = [sum(SIZES[:i]) for i in range(9)]


class Step:

    def __init__(self, s, par, half, low, high):
        self.s, self.par, self.half, self.low, self.high = s, par, half, low, high

    def since(self, n):
        return self.low >= n

    def before(self, n):
        return self.high < n


def steps(eng, body, total=B, front=4, back=2, chain=None, per_pair=0):
    for s in range(front):
        body(Step(s, s % 2, s // 2, s, s))
    pairs = (total - front - back) // 2
    start = chain.at if chain else 0
    with eng.Fori(0, pairs) as i:
        if chain:
            chain.at, chain.inside = i * per_pair + start, 0
        for par in range(2):
            body(Step(i * 2 + (front + par), par, i + front // 2, front + par, total - back - 2 + par))
        if chain:
            assert chain.inside == per_pair, chain.inside
    if chain:
        chain.at, chain.inside = start + pairs * per_pair, None
    for s in range(total - back, total):
        body(Step(s, s % 2, s // 2, s, s))


def alone(eng):
    eng.nop(nofuse=True)


class Chain:

    def __init__(self, eng, sem):
        self.eng, self.sem, self.at, self.inside = eng, sem, 0, None

    def link(self, ins, apart=False):
        self.at = self.at + 1
        if self.inside is not None:
            self.inside += 1
        ins.then_inc(self.sem, 1)
        self.eng.wait_ge(self.sem, self.at)
        if apart:
            alone(self.eng)


def kept_at(b, plane):
    return 2 - plane if b else plane


def project_first(nc, hbm, kept):
    fp32, bf16 = mybir.dt.float32, mybir.dt.bfloat16
    ALU = mybir.AluOpType
    ctx = ExitStack()
    with ctx:
        def sb(name, shape, dt=fp32):
            return ctx.enter_context(nc.sbuf_tensor(name, shape, dt))

        def sem(name):
            return ctx.enter_context(nc.semaphore(name))

        w = sb("a_w", [P, KT, 3 * C])
        xT = sb("a_xT", [P, 2, KT, N])
        cT = sb("a_cT", [P, 2, KT * NCTX])
        res = sb("a_res", [P, 2, 2, KT * N])
        planes = sb("a_planes", [P, 2, 2, 3, KT * N], bf16)
        cres = sb("a_cres", [P, 2, KT * NCTX])
        cplanes = sb("a_cplanes", [P, 2, 3, KT * NCTX], bf16)
        vo = sb("a_vo", [P, 2, TT, H, 2 * D])
        ps = [[ctx.enter_context(nc.psum_tensor(f"a_ps{a}{b}", [P, 512], fp32)) for b in range(3)]
              for a in range(2)]
        weights_loaded, kept_loaded, zeroed = sem("a_weights_loaded"), sem("a_kept_loaded"), sem("a_zeroed")
        x_loaded = [sem(f"a_x_loaded{i}") for i in range(2)]
        ones_set = sem("a_ones_set")
        q_filled, k_filled, v_filled = sem("a_q_filled"), sem("a_k_filled"), sem("a_v_filled")
        high_ready, res_ready, mid_ready = sem("a_high_ready"), sem("a_res_ready"), sem("a_mid_ready")
        v_ready, low_ready = sem("a_v_ready"), sem("a_low_ready")
        stored = [sem(f"a_stored{i}") for i in range(2)]
        pool_seq = sem("a_pool_seq")
        block = ctx.enter_context(nc.Block())

        @block.sync
        def _(sp):
            sp.dma_start(w[:], hbm["wqkv"].rearrange("(k p) n -> p k n", p=P)).then_inc(weights_loaded, 16)

            def load(st):
                if st.since(2):
                    sp.wait_ge(v_filled, st.s - 1)
                    sp.wait_ge(low_ready, st.s * 3 - 3)
                    alone(sp)
                sp.dma_start(xT[:, st.par], hbm["xT"][bass.ds(st.s, 1)].rearrange("a (k p) t -> p (a k) t", p=P)
                             ).then_inc(x_loaded[st.par], 16)
                sp.dma_start(cT[:, st.par].rearrange("p (k t) -> p k t", k=KT),
                             hbm["ckT"][bass.ds(st.s, 1)].rearrange("a (k p) t -> p (a k) t", p=P)
                             ).then_inc(x_loaded[st.par], 16)
                if st.since(2):
                    store(Step(st.s - 2, st.par, st.half - 1, st.low - 2, st.high - 2))

            def store(st):
                for b, name in ((0, "q1"), (1, "k1")):
                    sp.wait_ge(low_ready, st.s * 3 + (b + 2))
                    alone(sp)
                    sp.dma_start(hbm[name][bass.ds(st.s, 1)].rearrange("a l (m p) t -> p (a l) m t", p=P),
                                 planes[:, st.par, b].rearrange("p l (m t) -> p l m t", m=KT)
                                 ).then_inc(stored[st.par], 16)
                sp.dma_start(hbm["k2"][bass.ds(st.s, 1), :, :, N:].rearrange("a l (m p) t -> p (a l) m t", p=P),
                             cplanes[:, st.par].rearrange("p l (m t) -> p l m t", m=KT)
                             ).then_inc(stored[st.par], 16)
                sp.wait_ge(v_ready, st.s + 1)
                alone(sp)
                sp.dma_start(hbm["v1"][bass.ds(st.s, 1)].rearrange("a (t p) n -> p (a t) n", p=P),
                             vo[:, st.par].rearrange("p t h d -> p t (h d)")).then_inc(stored[st.par], 16)

            steps(sp, load)
            for s in range(B - 2, B):
                store(Step(s, s % 2, s // 2, s, s))
            for par in range(2):
                sp.wait_ge(stored[par], 64 * B // 2)
            sp.wait_ge(kept_loaded, 16 * kept["loads"])

        @block.tensor
        def _(pe):
            pe.wait_ge(weights_loaded, 16)

            def project(st):
                pe.wait_ge(x_loaded[st.par], st.half * 32 + 32)
                if st.since(2):
                    pe.wait_ge(res_ready, st.s * 3 - 3)
                    pe.wait_ge(v_ready, st.s - 1)
                for b, filled in ((0, q_filled), (1, k_filled)):
                    for m in range(KT):
                        for k in range(KT):
                            last = nc.tensor.matmul(ps[st.par][b][:, m * N:(m + 1) * N],
                                                    w[:, k, b * C + m * P:b * C + (m + 1) * P],
                                                    xT[:, st.par, k], start=(k == 0), stop=(k == KT - 1))
                    last.then_inc(filled, 1)
                for t in range(TT):
                    for k in range(KT):
                        last = nc.tensor.matmul(ps[st.par][2][:, t * C:(t + 1) * C],
                                                xT[:, st.par, k, t * P:(t + 1) * P], w[:, k, 2 * C:],
                                                start=(k == 0), stop=(k == KT - 1))
                last.then_inc(v_filled, 1)

            steps(pe, project)

        @block.scalar
        def _(act):
            for j in range(HU):
                for name in ("wp1", "wp2"):
                    if j == 0:
                        act.wait_ge(zeroed, 1 if name == "wp1" else 2)
                    act.dma_start(kept[name][32 * j:32 * j + D], hbm[name].rearrange(
                        "(a j d) n -> j d a n", j=HU, d=D)[j]).then_inc(kept_loaded, 16)
            act.dma_start(kept["wp1"][D:D + 1, 0], hbm["bp1"]).then_inc(kept_loaded, 16)
            act.dma_start(kept["wp2"][D:D + 1, 0], hbm["bp2"]).then_inc(kept_loaded, 16)
            act.dma_start(kept["wx"][:], hbm["wx"].rearrange("(k p) n -> p k n", p=P)).then_inc(kept_loaded, 16)
            act.dma_start(kept["const"][:], hbm["const"]).then_inc(kept_loaded, 16)
            act.dma_start(kept["rw"][:], hbm["rw"].rearrange("(k p) e -> p k e", p=P)).then_inc(kept_loaded, 16)
            for t in range(TT):
                act.dma_start(kept["rb"][:, t], hbm["rb"].to_broadcast([P, NE])).then_inc(kept_loaded, 16)
            act.wait_ge(ones_set, 1)

            def split(st):
                if st.since(2):
                    act.wait_ge(stored[st.par], st.half * 64)
                act.wait_ge(x_loaded[st.par], st.half * 32 + 32)
                nc.scalar.copy(cplanes[:, st.par, kept_at(1, 0)], cT[:, st.par]).then_inc(high_ready, 1)
                for b, filled in ((0, q_filled), (1, k_filled)):
                    act.wait_ge(filled, st.s + 1)
                    nc.scalar.copy(planes[:, st.par, b, kept_at(b, 0)], ps[st.par][b][:]).then_inc(high_ready, 1)
                act.wait_ge(res_ready, st.s * 3 + 1)
                nc.scalar.copy(cplanes[:, st.par, kept_at(1, 1)], cres[:, st.par]).then_inc(mid_ready, 1)
                for b in range(2):
                    act.wait_ge(res_ready, st.s * 3 + (b + 2))
                    nc.scalar.copy(planes[:, st.par, b, kept_at(b, 1)], res[:, st.par, b]).then_inc(mid_ready, 1)
                act.wait_ge(v_filled, st.s + 1)
                nc.scalar.copy(vo[:, st.par, :, :, 0:D],
                               ps[st.par][2][:].rearrange("p (t h d) -> p t h d", t=TT, h=H)).then_inc(v_ready, 1)

            steps(act, split)

        @block.vector
        def _(dve):
            nc.vector.memset(vo[:, :, :, :, D:], 1.0).then_inc(ones_set, 1)

            def split(st):
                dve.wait_ge(high_ready, st.s * 3 + 1)
                nc.vector.tensor_tensor(cres[:, st.par], cT[:, st.par], cplanes[:, st.par, kept_at(1, 0)],
                                        ALU.subtract).then_inc(res_ready, 1)
                for b in range(2):
                    dve.wait_ge(high_ready, st.s * 3 + (b + 2))
                    nc.vector.tensor_tensor(res[:, st.par, b], ps[st.par][b][:],
                                            planes[:, st.par, b, kept_at(b, 0)], ALU.subtract).then_inc(res_ready, 1)
                dve.wait_ge(mid_ready, st.s * 3 + 1)
                nc.vector.tensor_tensor(cplanes[:, st.par, kept_at(1, 2)], cres[:, st.par],
                                        cplanes[:, st.par, kept_at(1, 1)], ALU.subtract).then_inc(low_ready, 1)
                for b in range(2):
                    dve.wait_ge(mid_ready, st.s * 3 + (b + 2))
                    nc.vector.tensor_tensor(planes[:, st.par, b, kept_at(b, 2)], res[:, st.par, b],
                                            planes[:, st.par, b, kept_at(b, 1)], ALU.subtract).then_inc(low_ready, 1)

            steps(dve, split)
            dve.wait_ge(kept_loaded, 16 * kept["loads"])
            const = kept["const"]
            nc.vector.tensor_copy(kept["identb"][:], const[:, IDENT:IDENT + P])
            nc.vector.tensor_copy(kept["trib"][:], const[:, UPPER:UPPER + P])
            nc.vector.tensor_copy(kept["maskb"][:].rearrange("p t n -> p (t n)"), const[:, MASK:MASK + TT * WIN])
            for i in range(2 * TT):
                nc.vector.tensor_copy(kept["iota4"][:, i], const[:, EXPERT:EXPERT + NE])

        @block.gpsimd
        def _(pool):
            nc.gpsimd.memset(kept["wp1"][:], 0.0).then_inc(zeroed, 1)
            pool.wait_ge(zeroed, 1)
            nc.gpsimd.memset(kept["wp2"][:], 0.0).then_inc(zeroed, 1)
            pool.wait_ge(zeroed, 2)
            chain = Chain(pool, pool_seq)
            chain.link(nc.gpsimd.memset(kept["ks"][ROWS:ROWS + 3], 1.0))
            chain.link(nc.gpsimd.memset(kept["va"][:, :, :, :, D:], 1.0))
            chain.link(nc.gpsimd.memset(kept["onesb"][:], 1.0))
            chain.link(nc.gpsimd.memset(kept["eps"][:], EPS))
            chain.link(nc.gpsimd.memset(kept["count"][:], 0.0))


def attention(nc, hbm, kept, cross):
    fp32, bf16, i32, u32 = mybir.dt.float32, mybir.dt.bfloat16, mybir.dt.int32, mybir.dt.uint32
    ALU, ACT, AX = mybir.AluOpType, mybir.ActivationFunctionType, mybir.AxisListType
    u = "c_" if cross else "b_"
    keys = NK if cross else N
    qd, kd, vd = (hbm[n + ("2" if cross else "1")] for n in "qkv")
    x_in, x_out = (hbm["x1"], hbm["x2"]) if cross else (hbm["x"], hbm["x1"])
    wide = TT * N if cross else TT * WIN
    tiles = H * TT if cross else H
    chunks = 3 if cross else 2
    ctx = ExitStack()
    with ctx:
        def sb(name, shape, dt=fp32):
            return ctx.enter_context(nc.sbuf_tensor(u + name, shape, dt))

        def sem(name):
            return ctx.enter_context(nc.semaphore(u + name))

        def bank(name):
            return ctx.enter_context(nc.psum_tensor(u + name, [P, 512], fp32))

        qs, ks, va = kept["qs"], kept["ks"], kept["va"]
        resid = sb("resid", [P, 2, TT, C])
        pm = sb("pm", [P, 2, HU, wide])
        pt = sb("pt", [NCTX, 2, HU, N]) if cross else None
        nm = sb("nm", [P, 2, H, TT])
        nmr = sb("nmr", [P, 2, TT, H])
        nmp = sb("nmp", [P, 2, TT, 3, H], bf16)
        nmT = sb("nmT", [3 * H, 2, N], bf16)
        turned = sb("turned", [P, 2, N])
        rden = sb("rden", [P, 2, N // 32, 1])
        on = sb("on", [P, UNITS, N])
        wp = kept["wp2" if cross else "wp1"]
        y = sb("y", [P, 2, TT, C])
        stats = sb("stats", [P, TT, 6])
        mv = sb("mv", [P, 2, TT, 2])
        lnv = sb("lnv", [P, 2, TT])
        rstd = sb("rstd", [P, 2, TT])
        newton = sb("newton", [P, 2, TT])
        xn = sb("xn", [P, 2, TT, C])
        xnT = sb("xnT", [P, KT, N])
        const, identb, maskb, eps = kept["const"], kept["identb"], kept["maskb"], kept["eps"]
        ident = const[:, IDENT:IDENT + P]
        if cross:
            rw, rb, trib, onesb, iota4 = (kept[n] for n in ("rw", "rb", "trib", "onesb", "iota4"))
            logit = sb("logit", [P, TT, NE])
            top = sb("top", [P, TT, 8])
            topi = sb("topi", [P, TT, 8], u32)
            idxf = sb("idxf", [P, TT, 2])
            hot = sb("hot", [P, TT * 2, NE])
            hotb = sb("hotb", [P, TT, NE], bf16)
            gap = sb("gap", [P, TT])
            egap = sb("egap", [P, TT])
            oneg = sb("oneg", [P, TT])
            gate = sb("gate", [P, 2, TT])
            place = sb("place", [P, TT, NE])
            pick = sb("pick", [P, TT * 2, NE])
            slotf = sb("slotf", [P, TT * 2])
            slot = sb("slot", [P, 2, TT * 2], u32)
            base = kept["count"]
        else:
            w = kept["wx"]
            res = sb("res", [P, 2, KT * N])
            planes = sb("planes", [P, 2, 3, KT * N], bf16)
            vo = sb("vo", [P, TT, H, 2 * D])
        st_bank = [bank(f"st{i}") for i in range(2)]
        tl_bank = bank("tl")
        sm_bank = [bank(f"sm{i}") for i in range(2)]
        pv_bank = bank("pv")
        m0, m1 = bank("m0"), bank("m1")

        ones_set = sem("ones_set")
        qk_loaded = [[sem(f"qk_loaded{a}{b}") for b in range(HALVES)] for a in range(2)]
        nm_loaded = [sem(f"nm_loaded{i}") for i in range(2)]
        rest_loaded = [sem(f"rest_loaded{i}") for i in range(2)]
        sm_filled, sm_drained = sem("sm_filled"), sem("sm_drained")
        st_filled, st_drained = sem("st_filled"), sem("st_drained")
        tl_filled, tl_drained = sem("tl_filled"), sem("tl_drained")
        pv_filled, pv_drained, on_ready = sem("pv_filled"), sem("pv_drained"), sem("on_ready")
        nmp_ready, nm_filled, nm_drained = sem("nmp_ready"), sem("nm_filled"), sem("nm_drained")
        op_filled, op_drained = sem("op_filled"), sem("op_drained")
        stats_ready, rstd_ready, xn_ready = sem("stats_ready"), sem("rstd_ready"), sem("xn_ready")
        tr_filled, tr_drained = sem("tr_filled"), sem("tr_drained")
        dve_seq, act_seq, pool_seq = sem("dve_seq"), sem("act_seq"), sem("pool_seq")
        x_stored = [sem(f"x_stored{i}") for i in range(2)]
        if cross:
            lg_filled, lg_drained = sem("lg_filled"), sem("lg_drained")
            hot_ready, rk_filled, rk_drained = sem("hot_ready"), sem("rk_filled"), sem("rk_drained")
            gap_ready, egap_ready = sem("gap_ready"), sem("egap_ready")
            slot_ready = sem("slot_ready")
            scattered = [sem(f"scattered{i}") for i in range(2)]
        else:
            q_filled, k_filled, v_filled = sem("q_filled"), sem("k_filled"), sem("v_filled")
            high_ready, res_ready = sem("high_ready"), sem("res_ready")
            v_drained, planes_ready = sem("v_drained"), sem("planes_ready")
            p_stored = sem("p_stored")
        block = ctx.enter_context(nc.Block())

        def tail(body, st):
            if st.since(1):
                body(Step(st.s - 1, 1 - st.par, st.half - (1 - st.par), st.low - 1, st.high - 1))

        @block.sync
        def _(sp):
            def load_qk(s, par, half):
                hs = slice(half * H // HALVES, (half + 1) * H // HALVES)
                for name, dst, src, n in (("q", qs, qd, N), ("k", ks, kd, keys)):
                    view, row = src.rearrange("s l (d h) t -> s (l d) h t", h=H), 0
                    for lo, hi in PLANES[name]:
                        sp.dma_start(dst[row:row + (hi - lo) * D, par, hs, 0:n],
                                     view[bass.ds(s, 1), lo * D:hi * D, hs].rearrange("a p h t -> p (a h) t")
                                     ).then_inc(qk_loaded[par][half], 16)
                        row += (hi - lo) * D

            def load_rest(s, par):
                sp.dma_start(va[:, par, 0:TT].rearrange("p t h d -> p t (h d)"),
                             vd[bass.ds(s, 1)].rearrange("a (t p) n -> p (a t) n", p=P)).then_inc(rest_loaded[par], 16)
                sp.dma_start(resid[:, par], x_in[bass.ds(s, 1)].rearrange("a (t p) n -> p (a t) n", p=P)
                             ).then_inc(rest_loaded[par], 16)
                if cross:
                    sp.dma_start(va[0:NCTX, par, TT, :, 0:D], hbm["ctx"][bass.ds(s, 1), :, C:].rearrange(
                        "a p (h d) -> p (a h) d", h=H)).then_inc(rest_loaded[par], 16)

            for s in range(2):
                for half in range(HALVES):
                    load_qk(s, s, half)
                load_rest(s, s)

            def store_x(st):
                sp.wait_ge(xn_ready, st.s + 1)
                sp.dma_start(x_out[bass.ds(st.s, 1)].rearrange("a (t p) n -> p (a t) n", p=P), xn[:, st.par]
                             ).then_inc(x_stored[st.par], 16)

            def store_projected(st):
                sp.wait_ge(planes_ready, st.s * 2 + 2)
                for b, name in ((0, "q2"), (1, "k2")):
                    sp.dma_start(hbm[name][bass.ds(st.s, 1), :, :, 0:N].rearrange(
                        "a l (m p) t -> p (a l) m t", p=P), planes[:, b].rearrange(
                        "p l (m t) -> p l m t", m=KT)).then_inc(p_stored, 16)
                sp.wait_ge(v_drained, st.s + 1)
                alone(sp)
                sp.dma_start(hbm["v2"][bass.ds(st.s, 1)].rearrange("a (t p) n -> p (a t) n", p=P),
                             vo[:].rearrange("p t h d -> p t (h d)")).then_inc(p_stored, 16)

            def step(st):
                for half in range(HALVES):
                    if st.before(B - 2):
                        if cross:
                            sp.wait_ge(tl_filled, st.s * (H // 2) + (half + 1) * (H // 2 // HALVES))
                        else:
                            sp.wait_ge(st_filled, st.s * H + (half + 1) * (H // HALVES))
                        load_qk(st.s + 2, st.par, half)
                    if half == 0:
                        tail(store_x, st)
                if not cross:
                    tail(store_projected, st)
                if st.before(B - 2):
                    sp.wait_ge(pv_filled, st.s * UNITS + UNITS)
                    alone(sp)
                    sp.wait_ge(op_drained, st.s + 1)
                    alone(sp)
                    load_rest(st.s + 2, st.par)

            steps(sp, step)
            last = Step(B - 1, 1, B // 2 - 1, B - 1, B - 1)
            store_x(last)
            if not cross:
                store_projected(last)
                sp.wait_ge(p_stored, 48 * B)
            for par in range(2):
                sp.wait_ge(x_stored[par], 16 * B // 2)

        @block.tensor
        def _(pe):
            def maximum(st, n):
                h, t = (n // TT, n % TT) if cross else (n, 0)
                if h % (H // HALVES) == 0 and t == 0:
                    pe.wait_ge(qk_loaded[st.par][h // (H // HALVES)], (st.half + 1) * 6 * 16)
                if st.since(1) or n >= 2:
                    pe.wait_ge(sm_drained, st.s * tiles + (n - 1))
                out = sm_bank[n % 2]
                if cross:
                    last = nc.tensor.matmul(out[:, 0:NK], qs[0:ROWS, st.par, h, t * P:(t + 1) * P],
                                            ks[0:ROWS, st.par, h, 0:NK], start=True, stop=True)
                else:
                    nc.tensor.matmul(out[:, 0:TT * WIN], identb[:], maskb[:], start=True, stop=False,
                                     skip_group_check=True)
                    for t in range(TT):
                        last = nc.tensor.matmul(
                            out[:, t * WIN:(t + 1) * WIN], qs[0:ROWS, st.par, h, t * P:(t + 1) * P],
                            ks[0:ROWS, st.par, h, W0[t]:W0[t] + WIN], start=False, stop=(t == TT - 1),
                            skip_group_check=True)
                last.then_inc(sm_filled, 1)

            def scores(st, h):
                if h == 0:
                    pe.wait_ge(nm_loaded[st.par], st.half * 48 + 48)
                if st.since(1) or h >= 2:
                    pe.wait_ge(st_drained, st.s * H + (h - 1))
                out = st_bank[h % 2]
                if cross:
                    for c in range(TT):
                        last = nc.tensor.matmul(out[:, c * N:(c + 1) * N], ks[:, st.par, h, c * P:(c + 1) * P],
                                                qs[:, st.par, h], start=True, stop=True)
                else:
                    nc.tensor.matmul(out[:, 0:TT * WIN], identb[:], maskb[:], start=True, stop=False,
                                     skip_group_check=True)
                    for c in range(TT):
                        last = nc.tensor.matmul(
                            out[:, c * WIN:(c + 1) * WIN], ks[:, st.par, h, c * P:(c + 1) * P],
                            qs[:, st.par, h, W0[c]:W0[c] + WIN], start=False, stop=(c == TT - 1),
                            skip_group_check=True)
                last.then_inc(st_filled, 1)

            def scores_context(st, pair):
                if st.since(1) or pair >= 1:
                    pe.wait_ge(tl_drained, st.s * (H // 2) + pair)
                for e in range(2):
                    last = nc.tensor.matmul(tl_bank[0:NCTX, e * N:(e + 1) * N],
                                            ks[:, st.par, pair * 2 + e, N:], qs[:, st.par, pair * 2 + e],
                                            start=True, stop=True)
                last.then_inc(tl_filled, 1)

            def weigh(st, g, c):
                if c == 0:
                    if g == 0:
                        pe.wait_ge(rest_loaded[st.par], (st.half + 1) * (3 if cross else 2) * 16)
                    pe.wait_ge(st_drained, st.s * H + (g + 1) * HU)
                    if cross:
                        pe.wait_ge(tl_drained, st.s * (H // 2) + (g + 1) * (HU // 2))
                    if st.since(1) or g >= 1:
                        pe.wait_ge(pv_drained, st.s * UNITS + g)
                for j in range(HU):
                    kc = NCTX if c == TT else P
                    lhsT = va[0:kc, st.par, c, g * HU + j]
                    if c == TT:
                        cols, rhs = slice(0, N), pt[:, g % 2, j]
                    elif cross:
                        cols, rhs = slice(0, N), pm[:, g % 2, j, c * N:(c + 1) * N]
                    else:
                        cols, rhs = slice(W0[c], W0[c] + WIN), pm[:, g % 2, j, c * WIN:(c + 1) * WIN]
                    last = nc.tensor.matmul(pv_bank[32 * j:32 * j + 32, cols], lhsT, rhs, start=(c == 0),
                                            stop=(c == chunks - 1), skip_group_check=True)
                if c == chunks - 1:
                    last.then_inc(pv_filled, 1)

            def turn_maxima(st):
                pe.wait_ge(nmp_ready, st.s + 1)
                if st.since(2):
                    pe.wait_ge(rk_drained if cross else res_ready, st.s - 1 if cross else st.s * 2 - 2)
                alone(pe)
                out = m1[0:3 * H, 0:N // 2].bitcast(bf16)
                for t in range(TT):
                    last = nc.tensor.transpose(out[:, t * P:(t + 1) * P],
                                               nmp[:, st.par, t].rearrange("p l h -> p (l h)"), identb[:])
                last.then_inc(nm_filled, 1)

            def project(st):
                pe.wait_ge(on_ready, st.s * UNITS + UNITS)
                if st.since(1):
                    pe.wait_ge(lg_drained if cross else v_drained, st.s)
                for t in range(TT):
                    for g in range(UNITS):
                        last = nc.tensor.matmul(m0[:, t * C:(t + 1) * C], on[:, g, t * P:(t + 1) * P], wp[:, g],
                                                start=(g == 0), stop=(g == UNITS - 1))
                last.then_inc(op_filled, 1)

            def turn_x(st):
                pe.wait_ge(xn_ready, st.s + 1)
                if st.before(B - 1):
                    pe.wait_ge(nm_drained, st.s + 2)
                else:
                    pe.wait_ge(nm_drained, B)
                for k in range(KT):
                    for t in range(TT):
                        last = nc.tensor.transpose(m1[:, k * N + t * P:k * N + (t + 1) * P],
                                                   xn[:, st.par, t, k * P:(k + 1) * P], ident)
                last.then_inc(tr_filled, 1)

            def project_part(b, out):
                for m in range(KT):
                    for k in range(KT):
                        last = nc.tensor.matmul(out[:, m * N:(m + 1) * N], w[:, k, b * C + m * P:b * C + (m + 1) * P],
                                                xnT[:, k], start=(k == 0), stop=(k == KT - 1))
                return last

            def project_q(st):
                pe.wait_ge(tr_drained, st.s + 1)
                pe.wait_ge(op_drained, st.s + 1)
                project_part(0, m0).then_inc(q_filled, 1)

            def project_k(st):
                project_part(1, m1).then_inc(k_filled, 1)

            def project_v(st):
                pe.wait_ge(res_ready, st.s * 2 + 1)
                for t in range(TT):
                    for k in range(KT):
                        last = nc.tensor.matmul(m0[:, t * C:(t + 1) * C], xnT[:, k, t * P:(t + 1) * P],
                                                w[:, k, 2 * C:], start=(k == 0), stop=(k == KT - 1))
                last.then_inc(v_filled, 1)

            def logits(st):
                pe.wait_ge(tr_drained, st.s + 1)
                pe.wait_ge(op_drained, st.s + 1)
                for t in range(TT):
                    for k in range(KT):
                        last = nc.tensor.matmul(m0[:, t * NE:(t + 1) * NE], xnT[:, k, t * P:(t + 1) * P], rw[:, k],
                                                start=(k == 0), stop=(k == KT - 1))
                last.then_inc(lg_filled, 1)

            def ranks(st):
                pe.wait_ge(hot_ready, st.s + 1)
                nc.tensor.matmul(m1[:, 0:NE], trib[:], hotb[:, 0], start=True, stop=True)
                nc.tensor.matmul(m1[:, NE:2 * NE], onesb[:], hotb[:, 0], start=True, stop=False)
                nc.tensor.matmul(m1[:, NE:2 * NE], trib[:], hotb[:, 1], start=False, stop=True)
                nc.tensor.matmul(m1[:, 2 * NE:3 * NE], onesb[:], hotb[:, 0], start=True, stop=False)
                nc.tensor.matmul(m1[:, 2 * NE:3 * NE], onesb[:], hotb[:, 1], start=False, stop=True
                                 ).then_inc(rk_filled, 1)

            first = Step(0, 0, 0, 0, 0)
            for n in range(tiles):
                maximum(first, n)
            turn_maxima(first)

            def step(st):
                nxt = Step(st.s + 1, 1 - st.par, st.half + st.par, st.low + 1, st.high + 1)
                n = 0

                def then(piece, *args):
                    nonlocal n
                    piece(*args)
                    if n < tiles and st.before(B - 1):
                        maximum(nxt, n)
                        n += 1

                for pair in range(H // 2):
                    then(scores, st, 2 * pair)
                    then(scores, st, 2 * pair + 1)
                    if cross:
                        then(scores_context, st, pair)
                    if pair in (2, 4, 6):
                        for c in range(chunks):
                            then(weigh, st, pair // 2 - 1, c)
                    if pair == 2:
                        then(tail, turn_x, st)
                    if pair == 3:
                        then(tail, logits if cross else project_q, st)
                    if pair == 5:
                        then(tail, ranks if cross else project_k, st)
                    if pair == 7 and not cross:
                        tail(project_v, st)
                if st.before(B - 1):
                    turn_maxima(nxt)
                for c in range(chunks):
                    weigh(st, UNITS - 1, c)
                project(st)

            steps(pe, step)
            last = Step(B - 1, 1, B // 2 - 1, B - 1, B - 1)
            turn_x(last)
            if cross:
                logits(last)
                ranks(last)
            else:
                project_q(last)
                project_k(last)
                project_v(last)

        @block.scalar
        def _(act):
            chain = Chain(act, act_seq)
            nc.scalar.preload_act_table_set("natural_log_exp_and_others")

            def probabilities(st, pair):
                g = pair // 2
                if pair % 2 == 0 and (st.since(1) or g >= 2):
                    act.wait_ge(pv_filled, st.s * UNITS + (g - 1))
                for e in range(2):
                    h = pair * 2 + e
                    act.wait_ge(st_filled, st.s * H + (h + 1))
                    nc.scalar.activation(pm[:, g % 2, h % HU], st_bank[e][:, 0:wide], ACT.Exp,
                                         scale=SCALE).then_inc(st_drained, 1)
                if cross:
                    act.wait_ge(tl_filled, st.s * (H // 2) + (pair + 1))
                    nc.scalar.activation(pt[:, g % 2, pair % 2 * 2:pair % 2 * 2 + 2], tl_bank[0:NCTX].rearrange(
                        "p (e t) -> p e t", e=2), ACT.Exp, scale=SCALE).then_inc(tl_drained, 1)

            def drain_maxima(st):
                act.wait_ge(nm_filled, st.s + 1)
                if st.since(2):
                    act.wait_ge(nm_loaded[st.par], st.half * 48)
                nc.scalar.copy(nmT[:, st.par], m1[0:3 * H, 0:N // 2].bitcast(bf16)).then_inc(nm_drained, 1)
                act.wait_ge(nm_drained, st.s + 1)
                for pl in range(3):
                    act.dma_start(qs[ROWS + pl:ROWS + pl + 1, st.par], nmT[pl * H:pl * H + H, st.par]
                                  ).then_inc(nm_loaded[st.par], 16)

            def drain_x(st):
                act.wait_ge(tr_filled, st.s + 1)
                if st.since(1):
                    act.wait_ge(lg_filled if cross else v_filled, st.s)
                nc.scalar.copy(xnT[:].rearrange("p k t -> p (k t)"), m1[:]).then_inc(tr_drained, 1)

            def high_q(st):
                if st.since(1):
                    act.wait_ge(p_stored, st.s * 48)
                act.wait_ge(q_filled, st.s + 1)
                nc.scalar.copy(planes[:, 0, kept_at(0, 0)], m0[:]).then_inc(high_ready, 1)

            def high_k(st):
                act.wait_ge(k_filled, st.s + 1)
                nc.scalar.copy(planes[:, 1, kept_at(1, 0)], m1[:]).then_inc(high_ready, 1)

            def drain_v(st):
                if not st.since(1):
                    act.wait_ge(ones_set, 1)
                act.wait_ge(v_filled, st.s + 1)
                nc.scalar.copy(vo[:, :, :, 0:D], m0[:].rearrange("p (t h d) -> p t h d", t=TT, h=H)
                               ).then_inc(v_drained, 1)

            def gates(st):
                act.wait_ge(gap_ready, st.s + 1)
                nc.scalar.activation(egap[:], gap[:], ACT.Exp).then_inc(egap_ready, 1)

            def spread(st):
                act.wait_ge(stats_ready, st.s + 1)
                chain.link(nc.scalar.activation(lnv[:, st.par], mv[:, st.par, :, 1], ACT.Ln, bias=eps[:]))
                nc.scalar.activation(rstd[:, st.par], lnv[:, st.par], ACT.Exp, scale=-0.5).then_inc(rstd_ready, 1)

            drain_maxima(Step(0, 0, 0, 0, 0))

            def step(st):
                for pair in range(H // 2):
                    probabilities(st, pair)
                    if pair == 2:
                        tail(drain_x, st)
                    if pair == 4:
                        tail(gates if cross else high_q, st)
                    if pair == 6 and not cross:
                        tail(high_k, st)
                    if pair == 7 and not cross:
                        tail(drain_v, st)
                if st.before(B - 1):
                    drain_maxima(Step(st.s + 1, 1 - st.par, st.half + st.par, st.low + 1, st.high + 1))
                spread(st)

            steps(act, step, chain=chain, per_pair=2)
            last = Step(B - 1, 1, B // 2 - 1, B - 1, B - 1)
            drain_x(last)
            if cross:
                gates(last)
            else:
                high_q(last)
                high_k(last)
                drain_v(last)

        @block.vector
        def _(dve):
            chain = Chain(dve, dve_seq)
            if not cross:
                nc.vector.memset(vo[:, :, :, D:], 1.0).then_inc(ones_set, 1)

            def maximum(st, n):
                if n == 0 and st.since(2):
                    dve.wait_ge(nmp_ready, st.s - 1)
                dve.wait_ge(sm_filled, st.s * tiles + (n + 1))
                if cross:
                    nc.vector.reduce_max(nm[:, st.par, n // TT, n % TT:n % TT + 1], sm_bank[n % 2][:, 0:NK], AX.X,
                                         negate=True).then_inc(sm_drained, 1)
                else:
                    nc.vector.reduce_max(nm[:, st.par, n], sm_bank[n % 2][:, 0:TT * WIN].rearrange(
                        "p (t n) -> p t n", t=TT), AX.X, negate=True).then_inc(sm_drained, 1)

            def normalize(st, g):
                dve.wait_ge(pv_filled, st.s * UNITS + (g + 1))
                nc.vector.transpose(turned[:, 0], pv_bank[:, 0:N]).then_inc(pv_drained, 1)
                dve.wait_ge(pv_drained, st.s * UNITS + (g + 1))
                block = turned[:, 0].rearrange("p (b r) -> p b r", r=32)
                chain.link(nc.vector.reciprocal(rden[:, 0], block[:, :, D:D + 1]))
                chain.link(nc.vector.tensor_tensor(turned[:, 1].rearrange("p (b r) -> p b r", r=32), block,
                                                   rden[:, 0].to_broadcast([P, N // 32, 32]), ALU.mult))
                if g == 0 and st.since(1):
                    dve.wait_ge(op_filled, st.s)
                nc.vector.transpose(on[:, g], turned[:, 1]).then_inc(on_ready, 1)

            def residual(st):
                dve.wait_ge(op_filled, st.s + 1)
                dve.wait_ge(rest_loaded[st.par], (st.half + 1) * (3 if cross else 2) * 16)
                nc.vector.tensor_tensor(y[:, st.par].rearrange("p t n -> p (t n)"), m0[:],
                                        resid[:, st.par].rearrange("p t n -> p (t n)"), ALU.add
                                        ).then_inc(op_drained, 1)
                dve.wait_ge(op_drained, st.s + 1)
                for t in range(TT):
                    last = nc.vector.bn_stats(stats[:, t], y[:, st.par, t])
                chain.link(last, apart=True)
                for t in range(TT):
                    last = nc.vector.bn_aggr(mv[:, st.par, t], stats[:, t])
                last.then_inc(stats_ready, 1)

            def norm(st):
                dve.wait_ge(rstd_ready, st.s + 1)
                r, t1, var = rstd[:, st.par], newton[:, st.par], mv[:, st.par, :, 1]
                chain.link(nc.vector.tensor_tensor(t1, r, r, ALU.mult))
                chain.link(nc.vector.scalar_tensor_tensor(t1, var, EPS, t1, ALU.add, ALU.mult))
                chain.link(nc.vector.tensor_scalar(t1, t1, -0.5, 1.5, ALU.mult, ALU.add))
                chain.link(nc.vector.tensor_tensor(t1, t1, r, ALU.mult))
                if st.since(2):
                    dve.wait_ge(x_stored[st.par], st.half * 16)
                    dve.wait_ge(tr_filled, st.s - 1)
                    if cross:
                        dve.wait_ge(scattered[st.par], st.half * 64)
                for t in range(TT):
                    last = nc.vector.tensor_scalar(xn[:, st.par, t], y[:, st.par, t], mv[:, st.par, t, 0:1],
                                                   newton[:, st.par, t:t + 1], ALU.subtract, ALU.mult)
                last.then_inc(xn_ready, 1)

            def residue(st, b, out):
                dve.wait_ge(high_ready, st.s * 2 + (b + 1))
                if st.since(1):
                    dve.wait_ge(planes_ready, st.s * 2)
                nc.vector.tensor_tensor(res[:, b], out[:], planes[:, b, kept_at(b, 0)], ALU.subtract
                                        ).then_inc(res_ready, 1)

            def residue_q(st):
                residue(st, 0, m0)

            def residue_k(st):
                residue(st, 1, m1)

            def choose(st):
                dve.wait_ge(lg_filled, st.s + 1)
                nc.vector.tensor_tensor(logit[:].rearrange("p t e -> p (t e)"), m0[:, 0:TT * NE],
                                        rb[:].rearrange("p t e -> p (t e)"), ALU.add).then_inc(lg_drained, 1)
                dve.wait_ge(lg_drained, st.s + 1)
                alone(dve)
                for t in range(TT):
                    last = nc.vector.max(top[:, t], logit[:, t])
                chain.link(last, apart=True)
                for t in range(TT):
                    last = nc.vector.max_index(topi[:, t], top[:, t], logit[:, t])
                chain.link(last)
                nc.vector.tensor_tensor(gap[:], top[:, :, 1], top[:, :, 0], ALU.subtract).then_inc(gap_ready, 1)
                chain.link(nc.vector.tensor_copy(idxf[:], topi[:, :, 0:2]))
                chain.link(nc.vector.tensor_tensor(
                    hot[:], iota4[:], idxf[:].rearrange("p t k -> p (t k)").unsqueeze(2).to_broadcast([P, 2 * TT, NE]),
                    ALU.is_equal))
                hv = hot[:].rearrange("p (t k) e -> p t k e", t=TT)
                nc.vector.tensor_tensor(hotb[:], hv[:, :, 0], hv[:, :, 1], ALU.add).then_inc(hot_ready, 1)
                dve.wait_ge(egap_ready, st.s + 1)
                chain.link(nc.vector.tensor_scalar(oneg[:], egap[:], 1.0, None, ALU.add))
                chain.link(nc.vector.reciprocal(gate[:, 0], oneg[:]))
                chain.link(nc.vector.tensor_tensor(gate[:, 1], egap[:], gate[:, 0], ALU.mult))
                nc.vector.tensor_copy(kept["gate"][:, bass.ds(st.s * 2 * TT, 2 * TT)],
                                      gate[:].rearrange("p k t -> p (k t)"))

            def assign(st):
                dve.wait_ge(rk_filled, st.s + 1)
                if st.since(1):
                    dve.wait_ge(rk_drained, st.s)
                ecap = const[:, REGION:REGION + NE]
                chain.link(nc.vector.tensor_tensor(
                    place[:], m1[:, 0:TT * NE].rearrange("p (t e) -> p t e", t=TT),
                    base[:].unsqueeze(1).to_broadcast([P, TT, NE]), ALU.add))
                nc.vector.tensor_tensor(base[:], m1[:, TT * NE:(TT + 1) * NE], base[:], ALU.add).then_inc(rk_drained, 1)
                chain.link(nc.vector.tensor_tensor(place[:], place[:], ecap.unsqueeze(1).to_broadcast([P, TT, NE]),
                                                   ALU.add))
                for t in range(TT):
                    last = nc.vector.tensor_tensor(pick[:, 2 * t:2 * t + 2], hot[:, 2 * t:2 * t + 2],
                                                   place[:, t:t + 1].to_broadcast([P, 2, NE]), ALU.mult)
                chain.link(last)
                chain.link(nc.vector.reduce_sum(slotf[:], pick[:], AX.X))
                if st.since(2):
                    dve.wait_ge(scattered[st.par], st.half * 64)
                nc.vector.tensor_copy(kept["slot"][:, bass.ds(st.s * 2 * TT, 2 * TT)], slotf[:])
                nc.vector.tensor_copy(slot[:, st.par], slotf[:]).then_inc(slot_ready, 1)

            first = Step(0, 0, 0, 0, 0)
            for n in range(tiles):
                maximum(first, n)

            def step(st):
                nxt = Step(st.s + 1, 1 - st.par, st.half + st.par, st.low + 1, st.high + 1)
                if cross:
                    due = [(2, tail, norm, st), (13, normalize, st, 0), (18, tail, choose, st),
                           (24, normalize, st, 1), (28, tail, assign, st)]
                else:
                    due = [(2, tail, norm, st), (9, normalize, st, 0), (14, tail, residue_q, st),
                           (16, normalize, st, 1), (16, tail, residue_k, st)]
                n = 0
                for at, what, *args in due:
                    while n < at and st.before(B - 1):
                        maximum(nxt, n)
                        n += 1
                    what(*args)
                while n < tiles and st.before(B - 1):
                    maximum(nxt, n)
                    n += 1
                normalize(st, 2)
                normalize(st, 3)
                residual(st)

            steps(dve, step, chain=chain, per_pair=2 * (8 + 1 + 4 + (7 + 4 if cross else 0)))
            last = Step(B - 1, 1, B // 2 - 1, B - 1, B - 1)
            norm(last)
            if cross:
                choose(last)
                assign(last)
            else:
                residue_q(last)
                residue_k(last)

        @block.gpsimd
        def _(pool):
            chain = Chain(pool, pool_seq)

            def split_maxima(st):
                pool.wait_ge(sm_drained, st.s * tiles + tiles)
                if st.since(2):
                    pool.wait_ge(nm_filled, st.s - 1)
                alone(pool)
                v = nm[:, st.par].rearrange("p h t -> p t h")
                chain.link(nc.gpsimd.tensor_copy(nmp[:, st.par, :, 0], v))
                chain.link(nc.gpsimd.tensor_tensor(nmr[:, st.par], v, nmp[:, st.par, :, 0], ALU.subtract), apart=True)
                chain.link(nc.gpsimd.tensor_copy(nmp[:, st.par, :, 1], nmr[:, st.par]))
                nc.gpsimd.tensor_tensor(nmp[:, st.par, :, 2], nmr[:, st.par], nmp[:, st.par, :, 1],
                                        ALU.subtract).then_inc(nmp_ready, 1)

            def low(st):
                for b in range(2):
                    pool.wait_ge(res_ready, st.s * 2 + (b + 1))
                    if st.since(1) and b == 0:
                        pool.wait_ge(p_stored, st.s * 48)
                    alone(pool)
                    chain.link(nc.gpsimd.tensor_copy(planes[:, b, kept_at(b, 1)], res[:, b]))
                    nc.gpsimd.tensor_tensor(planes[:, b, kept_at(b, 2)], res[:, b], planes[:, b, kept_at(b, 1)],
                                            ALU.subtract
                                            ).then_inc(planes_ready, 1)

            def scatter(st):
                pool.wait_ge(slot_ready, st.s + 1)
                alone(pool)
                for t in range(TT):
                    for k in range(2):
                        pool.indirect_dma_start(
                            out=hbm["xs"], out_offset=bass.IndirectOffsetOnAxis(
                                ap=slot[:, st.par, 2 * t + k:2 * t + k + 1], axis=0),
                            in_=xn[:, st.par, t], in_offset=None).then_inc(scattered[st.par], 16)

            split_maxima(Step(0, 0, 0, 0, 0))

            def step(st):
                if st.before(B - 1):
                    split_maxima(Step(st.s + 1, 1 - st.par, st.half + st.par, st.low + 1, st.high + 1))
                tail(scatter if cross else low, st)

            steps(pool, step, chain=chain, per_pair=6 if cross else 10)
            last = Step(B - 1, 1, B // 2 - 1, B - 1, B - 1)
            if cross:
                scatter(last)
                for par in range(2):
                    pool.wait_ge(scattered[par], 64 * B // 2)
            else:
                low(last)


def experts(nc, hbm, kept):
    fp32, fp32r, i32 = mybir.dt.float32, mybir.dt.float32r, mybir.dt.int32
    ALU, ACT, AX = mybir.AluOpType, mybir.ActivationFunctionType, mybir.AxisListType
    ctx = ExitStack()
    with ctx:
        def sb(name, shape, dt=fp32):
            return ctx.enter_context(nc.sbuf_tensor("e_" + name, shape, dt))

        def sem(name):
            return ctx.enter_context(nc.semaphore("e_" + name))

        def bank(name):
            return ctx.enter_context(nc.psum_tensor("e_" + name, [P, 512], fp32))

        const = sb("const", [P, NCONST])
        zeros = sb("zeros", [P, TMT, C])
        gu_raw = sb("gu_raw", [P, 2, 2, KT, F])
        wd_raw = sb("wd_raw", [P, FM, C])
        gu_hi = sb("gu_hi", [P, 2, KT, F], fp32r)
        gu_lo = sb("gu_lo", [P, 2, KT, F], fp32r)
        wd = sb("wd", [P, 2, FM, 2, C], fp32r)
        xs = sb("xs", [P, 2, TMT, C])
        x_hi, x_lo = sb("x_hi", [P, KT, TM], fp32r), sb("x_lo", [P, KT, TM], fp32r)
        silu = sb("silu", [P, 2, TM])
        h = sb("h", [P, 2, TM])
        h_hi, h_lo = sb("h_hi", [P, FM, TM], fp32r), sb("h_lo", [P, FM, TM], fp32r)
        cross = sb("cross", [P, 2, C])
        y = sb("y", [P, 2, TMT, C])
        over = sb("over", [P, NE, LEVELS])
        tiles = sb("tiles", [P, NE])
        below = sb("below", [P, NE, NE])
        ends = sb("ends", [P, NE])
        skip = kept["skip"]
        past = sb("past", [1, NTILE, NE])
        past2 = sb("past2", [1, NTILE, NE])
        expf = sb("expf", [1, NTILE])
        rowf = sb("rowf", [1, NTILE])
        expert_of = sb("expert_of", [1, NTILE], i32)
        row_of = sb("row_of", [1, NTILE], i32)
        tail_of = sb("tail_of", [1, NE], i32)
        tailf = sb("tailf", [1, NE])
        g_bank = [bank(f"g{i}") for i in range(2)]
        u_bank = [bank(f"u{i}") for i in range(2)]
        y_bank = [bank(f"y{i}") for i in range(2)]
        t_bank = [bank(f"t{i}") for i in range(2)]
        const_loaded, map_ready, padded = sem("const_loaded"), sem("map_ready"), sem("padded")
        zeros_set = sem("zeros_set")
        gu_loaded = [sem(f"gu_loaded{i}") for i in range(2)]
        wd_loaded = sem("wd_loaded")
        xs_loaded = [sem(f"xs_loaded{i}") for i in range(2)]
        gu_high, gu_split = sem("gu_high"), sem("gu_split")
        wd_high, wd_split = sem("wd_high"), sem("wd_split")
        x_filled, x_high, x_split = sem("x_filled"), sem("x_high"), sem("x_split")
        gu_filled, silu_ready = sem("gu_filled"), sem("silu_ready")
        h_ready, h_high, h_split = sem("h_ready"), sem("h_high"), sem("h_split")
        y_filled, cross_ready, y_ready = sem("y_filled"), sem("cross_ready"), sem("y_ready")
        y_stored = [sem(f"y_stored{i}") for i in range(2)]
        dve_seq = sem("dve_seq")
        block = ctx.enter_context(nc.Block())
        DM = FM // WDQ

        def slots(name, row):
            return hbm[name][bass.ds(row, TM)].rearrange("(t p) n -> p t n", p=P)

        def following(st):
            return Step(st.s + 1, 1 - st.par, st.half + st.par, st.low + 1, st.high + 1)

        def y_place(st, t):
            return (t + st.par * TMT) % 2

        @block.sync
        def _(sp):
            sp.dma_start(const[:], hbm["const"]).then_inc(const_loaded, 16)
            sp.wait_ge(map_ready, 1)
            sp.wait_ge(zeros_set, 1)
            for e in range(NE):
                row = sp.value_load(tail_of[0:1, e:e + 1], min_val=0, max_val=SPARE - TM)
                sp.dma_start(slots("xs", row), zeros[:]).then_inc(padded, 16)
            for n in range(NSPARE):
                sp.dma_start(slots("xs", SPARE + n * TM), zeros[:]).then_inc(padded, 16)

            def store(st):
                sp.wait_ge(y_ready, st.s * TMT + TMT)
                alone(sp)
                sp.dma_start(slots("ys", st.s * TM), y[:, st.par]).then_inc(y_stored[st.par], 16)

            def load(st):
                e = sp.value_load(expert_of[0:1, bass.ds(st.s, 1)], min_val=0, max_val=NE - 1)
                if st.since(2):
                    sp.wait_ge(gu_split, st.s * FM - FM)
                for i, name in enumerate(("wg", "wu")):
                    sp.dma_start(gu_raw[:, st.par, i].rearrange("p k n -> p (k n)"), hbm[name][bass.ds(e, 1)].rearrange(
                        "a p n -> p (a n)")).then_inc(gu_loaded[st.par], 16)
                if st.high < 1:
                    sp.wait_ge(padded, (NE + NSPARE) * 16)
                if st.since(2):
                    sp.wait_ge(x_filled, st.s - 1)
                    alone(sp)
                row = sp.value_load(row_of[0:1, bass.ds(st.s, 1)], min_val=0, max_val=NSLOT - TM)
                sp.dma_start(xs[:, st.par], slots("xs", row)).then_inc(xs_loaded[st.par], 16)
                if st.since(1):
                    sp.wait_ge(wd_split, st.s * WDQ)
                sp.dma_start(wd_raw[:].rearrange("p k n -> p (k n)"), hbm["wd"][bass.ds(e, 1)].rearrange(
                    "a p n -> p (a n)")).then_inc(wd_loaded, 16)
                if st.since(2):
                    store(Step(st.s - 2, st.par, st.half - 1, st.low - 2, st.high - 2))

            steps(sp, load, total=NTILE, front=2, back=1)
            for s in range(NTILE - 2, NTILE):
                store(Step(s, s % 2, s // 2, s, s))
            for par in range(2):
                sp.wait_ge(y_stored[par], ((NTILE + 1 - par) // 2) * 16)

        @block.tensor
        def _(pe):
            pe.wait_ge(const_loaded, 16)

            def turn(st):
                pe.wait_ge(xs_loaded[st.par], st.half * 16 + 16)
                for k in range(KT):
                    for t in range(TMT):
                        last = nc.tensor.transpose(t_bank[k][:, t * P:(t + 1) * P],
                                                   xs[:, st.par, t, k * P:(k + 1) * P], const[:, IDENT:IDENT + P])
                last.then_inc(x_filled, 1)

            turn(Step(0, 0, 0, 0, 0))

            def tile(st):
                pe.wait_ge(x_split, st.s + 1)
                for m in range(FM):
                    if st.since(1) or m >= 2:
                        pe.wait_ge(h_ready, st.s * FM + (m - 1))
                    pe.wait_ge(gu_split, st.s * FM + (m + 1))
                    for i, out in enumerate((g_bank, u_bank)):
                        for k in range(KT):
                            hi, lo = (a[:, i, k, m * P:(m + 1) * P] for a in (gu_hi, gu_lo))
                            nc.tensor.matmul(out[m % 2][:, 0:TM], hi, x_hi[:, k], start=(k == 0), stop=False)
                            nc.tensor.matmul(out[m % 2][:, 0:TM], hi, x_lo[:, k], start=False, stop=False)
                            last = nc.tensor.matmul(out[m % 2][:, 0:TM], lo, x_hi[:, k], start=False,
                                                    stop=(k == KT - 1))
                    last.then_inc(gu_filled, 1)
                if st.before(NTILE - 1):
                    turn(following(st))
                pe.wait_ge(wd_split, st.s * WDQ + WDQ)
                for t in range(TMT):
                    if st.since(1) or t >= 2:
                        pe.wait_ge(y_ready, st.s * TMT + (t - 1))
                    out = y_bank[y_place(st, t)]
                    for m in range(FM):
                        if t == 0:
                            pe.wait_ge(h_split, st.s * FM + (m + 1))
                        hi, lo = (a[:, m, t * P:(t + 1) * P] for a in (h_hi, h_lo))
                        for high in (True, False) if m < FM - 1 else (False, True):
                            if high:
                                last = nc.tensor.matmul(out[:], hi, wd[:, st.par, m].rearrange("p a n -> p (a n)"),
                                                        start=(m == 0), stop=(m == FM - 1))
                            else:
                                nc.tensor.matmul(out[:, 0:C], lo, wd[:, st.par, m, 0], start=False, stop=False)
                    last.then_inc(y_filled, 1)

            steps(pe, tile, total=NTILE, front=2, back=1)

        @block.scalar
        def _(act):
            def gu_part(st, m):
                if m == 0:
                    act.wait_ge(gu_loaded[st.par], st.half * 32 + 32)
                for i in range(2):
                    last = nc.scalar.copy(gu_hi[:, i, :, m * P:(m + 1) * P], gu_raw[:, st.par, i, :, m * P:(m + 1) * P])
                last.then_inc(gu_high, 1)

            def wd_part(st, q):
                if q == 0:
                    act.wait_ge(wd_loaded, st.s * 16 + 16)
                nc.scalar.copy(wd[:, st.par, q * DM:(q + 1) * DM, 0], wd_raw[:, q * DM:(q + 1) * DM]
                               ).then_inc(wd_high, 1)

            def x_part(st):
                act.wait_ge(x_filled, st.s + 1)
                for k in range(KT):
                    last = nc.scalar.copy(x_hi[:, k], t_bank[k][:, 0:TM])
                last.then_inc(x_high, 1)

            first = Step(0, 0, 0, 0, 0)
            for m in range(FM):
                gu_part(first, m)
            x_part(first)
            for q in range(WDQ):
                wd_part(first, q)

            def tile(st):
                for m in range(FM):
                    act.wait_ge(gu_filled, st.s * FM + (m + 1))
                    if st.since(1) or m >= 2:
                        act.wait_ge(h_ready, st.s * FM + (m - 1))
                    nc.scalar.activation(silu[:, m % 2], g_bank[m % 2][:, 0:TM], ACT.Silu).then_inc(silu_ready, 1)
                    if st.before(NTILE - 1):
                        gu_part(following(st), m)
                    act.wait_ge(h_ready, st.s * FM + (m + 1))
                    nc.scalar.copy(h_hi[:, m], h[:, m % 2]).then_inc(h_high, 1)
                if st.before(NTILE - 1):
                    x_part(following(st))
                    for q in range(WDQ):
                        wd_part(following(st), q)
                for t in range(TMT):
                    act.wait_ge(y_filled, st.s * TMT + (t + 1))
                    nc.scalar.copy(cross[:, y_place(st, t)], y_bank[y_place(st, t)][:, C:]).then_inc(cross_ready, 1)

            steps(act, tile, total=NTILE, front=2, back=1)

        @block.vector
        def _(dve):
            chain = Chain(dve, dve_seq)
            count = kept["count"][:]
            nc.vector.memset(zeros[:], 0.0).then_inc(zeros_set, 1)
            dve.wait_ge(const_loaded, 16)

            def table(at, *shape):
                n = 1
                for x in shape:
                    n *= x
                v = const[:, at:at + n]
                return v.rearrange("p (a b) -> p a b", b=shape[-1]) if len(shape) == 2 else v

            chain.link(nc.vector.tensor_tensor(over[:], count.unsqueeze(2).to_broadcast([P, NE, LEVELS]),
                                               table(LEVEL, NE, LEVELS), ALU.is_gt))
            chain.link(nc.vector.reduce_sum(tiles[:], over[:], AX.X))
            chain.link(nc.vector.tensor_tensor(below[:], tiles[:].unsqueeze(1).to_broadcast([P, NE, NE]),
                                               table(LOWER, NE, NE), ALU.mult))
            chain.link(nc.vector.reduce_sum(ends[:], below[:], AX.X))
            chain.link(nc.vector.tensor_scalar(skip[:], tiles[:], -float(TM), float(CAP), ALU.mult, ALU.add))
            chain.link(nc.vector.tensor_tensor(past[:], table(TILE, NTILE, NE)[0:1],
                                               ends[0:1].unsqueeze(1).to_broadcast([1, NTILE, NE]), ALU.is_ge))
            chain.link(nc.vector.reduce_sum(expf[:], past[:], AX.X))
            chain.link(nc.vector.tensor_tensor(past2[:], past[:],
                                               skip[0:1].unsqueeze(1).to_broadcast([1, NTILE, NE]), ALU.mult))
            chain.link(nc.vector.reduce_sum(rowf[:], past2[:], AX.X))
            chain.link(nc.vector.tensor_scalar(expf[:], expf[:], float(NE - 1), None, ALU.min))
            chain.link(nc.vector.tensor_copy(expert_of[:], expf[:]))
            chain.link(nc.vector.scalar_tensor_tensor(rowf[:], table(TILE, NTILE, NE)[0:1, :, 0], float(TM), rowf[:],
                                                      ALU.mult, ALU.add))
            chain.link(nc.vector.tensor_copy(row_of[:], rowf[:]))
            chain.link(nc.vector.tensor_tensor(tailf[:], kept["count"][0:1], table(REGION, NE)[0:1], ALU.add))
            nc.vector.tensor_copy(tail_of[:], tailf[:]).then_inc(map_ready, 1)

            def gu_part(st, m):
                dve.wait_ge(gu_high, st.s * FM + (m + 1))
                for i in range(2):
                    cut = slice(m * P, (m + 1) * P)
                    last = nc.vector.tensor_tensor(gu_lo[:, i, :, cut], gu_raw[:, st.par, i, :, cut],
                                                   gu_hi[:, i, :, cut], ALU.subtract)
                last.then_inc(gu_split, 1)

            def wd_part(st, q):
                dve.wait_ge(wd_high, st.s * WDQ + (q + 1))
                cut = slice(q * DM, (q + 1) * DM)
                nc.vector.tensor_tensor(wd[:, st.par, cut, 1], wd_raw[:, cut], wd[:, st.par, cut, 0], ALU.subtract
                                        ).then_inc(wd_split, 1)

            def x_part(st):
                dve.wait_ge(x_high, st.s + 1)
                for k in range(KT):
                    last = nc.vector.tensor_tensor(x_lo[:, k], t_bank[k][:, 0:TM], x_hi[:, k], ALU.subtract)
                last.then_inc(x_split, 1)

            first = Step(0, 0, 0, 0, 0)
            for m in range(FM):
                gu_part(first, m)
            x_part(first)
            for q in range(WDQ):
                wd_part(first, q)

            def tile(st):
                for m in range(FM):
                    dve.wait_ge(silu_ready, st.s * FM + (m + 1))
                    if st.since(1) or m >= 2:
                        dve.wait_ge(h_split, st.s * FM + (m - 1))
                    nc.vector.tensor_tensor(h[:, m % 2], u_bank[m % 2][:, 0:TM], silu[:, m % 2], ALU.mult
                                            ).then_inc(h_ready, 1)
                    if st.before(NTILE - 1):
                        gu_part(following(st), m)
                    dve.wait_ge(h_high, st.s * FM + (m + 1))
                    nc.vector.tensor_tensor(h_lo[:, m], h[:, m % 2], h_hi[:, m], ALU.subtract).then_inc(h_split, 1)
                if st.before(NTILE - 1):
                    x_part(following(st))
                    for q in range(WDQ):
                        wd_part(following(st), q)
                if st.since(2):
                    dve.wait_ge(y_stored[st.par], st.half * 16)
                for t in range(TMT):
                    dve.wait_ge(cross_ready, st.s * TMT + (t + 1))
                    nc.vector.tensor_tensor(y[:, st.par, t], y_bank[y_place(st, t)][:, 0:C],
                                            cross[:, y_place(st, t)], ALU.add).then_inc(y_ready, 1)

            steps(dve, tile, total=NTILE, front=2, back=1)


def combine(nc, hbm, kept):
    fp32, u32 = mybir.dt.float32, mybir.dt.uint32
    ALU, ACT = mybir.AluOpType, mybir.ActivationFunctionType
    ctx = ExitStack()
    with ctx:
        def sb(name, shape, dt=fp32):
            return ctx.enter_context(nc.sbuf_tensor("o_" + name, shape, dt))

        def sem(name):
            return ctx.enter_context(nc.semaphore("o_" + name))

        x = sb("x", [P, 2, TT, C])
        picked = sb("picked", [P, 2, TT, 2, C])
        region = sb("region", [P, NE])
        behind = sb("behind", [P, B * TT * 2, NE - 1])
        gaps = sb("gaps", [P, B * TT * 2])
        yslot = sb("yslot", [P, B * TT * 2])
        slot = sb("slot", [P, 2, TT * 2], u32)
        gate = sb("gate", [P, 2, 2, TT])
        y = sb("y", [P, 2, TT, C])
        out = sb("out", [P, 2, TT, C])
        stats = sb("stats", [P, TT, 6])
        mv = sb("mv", [P, 2, TT, 2])
        lnv = sb("lnv", [P, 2, TT])
        rstd = sb("rstd", [P, 2, TT])
        newton = sb("newton", [P, 2, TT])
        eps = sb("eps", [P, 1])
        eps_set, region_loaded = sem("eps_set"), sem("region_loaded")
        x_loaded = [sem(f"x_loaded{i}") for i in range(2)]
        gathered = [sem(f"gathered{i}") for i in range(2)]
        slot_ready, sum_ready, stats_ready = sem("slot_ready"), sem("sum_ready"), sem("stats_ready")
        rstd_ready, out_ready = sem("rstd_ready"), sem("out_ready")
        stored = [sem(f"stored{i}") for i in range(2)]
        dve_seq, act_seq = sem("dve_seq"), sem("act_seq")
        block = ctx.enter_context(nc.Block())

        def rows(name, st):
            return hbm[name][bass.ds(st.s, 1)].rearrange("a (t p) n -> p (a t) n", p=P)

        @block.sync
        def _(sp):
            sp.dma_start(region[:], hbm["const"][:, REGION:REGION + NE]).then_inc(region_loaded, 16)

            def step(st):
                if st.since(2):
                    sp.wait_ge(sum_ready, st.s - 1)
                sp.dma_start(x[:, st.par], rows("x2", st)).then_inc(x_loaded[st.par], 16)
                if st.since(2):
                    before = Step(st.s - 2, st.par, st.half - 1, st.low - 2, st.high - 2)
                    sp.wait_ge(out_ready, st.s - 1)
                    sp.dma_start(rows("out", before), out[:, st.par]).then_inc(stored[st.par], 16)

            steps(sp, step)
            for s in range(B - 2, B):
                sp.wait_ge(out_ready, s + 1)
                sp.dma_start(rows("out", Step(s, s % 2, s // 2, s, s)), out[:, s % 2]).then_inc(stored[s % 2], 16)
            for par in range(2):
                sp.wait_ge(stored[par], 16 * B // 2)

        @block.gpsimd
        def _(pool):
            def gather(st):
                pool.wait_ge(slot_ready, st.s + 1)
                if st.since(2):
                    pool.wait_ge(sum_ready, st.s - 1)
                alone(pool)
                for t in range(TT):
                    for k in range(2):
                        pool.indirect_dma_start(
                            out=picked[:, st.par, t, k], out_offset=None, in_=hbm["ys"],
                            in_offset=bass.IndirectOffsetOnAxis(ap=slot[:, st.par, 2 * t + k:2 * t + k + 1], axis=0),
                        ).then_inc(gathered[st.par], 16)

            steps(pool, gather)

        @block.scalar
        def _(act):
            chain = Chain(act, act_seq)
            nc.scalar.preload_act_table_set("natural_log_exp_and_others")
            act.wait_ge(eps_set, 1)

            def spread(st):
                act.wait_ge(stats_ready, st.s + 1)
                chain.link(nc.scalar.activation(lnv[:, st.par], mv[:, st.par, :, 1], ACT.Ln, bias=eps[:]))
                nc.scalar.activation(rstd[:, st.par], lnv[:, st.par], ACT.Exp, scale=-0.5).then_inc(rstd_ready, 1)

            steps(act, spread, chain=chain, per_pair=2)

        @block.vector
        def _(dve):
            chain = Chain(dve, dve_seq)
            nc.vector.memset(eps[:], EPS).then_inc(eps_set, 1)
            n = B * TT * 2
            dve.wait_ge(region_loaded, 16)
            chain.link(nc.vector.tensor_tensor(
                behind[:], kept["slot"][:].unsqueeze(2).to_broadcast([P, n, NE - 1]),
                region[:, 1:].unsqueeze(1).to_broadcast([P, n, NE - 1]), ALU.is_ge))
            chain.link(nc.vector.tensor_tensor(
                behind[:], behind[:], kept["skip"][:, 0:NE - 1].unsqueeze(1).to_broadcast([P, n, NE - 1]), ALU.mult))
            chain.link(nc.vector.reduce_sum(gaps[:], behind[:], mybir.AxisListType.X))
            chain.link(nc.vector.tensor_tensor(yslot[:], kept["slot"][:], gaps[:], ALU.subtract))

            def address(st):
                nc.vector.tensor_copy(gate[:, st.par].rearrange("p k t -> p (k t)"),
                                      kept["gate"][:, bass.ds(st.s * 2 * TT, 2 * TT)])
                if st.since(2):
                    dve.wait_ge(gathered[st.par], st.half * 64)
                nc.vector.tensor_copy(slot[:, st.par], yslot[:, bass.ds(st.s * 2 * TT, 2 * TT)]
                                      ).then_inc(slot_ready, 1)

            def add(st):
                dve.wait_ge(x_loaded[st.par], st.half * 16 + 16)
                dve.wait_ge(gathered[st.par], st.half * 64 + 64)
                dve.wait_ge(slot_ready, st.s + 1)
                if st.since(2):
                    dve.wait_ge(out_ready, st.s - 1)
                for t in range(TT):
                    last = nc.vector.scalar_tensor_tensor(y[:, st.par, t], picked[:, st.par, t, 0],
                                                          gate[:, st.par, 0, t:t + 1], x[:, st.par, t],
                                                          ALU.mult, ALU.add)
                chain.link(last)
                for t in range(TT):
                    last = nc.vector.scalar_tensor_tensor(y[:, st.par, t], picked[:, st.par, t, 1],
                                                          gate[:, st.par, 1, t:t + 1], y[:, st.par, t],
                                                          ALU.mult, ALU.add)
                last.then_inc(sum_ready, 1)
                dve.wait_ge(sum_ready, st.s + 1)
                for t in range(TT):
                    last = nc.vector.bn_stats(stats[:, t], y[:, st.par, t])
                chain.link(last, apart=True)
                for t in range(TT):
                    last = nc.vector.bn_aggr(mv[:, st.par, t], stats[:, t])
                last.then_inc(stats_ready, 1)

            def norm(st):
                dve.wait_ge(rstd_ready, st.s + 1)
                r, t1, var = rstd[:, st.par], newton[:, st.par], mv[:, st.par, :, 1]
                chain.link(nc.vector.tensor_tensor(t1, r, r, ALU.mult))
                chain.link(nc.vector.scalar_tensor_tensor(t1, var, EPS, t1, ALU.add, ALU.mult))
                chain.link(nc.vector.tensor_scalar(t1, t1, -0.5, 1.5, ALU.mult, ALU.add))
                chain.link(nc.vector.tensor_tensor(t1, t1, r, ALU.mult))
                if st.since(2):
                    dve.wait_ge(stored[st.par], st.half * 16)
                for t in range(TT):
                    last = nc.vector.tensor_scalar(out[:, st.par, t], y[:, st.par, t], mv[:, st.par, t, 0:1],
                                                   newton[:, st.par, t:t + 1], ALU.subtract, ALU.mult)
                last.then_inc(out_ready, 1)

            address(Step(0, 0, 0, 0, 0))

            def step(st):
                if st.before(B - 1):
                    address(Step(st.s + 1, 1 - st.par, st.half + st.par, st.low + 1, st.high + 1))
                add(st)
                if st.since(1):
                    norm(Step(st.s - 1, 1 - st.par, st.half - (1 - st.par), st.low - 1, st.high - 1))

            steps(dve, step, chain=chain, per_pair=12)
            norm(Step(B - 1, 1, B // 2 - 1, B - 1, B - 1))


def program(nc, hbm):
    fp32, bf16 = mybir.dt.float32, mybir.dt.bfloat16

    def scratch(name, shape, dt=fp32):
        hbm[name] = nc.dram_tensor("scratch_" + name, shape, dt, kind="Internal").ap()

    scratch("q1", [B, 3, C, N], bf16)
    scratch("k1", [B, 3, C, N], bf16)
    scratch("v1", [B, N, H * 2 * D])
    scratch("q2", [B, 3, C, N], bf16)
    scratch("k2", [B, 3, C, NK], bf16)
    scratch("v2", [B, N, H * 2 * D])
    scratch("x1", [B, N, C])
    scratch("x2", [B, N, C])
    scratch("xs", [NSLOT, C])
    scratch("ys", [NTILE * TM, C])
    with ExitStack() as ctx:
        routed = {name: ctx.enter_context(nc.sbuf_tensor(name + "s", [P, n], fp32))
                  for name, n in (("slot", B * TT * 2), ("gate", B * TT * 2), ("skip", NE), ("count", NE))}
        first = ctx.enter_context(ExitStack())

        def keep(name, shape, dt=fp32):
            return first.enter_context(nc.sbuf_tensor(name, shape, dt))

        kept = {
            "qs": keep("qs", [ROWS + 3, 2, H, N], bf16),
            "ks": keep("ks", [ROWS + 3, 2, H, NK], bf16),
            "va": keep("va", [P, 2, TT + 1, H, 2 * D]),
            "wp1": keep("wp1", [P, UNITS, C]), "wp2": keep("wp2", [P, UNITS, C]),
            "wx": keep("wx", [P, KT, 3 * C]),
            "const": keep("const", [P, NCONST]), "identb": keep("identb", [P, P], bf16),
            "maskb": keep("maskb", [P, TT, WIN], bf16), "eps": keep("eps", [P, 1]),
            "rw": keep("rw", [P, KT, NE]), "rb": keep("rb", [P, TT, NE]),
            "trib": keep("trib", [P, P], bf16), "onesb": keep("onesb", [P, P], bf16),
            "iota4": keep("iota4", [P, 2 * TT, NE]), "loads": 2 * HU + 5 + TT,
        }
        kept.update(routed)
        project_first(nc, hbm, kept)
        attention(nc, hbm, kept, cross=False)
        attention(nc, hbm, kept, cross=True)
        first.close()
        experts(nc, hbm, kept)
        combine(nc, hbm, kept)


def constants():
    import numpy as np
    p = np.arange(P)[:, None]
    out = np.zeros((P, NCONST), np.float32)
    out[:, IDENT:IDENT + P] = p == np.arange(P)
    out[:, UPPER:UPPER + P] = p < np.arange(P)
    for t in range(TT):
        apart = np.abs(t * P + p - (W0[t] + np.arange(WIN)))
        out[:, MASK + t * WIN:MASK + (t + 1) * WIN] = np.where(apart <= BAND, 0.0, MASKED)
    out[:, EXPERT:EXPERT + NE] = np.arange(NE)
    out[:, LEVEL:LEVEL + NE * LEVELS] = np.tile(np.arange(LEVELS) * TM, NE)
    out[:, LOWER:LOWER + NE * NE] = (np.arange(NE)[:, None] >= np.arange(NE)).reshape(-1)
    out[:, TILE:TILE + NTILE * NE] = np.repeat(np.arange(NTILE), NE)
    out[:, REGION:REGION + NE] = np.arange(NE) * CAP
    return out


def kernel(x, ctx_2048, L0_attn_Wqkv, L0_attn_Wproj, L0_attn_bproj, L0_xattn_w_qkv, L0_xattn_w_proj,
           L0_xattn_b_proj, L0_ffn_router_w, L0_ffn_router_b, L0_ffn_gate_w, L0_ffn_up_w, L0_ffn_down_w):
    import numpy as np
    import concourse.bacc as bacc
    from concourse.bass_utils import run_bass_kernel_spmd

    def lay(a, *order):
        return np.ascontiguousarray(np.transpose(np.asarray(a), order))

    def heads_last(a, axis):
        shape = a.shape
        a = a.reshape(*shape[:axis], H, D, *shape[axis + 1:])
        return np.ascontiguousarray(np.swapaxes(a, axis, axis + 1)).reshape(shape)

    def qkv(a):
        return np.concatenate([heads_last(a[:, :C], 1), heads_last(a[:, C:2 * C], 1), a[:, 2 * C:]], axis=1)

    def up(a):
        a = np.asarray(a).reshape(NE, F, KT, P)
        return np.ascontiguousarray(a.transpose(0, 3, 2, 1).reshape(NE, P, KT * F))

    def down(a):
        a = np.asarray(a).reshape(NE, C, FM, P)
        return np.ascontiguousarray(a.transpose(0, 3, 2, 1).reshape(NE, P, FM * C))

    arrays = {
        "x": np.ascontiguousarray(x), "xT": lay(x, 0, 2, 1),
        "ctx": np.ascontiguousarray(ctx_2048), "ckT": heads_last(np.transpose(np.asarray(ctx_2048)[:, :, :C], (0, 2, 1)), 1),
        "wqkv": qkv(np.asarray(L0_attn_Wqkv)), "wp1": np.ascontiguousarray(L0_attn_Wproj),
        "bp1": np.asarray(L0_attn_bproj).reshape(1, C),
        "wx": qkv(np.transpose(np.asarray(L0_xattn_w_qkv), (1, 0))), "wp2": lay(L0_xattn_w_proj, 1, 0),
        "bp2": np.asarray(L0_xattn_b_proj).reshape(1, C),
        "rw": lay(L0_ffn_router_w, 1, 0), "rb": np.asarray(L0_ffn_router_b).reshape(1, NE),
        "wg": up(L0_ffn_gate_w), "wu": up(L0_ffn_up_w), "wd": down(L0_ffn_down_w),
        "const": constants(),
    }
    nc = bacc.Bacc("TRN2", target_bir_lowering=False, num_devices=1)
    hbm = {n: nc.dram_tensor("in_" + n, a.shape, mybir.dt.from_np(a.dtype), kind="ExternalInput").ap()
           for n, a in arrays.items()}
    hbm["out"] = nc.dram_tensor("out_x", [B, N, C], mybir.dt.float32, kind="ExternalOutput").ap()
    program(nc, hbm)
    r = run_bass_kernel_spmd(nc, [{"in_" + n: a for n, a in arrays.items()}], core_ids=[0])
    return r.results[0]["out_x"]
```

```python
import concourse.bass as bass
from concourse import mybir
from contextlib import ExitStack

B, N, C, H, D = 16, 256, 256, 16, 16
NCTX = 77
BAND = 8
P = 128
TT = N // P
KT = C // P
WIN = P + BAND
W0 = [0, N - WIN]
NK = N + NCTX
EPS = 1e-5
SCALE = float(D) ** -0.5
NE, F = 8, 1024
FM = F // P
TM = 384
TMT = TM // P
WDQ = 4
NTILE = (2 * B * N + NE * (TM - 1)) // TM
CAP = B * N + TM
SPARE = NE * CAP
NSLOT = SPARE + TM
LEVELS = (B * N + TM - 1) // TM
NTOK = B * N // P
UNITS, HU = 4, 4
PAIRS = UNITS // 2
MASKED = -1e30
PLANES = {"q": [(0, 3), (0, 2), (0, 1)], "k": [(0, 3), (1, 3), (2, 3)]}
ROWS = 6 * D
AHEAD = 8
LANES = 4
HALVES = 2
SIZES = [P, P, TT * WIN, NE, NE * LEVELS, NE * NE, NTILE * NE, NE]
IDENT, UPPER, MASK, EXPERT, LEVEL, LOWER, TILE, REGION, NCONST = [sum(SIZES[:i]) for i in range(9)]


class Step:

    def __init__(self, s, par, half, low, high):
        self.s, self.par, self.half, self.low, self.high = s, par, half, low, high

    def since(self, n):
        return self.low >= n

    def before(self, n):
        return self.high < n


def steps(eng, body, total=B, front=4, back=2, chain=None, per_pair=0, lanes=2):
    for s in range(front):
        body(Step(s, s % lanes, s // lanes, s, s))
    turns = (total - front - back) // lanes
    start = chain.at if chain else 0
    with eng.Fori(0, turns) as i:
        if chain:
            chain.at, chain.inside = i * per_pair + start, 0
        for par in range(lanes):
            body(Step(i * lanes + (front + par), par, i + front // lanes, front + par, total - back - lanes + par))
        if chain:
            assert chain.inside == per_pair, chain.inside
    if chain:
        chain.at, chain.inside = start + turns * per_pair, None
    for s in range(total - back, total):
        body(Step(s, s % lanes, s // lanes, s, s))


def alone(eng):
    eng.nop(nofuse=True)


class Chain:

    def __init__(self, eng, sem):
        self.eng, self.sem, self.at, self.inside = eng, sem, 0, None

    def mark(self, ins):
        self.at = self.at + 1
        if self.inside is not None:
            self.inside += 1
        ins.then_inc(self.sem, 1)

    def wait(self, apart=False):
        self.eng.wait_ge(self.sem, self.at)
        if apart:
            alone(self.eng)

    def link(self, ins, apart=False):
        self.mark(ins)
        self.wait(apart)


def kept_at(b, plane):
    return 2 - plane if b else plane


def project_first(nc, hbm, kept):
    fp32, bf16 = mybir.dt.float32, mybir.dt.bfloat16
    ALU = mybir.AluOpType
    ctx = ExitStack()
    with ctx:
        def sb(name, shape, dt=fp32):
            return ctx.enter_context(nc.sbuf_tensor(name, shape, dt))

        def sem(name):
            return ctx.enter_context(nc.semaphore(name))

        w = sb("a_w", [P, KT, 3 * C])
        xT = sb("a_xT", [P, 2, KT, N])
        cT = sb("a_cT", [P, 2, KT * NCTX])
        res = sb("a_res", [P, 2, 2, KT * N])
        planes = sb("a_planes", [P, 2, 2, 3, KT * N], bf16)
        cres = sb("a_cres", [P, 2, KT * NCTX])
        cplanes = sb("a_cplanes", [P, 2, 3, KT * NCTX], bf16)
        vo = sb("a_vo", [P, 2, TT, H, 2 * D])
        ps = [[ctx.enter_context(nc.psum_tensor(f"a_ps{a}{b}", [P, 512], fp32)) for b in range(3)]
              for a in range(2)]
        weights_loaded, kept_loaded = sem("a_weights_loaded"), sem("a_kept_loaded")
        x_loaded = [sem(f"a_x_loaded{i}") for i in range(2)]
        ones_set = sem("a_ones_set")
        q_filled, k_filled, v_filled = sem("a_q_filled"), sem("a_k_filled"), sem("a_v_filled")
        high_ready, res_ready, mid_ready = sem("a_high_ready"), sem("a_res_ready"), sem("a_mid_ready")
        v_ready, low_ready = sem("a_v_ready"), sem("a_low_ready")
        stored = [sem(f"a_stored{i}") for i in range(2)]
        pool_seq = sem("a_pool_seq")
        block = ctx.enter_context(nc.Block())

        @block.sync
        def _(sp):
            sp.dma_start(w[:], hbm["wqkv"].rearrange("(k p) n -> p k n", p=P)).then_inc(weights_loaded, 16)

            def load(st):
                if st.since(2):
                    sp.wait_ge(v_filled, st.s - 1)
                    sp.wait_ge(low_ready, st.s * 3 - 3)
                    alone(sp)
                sp.dma_start(xT[:, st.par], hbm["xT"][bass.ds(st.s, 1)].rearrange("a (k p) t -> p (a k) t", p=P)
                             ).then_inc(x_loaded[st.par], 16)
                sp.dma_start(cT[:, st.par].rearrange("p (k t) -> p k t", k=KT),
                             hbm["ckT"][bass.ds(st.s, 1)].rearrange("a (k p) t -> p (a k) t", p=P)
                             ).then_inc(x_loaded[st.par], 16)
                if st.since(2):
                    store(Step(st.s - 2, st.par, st.half - 1, st.low - 2, st.high - 2))
                if st.low == st.high == 3:
                    sp.wait_ge(stored[0], 64)
                    load_qk(sp, hbm, kept, False, 0, 0, 0)
                if st.low == st.high == B - 2:
                    load_qk(sp, hbm, kept, False, 0, 0, 1)

            def store(st):
                for b, name in ((0, "q1"), (1, "k1")):
                    sp.wait_ge(low_ready, st.s * 3 + (b + 2))
                    alone(sp)
                    sp.dma_start(hbm[name][bass.ds(st.s, 1)].rearrange("a l (m p) t -> p (a l) m t", p=P),
                                 planes[:, st.par, b].rearrange("p l (m t) -> p l m t", m=KT)
                                 ).then_inc(stored[st.par], 16)
                sp.dma_start(hbm["k2"][bass.ds(st.s, 1), :, :, N:].rearrange("a l (m p) t -> p (a l) m t", p=P),
                             cplanes[:, st.par].rearrange("p l (m t) -> p l m t", m=KT)
                             ).then_inc(stored[st.par], 16)
                sp.wait_ge(v_ready, st.s + 1)
                alone(sp)
                sp.dma_start(hbm["v1"][bass.ds(st.s, 1)].rearrange("a (t p) n -> p (a t) n", p=P),
                             vo[:, st.par].rearrange("p t h d -> p t (h d)")).then_inc(stored[st.par], 16)

            steps(sp, load)
            for s in range(B - 2, B):
                store(Step(s, s % 2, s // 2, s, s))
            for par in range(2):
                sp.wait_ge(stored[par], 64 * B // 2)
            sp.wait_ge(kept_loaded, 16 * kept["loads"])

        @block.tensor
        def _(pe):
            pe.wait_ge(weights_loaded, 16)

            def project(st):
                pe.wait_ge(x_loaded[st.par], st.half * 32 + 32)
                if st.since(2):
                    pe.wait_ge(res_ready, st.s * 3 - 3)
                    pe.wait_ge(v_ready, st.s - 1)
                for b, filled in ((0, q_filled), (1, k_filled)):
                    for m in range(KT):
                        for k in range(KT):
                            last = nc.tensor.matmul(ps[st.par][b][:, m * N:(m + 1) * N],
                                                    w[:, k, b * C + m * P:b * C + (m + 1) * P],
                                                    xT[:, st.par, k], start=(k == 0), stop=(k == KT - 1))
                    last.then_inc(filled, 1)
                for t in range(TT):
                    for k in range(KT):
                        last = nc.tensor.matmul(ps[st.par][2][:, t * C:(t + 1) * C],
                                                xT[:, st.par, k, t * P:(t + 1) * P], w[:, k, 2 * C:],
                                                start=(k == 0), stop=(k == KT - 1))
                last.then_inc(v_filled, 1)

            steps(pe, project)

        @block.scalar
        def _(act):
            for name in ("wp1", "wp2"):
                act.dma_start(kept[name][:], hbm[name]).then_inc(kept_loaded, 16)
            for name in ("bp1", "bp2"):
                for t in range(TT):
                    act.dma_start(kept[name][:, t], hbm[name].to_broadcast([P, C])).then_inc(kept_loaded, 16)
            act.dma_start(kept["wx"][:], hbm["wx"].rearrange("(k p) n -> p k n", p=P)).then_inc(kept_loaded, 16)
            act.dma_start(kept["const"][:], hbm["const"]).then_inc(kept_loaded, 16)
            act.dma_start(kept["rw"][:], hbm["rw"].rearrange("(k p) e -> p k e", p=P)).then_inc(kept_loaded, 16)
            for t in range(TT):
                act.dma_start(kept["rb"][:, t], hbm["rb"].to_broadcast([P, NE])).then_inc(kept_loaded, 16)
            act.wait_ge(ones_set, 1)

            def split(st):
                if st.since(2):
                    act.wait_ge(stored[st.par], st.half * 64)
                act.wait_ge(x_loaded[st.par], st.half * 32 + 32)
                nc.scalar.copy(cplanes[:, st.par, kept_at(1, 0)], cT[:, st.par]).then_inc(high_ready, 1)
                for b, filled in ((0, q_filled), (1, k_filled)):
                    act.wait_ge(filled, st.s + 1)
                    nc.scalar.copy(planes[:, st.par, b, kept_at(b, 0)], ps[st.par][b][:]).then_inc(high_ready, 1)
                act.wait_ge(res_ready, st.s * 3 + 1)
                nc.scalar.copy(cplanes[:, st.par, kept_at(1, 1)], cres[:, st.par]).then_inc(mid_ready, 1)
                for b in range(2):
                    act.wait_ge(res_ready, st.s * 3 + (b + 2))
                    nc.scalar.copy(planes[:, st.par, b, kept_at(b, 1)], res[:, st.par, b]).then_inc(mid_ready, 1)
                act.wait_ge(v_filled, st.s + 1)
                nc.scalar.copy(vo[:, st.par, :, :, 0:D],
                               ps[st.par][2][:].rearrange("p (t h d) -> p t h d", t=TT, h=H)).then_inc(v_ready, 1)

            steps(act, split)

        @block.vector
        def _(dve):
            nc.vector.memset(vo[:, :, :, :, D:], 1.0).then_inc(ones_set, 1)

            def split(st):
                dve.wait_ge(high_ready, st.s * 3 + 1)
                nc.vector.tensor_tensor(cres[:, st.par], cT[:, st.par], cplanes[:, st.par, kept_at(1, 0)],
                                        ALU.subtract).then_inc(res_ready, 1)
                for b in range(2):
                    dve.wait_ge(high_ready, st.s * 3 + (b + 2))
                    nc.vector.tensor_tensor(res[:, st.par, b], ps[st.par][b][:],
                                            planes[:, st.par, b, kept_at(b, 0)], ALU.subtract).then_inc(res_ready, 1)
                dve.wait_ge(mid_ready, st.s * 3 + 1)
                nc.vector.tensor_tensor(cplanes[:, st.par, kept_at(1, 2)], cres[:, st.par],
                                        cplanes[:, st.par, kept_at(1, 1)], ALU.subtract).then_inc(low_ready, 1)
                for b in range(2):
                    dve.wait_ge(mid_ready, st.s * 3 + (b + 2))
                    nc.vector.tensor_tensor(planes[:, st.par, b, kept_at(b, 2)], res[:, st.par, b],
                                            planes[:, st.par, b, kept_at(b, 1)], ALU.subtract).then_inc(low_ready, 1)

            steps(dve, split)
            dve.wait_ge(kept_loaded, 16 * kept["loads"])
            const = kept["const"]
            nc.vector.tensor_copy(kept["identb"][:], const[:, IDENT:IDENT + P])
            nc.vector.tensor_copy(kept["trib"][:], const[:, UPPER:UPPER + P])
            nc.vector.tensor_copy(kept["maskb"][:].rearrange("p t n -> p (t n)"), const[:, MASK:MASK + TT * WIN])
            for i in range(2 * TT):
                nc.vector.tensor_copy(kept["iota4"][:, i], const[:, EXPERT:EXPERT + NE])

        @block.gpsimd
        def _(pool):
            chain = Chain(pool, pool_seq)
            chain.link(nc.gpsimd.memset(kept["ks"][ROWS:ROWS + 3], 1.0))
            chain.link(nc.gpsimd.memset(kept["va"][:, :, :, :, D:], 1.0))
            chain.link(nc.gpsimd.memset(kept["onesb"][:], 1.0))
            chain.link(nc.gpsimd.memset(kept["eps"][:], EPS))
            chain.link(nc.gpsimd.memset(kept["count"][:], 0.0))


def load_qk(sp, hbm, kept, cross, s, par, half):
    hs = slice(half * H // HALVES, (half + 1) * H // HALVES)
    which, keys = ("2", NK) if cross else ("1", N)
    for name, dst, n in (("q", kept["qs"], N), ("k", kept["ks"], keys)):
        view, row = hbm[name + which].rearrange("s l (d h) t -> s (l d) h t", h=H), 0
        for lo, hi in PLANES[name]:
            sp.dma_start(dst[row:row + (hi - lo) * D, par, hs, 0:n],
                         view[bass.ds(s, 1), lo * D:hi * D, hs].rearrange("a p h t -> p (a h) t")
                         ).then_inc(kept["qk_loaded" + which][par][half], 16)
            row += (hi - lo) * D


def load_rest(sp, hbm, kept, cross, s, par):
    which = "2" if cross else "1"
    loaded, va = kept["rest_loaded" + which][par], kept["va"]
    sp.dma_start(va[:, par, 0:TT].rearrange("p t h d -> p t (h d)"),
                 hbm["v" + which][bass.ds(s, 1)].rearrange("a (t p) n -> p (a t) n", p=P)).then_inc(loaded, 16)
    sp.dma_start(kept["resid"][:, par], hbm["x1" if cross else "x"][bass.ds(s, 1)].rearrange(
        "a (t p) n -> p (a t) n", p=P)).then_inc(loaded, 16)
    if cross:
        sp.dma_start(va[0:NCTX, par, TT, :, 0:D], hbm["ctx"][bass.ds(s, 1), :, C:].rearrange(
            "a p (h d) -> p (a h) d", h=H)).then_inc(loaded, 16)


def attention(nc, hbm, kept, cross):
    fp32, bf16, i32, u32 = mybir.dt.float32, mybir.dt.bfloat16, mybir.dt.int32, mybir.dt.uint32
    ALU, ACT, AX = mybir.AluOpType, mybir.ActivationFunctionType, mybir.AxisListType
    u = "c_" if cross else "b_"
    keys = NK if cross else N
    x_out = hbm["x2" if cross else "x1"]
    wide = TT * N if cross else TT * WIN
    tiles = H * TT if cross else H
    chunks = 3 if cross else 2
    ahead = AHEAD if cross else 0
    ctx = ExitStack()
    with ctx:
        def sb(name, shape, dt=fp32):
            return ctx.enter_context(nc.sbuf_tensor(u + name, shape, dt))

        def sem(name):
            return ctx.enter_context(nc.semaphore(u + name))

        def bank(name):
            return ctx.enter_context(nc.psum_tensor(u + name, [P, 512], fp32))

        qs, ks, va = kept["qs"], kept["ks"], kept["va"]
        resid = kept["resid"]
        pm = sb("pm", [P, 2, HU, wide])
        pt = sb("pt", [NCTX, 2, HU, N]) if cross else None
        nm = sb("nm", [P, 2, H, TT])
        nmr = sb("nmr", [P, 2, TT, H])
        nmp = sb("nmp", [P, 2, TT, 3, H], bf16)
        nmT = sb("nmT", [3 * H, 2, N], bf16)
        turned = sb("turned", [P, 2, N])
        rden = sb("rden", [P, 2, N // 32, 1])
        joined = sb("joined", [P, N])
        on = sb("on", [P, PAIRS, N])
        wp = kept["wp2" if cross else "wp1"]
        bias = kept["bp2" if cross else "bp1"]
        stats = sb("stats", [P, TT, 6])
        mv = sb("mv", [P, 2, TT, 2])
        lnv = sb("lnv", [P, 2, TT])
        rstd = sb("rstd", [P, 2, TT])
        newton = sb("newton", [P, 2, TT])
        shift = sb("shift", [P, 2, TT])
        xn = sb("xn", [P, 2, TT, C])
        xnT = sb("xnT", [P, KT, N])
        const, identb, maskb, eps = kept["const"], kept["identb"], kept["maskb"], kept["eps"]
        ident = const[:, IDENT:IDENT + P]
        if cross:
            rw, rb, trib, onesb, iota4 = (kept[n] for n in ("rw", "rb", "trib", "onesb", "iota4"))
            logit = sb("logit", [P, TT, NE])
            top = sb("top", [P, TT, 8])
            topi = sb("topi", [P, TT, 8], u32)
            idxf = sb("idxf", [P, TT, 2])
            hot = sb("hot", [P, TT * 2, NE])
            hotb = sb("hotb", [P, TT, NE], bf16)
            gap = sb("gap", [P, TT])
            egap = sb("egap", [P, TT])
            oneg = sb("oneg", [P, TT])
            gate = sb("gate", [P, 2, TT])
            place = sb("place", [P, TT, NE])
            pick = sb("pick", [P, TT * 2, NE])
            slotf = sb("slotf", [P, TT * 2])
            slot = sb("slot", [P, 2, TT * 2], u32)
            base = kept["count"]
        else:
            w = kept["wx"]
            res = sb("res", [P, 2, KT * N])
            planes = sb("planes", [P, 2, 3, KT * N], bf16)
            vo = sb("vo", [P, TT, H, 2 * D])
        st_bank = [bank(f"st{i}") for i in range(2)]
        tl_bank = bank("tl")
        sm_bank = [bank(f"sm{i}") for i in range(2)]
        pv_bank = bank("pv")
        m0, m1 = bank("m0"), bank("m1")
        mx_bank = m0 if cross else tl_bank

        ones_set = sem("ones_set")
        which = "2" if cross else "1"
        qk_loaded, rest_loaded = kept["qk_loaded" + which], kept["rest_loaded" + which]
        nm_loaded = [sem(f"nm_loaded{i}") for i in range(2)]
        sm_filled, sm_drained = sem("sm_filled"), sem("sm_drained")
        st_filled, st_drained = sem("st_filled"), sem("st_drained")
        tl_filled, tl_drained = sem("tl_filled"), sem("tl_drained")
        pv_filled, pv_drained, on_ready = sem("pv_filled"), sem("pv_drained"), sem("on_ready")
        nmp_ready, nm_filled, nm_drained = sem("nmp_ready"), sem("nm_filled"), sem("nm_drained")
        op_filled, resid_ready = sem("op_filled"), sem("resid_ready")
        stats_ready, rstd_ready, xn_ready = sem("stats_ready"), sem("rstd_ready"), sem("xn_ready")
        shift_ready = sem("shift_ready")
        tr_filled, tr_drained = sem("tr_filled"), sem("tr_drained")
        dve_seq, act_seq, pool_seq = sem("dve_seq"), sem("act_seq"), sem("pool_seq")
        x_stored = [sem(f"x_stored{i}") for i in range(2)]
        if cross:
            lg_filled, lg_drained = sem("lg_filled"), sem("lg_drained")
            hot_ready, rk_filled, rk_drained = sem("hot_ready"), sem("rk_filled"), sem("rk_drained")
            gap_ready, egap_ready = sem("gap_ready"), sem("egap_ready")
            slot_ready = sem("slot_ready")
            scattered = [sem(f"scattered{i}") for i in range(2)]
        else:
            q_filled, k_filled, v_filled = sem("q_filled"), sem("k_filled"), sem("v_filled")
            high_ready, res_ready = sem("high_ready"), sem("res_ready")
            v_drained, planes_ready = sem("v_drained"), sem("planes_ready")
            p_stored = sem("p_stored")
        block = ctx.enter_context(nc.Block())

        def tail(body, st, *args):
            if st.since(1):
                body(Step(st.s - 1, 1 - st.par, st.half - (1 - st.par), st.low - 1, st.high - 1), *args)

        def following_maximum(body, st, n):
            if n < tiles - ahead and st.before(B - 1):
                body(Step(st.s + 1, 1 - st.par, st.half + st.par, st.low + 1, st.high + 1), ahead + n)
            if tiles - ahead <= n < tiles and st.before(B - 2):
                body(Step(st.s + 2, st.par, st.half + 1, st.low + 2, st.high + 2), n - (tiles - ahead))

        @block.sync
        def _(sp):
            def load_maxima(st):
                sp.wait_ge(nm_drained, st.s + 1)
                for pl in range(3):
                    sp.dma_start(qs[ROWS + pl:ROWS + pl + 1, st.par], nmT[pl * H:pl * H + H, st.par]
                                 ).then_inc(nm_loaded[st.par], 16)

            if not cross:
                load_rest(sp, hbm, kept, cross, 0, 0)
                for half in range(HALVES):
                    load_qk(sp, hbm, kept, cross, 1, 1, half)
                load_rest(sp, hbm, kept, cross, 1, 1)
            load_maxima(Step(0, 0, 0, 0, 0))

            def store_x(st):
                sp.wait_ge(xn_ready, st.s + 1)
                sp.dma_start(x_out[bass.ds(st.s, 1)].rearrange("a (t p) n -> p (a t) n", p=P), xn[:, st.par]
                             ).then_inc(x_stored[st.par], 16)

            def store_projected(st):
                sp.wait_ge(planes_ready, st.s * 2 + 2)
                for b, name in ((0, "q2"), (1, "k2")):
                    sp.dma_start(hbm[name][bass.ds(st.s, 1), :, :, 0:N].rearrange(
                        "a l (m p) t -> p (a l) m t", p=P), planes[:, b].rearrange(
                        "p l (m t) -> p l m t", m=KT)).then_inc(p_stored, 16)
                sp.wait_ge(v_drained, st.s + 1)
                alone(sp)
                sp.dma_start(hbm["v2"][bass.ds(st.s, 1)].rearrange("a (t p) n -> p (a t) n", p=P),
                             vo[:].rearrange("p t h d -> p t (h d)")).then_inc(p_stored, 16)

            def step(st):
                more, behind = st.before(B - 2), not st.before(B - 2) and not cross
                for half in range(HALVES):
                    if more or behind:
                        if cross:
                            sp.wait_ge(tl_filled, st.s * (H // 2) + (half + 1) * (H // 2 // HALVES))
                        else:
                            sp.wait_ge(st_filled, st.s * H + (half + 1) * (H // HALVES))
                    if more:
                        load_qk(sp, hbm, kept, cross, st.s + 2, st.par, half)
                    elif behind:
                        load_qk(sp, hbm, kept, True, st.s + 2 - B, st.par, half)
                    if half == 0:
                        tail(store_x, st)
                        if st.before(B - 1):
                            load_maxima(Step(st.s + 1, 1 - st.par, st.half + st.par, st.low + 1, st.high + 1))
                if cross and st.high == 1:
                    for i, name in enumerate(("wg", "wu")):
                        sp.dma_start(kept["gu_raw"][:, 0, i].rearrange("p k n -> p (k n)"), hbm[name][0]
                                     ).then_inc(kept["gu_loaded"][0], 16)
                    sp.dma_start(kept["wd_raw"][:].rearrange("p k n -> p (k n)"), hbm["wd"][0]
                                 ).then_inc(kept["wd_loaded"], 16)
                if not cross:
                    tail(store_projected, st)
                if more or behind:
                    sp.wait_ge(pv_filled, st.s * UNITS + UNITS)
                    alone(sp)
                    sp.wait_ge(op_filled, st.s + 1)
                    alone(sp)
                if more:
                    load_rest(sp, hbm, kept, cross, st.s + 2, st.par)
                elif behind:
                    load_rest(sp, hbm, kept, True, st.s + 2 - B, st.par)

            steps(sp, step)
            last = Step(B - 1, 1, B // 2 - 1, B - 1, B - 1)
            store_x(last)
            if not cross:
                store_projected(last)
                sp.wait_ge(p_stored, 48 * B)
            for par in range(2):
                sp.wait_ge(x_stored[par], 16 * B // 2)

        @block.tensor
        def _(pe):
            def maximum(st, n):
                h, t = (n // TT, n % TT) if cross else (n, 0)
                if h % (H // HALVES) == 0 and t == 0:
                    pe.wait_ge(qk_loaded[st.par][h // (H // HALVES)], (st.half + 1) * 6 * 16)
                if st.since(1) or n >= 2:
                    pe.wait_ge(sm_drained, st.s * tiles + (n - 1))
                out = sm_bank[n % 2]
                if cross:
                    last = nc.tensor.matmul(out[:, 0:NK], qs[0:ROWS, st.par, h, t * P:(t + 1) * P],
                                            ks[0:ROWS, st.par, h, 0:NK], start=True, stop=True)
                else:
                    nc.tensor.matmul(out[:, 0:TT * WIN], identb[:], maskb[:], start=True, stop=False,
                                     skip_group_check=True)
                    for t in range(TT):
                        last = nc.tensor.matmul(
                            out[:, t * WIN:(t + 1) * WIN], qs[0:ROWS, st.par, h, t * P:(t + 1) * P],
                            ks[0:ROWS, st.par, h, W0[t]:W0[t] + WIN], start=False, stop=(t == TT - 1),
                            skip_group_check=True)
                last.then_inc(sm_filled, 1)

            def scores(st, h):
                if h == 0:
                    pe.wait_ge(nm_loaded[st.par], st.half * 48 + 48)
                if st.since(1) or h >= 2:
                    pe.wait_ge(st_drained, st.s * H + (h - 1))
                out = st_bank[h % 2]
                if cross:
                    for c in range(TT):
                        last = nc.tensor.matmul(out[:, c * N:(c + 1) * N], ks[:, st.par, h, c * P:(c + 1) * P],
                                                qs[:, st.par, h], start=True, stop=True)
                else:
                    nc.tensor.matmul(out[:, 0:TT * WIN], identb[:], maskb[:], start=True, stop=False,
                                     skip_group_check=True)
                    for c in range(TT):
                        last = nc.tensor.matmul(
                            out[:, c * WIN:(c + 1) * WIN], ks[:, st.par, h, c * P:(c + 1) * P],
                            qs[:, st.par, h, W0[c]:W0[c] + WIN], start=False, stop=(c == TT - 1),
                            skip_group_check=True)
                last.then_inc(st_filled, 1)

            def scores_context(st, pair):
                if st.since(1) or pair >= 1:
                    pe.wait_ge(tl_drained, st.s * (H // 2) + pair)
                for e in range(2):
                    last = nc.tensor.matmul(tl_bank[0:NCTX, e * N:(e + 1) * N],
                                            ks[:, st.par, pair * 2 + e, N:], qs[:, st.par, pair * 2 + e],
                                            start=True, stop=True)
                last.then_inc(tl_filled, 1)

            def weigh(st, g, c):
                if c == 0:
                    if g == 0:
                        pe.wait_ge(rest_loaded[st.par], (st.half + 1) * (3 if cross else 2) * 16)
                    pe.wait_ge(st_drained, st.s * H + (g + 1) * HU)
                    if cross:
                        pe.wait_ge(tl_drained, st.s * (H // 2) + (g + 1) * (HU // 2))
                    if st.since(1) or g >= 1:
                        pe.wait_ge(pv_drained, st.s * UNITS + g)
                for j in range(HU):
                    kc = NCTX if c == TT else P
                    lhsT = va[0:kc, st.par, c, g * HU + j]
                    if c == TT:
                        cols, rhs = slice(0, N), pt[:, g % 2, j]
                    elif cross:
                        cols, rhs = slice(0, N), pm[:, g % 2, j, c * N:(c + 1) * N]
                    else:
                        cols, rhs = slice(W0[c], W0[c] + WIN), pm[:, g % 2, j, c * WIN:(c + 1) * WIN]
                    last = nc.tensor.matmul(pv_bank[32 * j:32 * j + 32, cols], lhsT, rhs, start=(c == 0),
                                            stop=(c == chunks - 1), skip_group_check=True)
                if c == chunks - 1:
                    last.then_inc(pv_filled, 1)

            def turn_maxima(st):
                pe.wait_ge(nmp_ready, st.s + 1)
                if cross and st.since(2):
                    pe.wait_ge(lg_drained, st.s - 1)
                if not cross and st.since(1):
                    pe.wait_ge(nm_drained, st.s)
                alone(pe)
                out = mx_bank[0:3 * H, 0:N // 2].bitcast(bf16)
                for t in range(TT):
                    last = nc.tensor.transpose(out[:, t * P:(t + 1) * P],
                                               nmp[:, st.par, t].rearrange("p l h -> p (l h)"), identb[:])
                last.then_inc(nm_filled, 1)

            def project(st, t, a):
                if a == 0:
                    if t == 0:
                        pe.wait_ge(resid_ready, st.s + 1)
                        if cross:
                            pe.wait_ge(nm_drained, st.s + 2 if st.before(B - 1) else B)
                        elif st.since(1):
                            pe.wait_ge(v_drained, st.s)
                    nc.tensor.matmul(m0[:, t * C:(t + 1) * C], ident, resid[:, st.par, t], start=True, stop=False)
                if t == 0:
                    pe.wait_ge(on_ready, st.s * PAIRS + (a + 1))
                last = nc.tensor.matmul(m0[:, t * C:(t + 1) * C], on[:, a, t * P:(t + 1) * P], wp[:, a],
                                        start=False, stop=(a == PAIRS - 1))
                if t == TT - 1 and a == PAIRS - 1:
                    last.then_inc(op_filled, 1)

            def turn_x(st):
                pe.wait_ge(xn_ready, st.s + 1)
                if st.since(1):
                    pe.wait_ge(rk_drained if cross else res_ready, st.s if cross else st.s * 2)
                for k in range(KT):
                    for t in range(TT):
                        last = nc.tensor.transpose(m1[:, k * N + t * P:k * N + (t + 1) * P],
                                                   xn[:, st.par, t, k * P:(k + 1) * P], ident)
                last.then_inc(tr_filled, 1)

            def project_part(b, out):
                for m in range(KT):
                    for k in range(KT):
                        last = nc.tensor.matmul(out[:, m * N:(m + 1) * N], w[:, k, b * C + m * P:b * C + (m + 1) * P],
                                                xnT[:, k], start=(k == 0), stop=(k == KT - 1))
                return last

            def project_q(st):
                pe.wait_ge(tr_drained, st.s + 1)
                project_part(0, m0).then_inc(q_filled, 1)

            def project_k(st):
                project_part(1, m1).then_inc(k_filled, 1)

            def project_v(st):
                pe.wait_ge(res_ready, st.s * 2 + 1)
                for t in range(TT):
                    for k in range(KT):
                        last = nc.tensor.matmul(m0[:, t * C:(t + 1) * C], xnT[:, k, t * P:(t + 1) * P],
                                                w[:, k, 2 * C:], start=(k == 0), stop=(k == KT - 1))
                last.then_inc(v_filled, 1)

            def logits(st):
                pe.wait_ge(tr_drained, st.s + 1)
                for t in range(TT):
                    for k in range(KT):
                        last = nc.tensor.matmul(m0[:, t * NE:(t + 1) * NE], xnT[:, k, t * P:(t + 1) * P], rw[:, k],
                                                start=(k == 0), stop=(k == KT - 1))
                last.then_inc(lg_filled, 1)

            def ranks(st):
                pe.wait_ge(hot_ready, st.s + 1)
                nc.tensor.matmul(m1[:, 0:NE], trib[:], hotb[:, 0], start=True, stop=True)
                nc.tensor.matmul(m1[:, NE:2 * NE], onesb[:], hotb[:, 0], start=True, stop=False)
                nc.tensor.matmul(m1[:, NE:2 * NE], trib[:], hotb[:, 1], start=False, stop=True)
                nc.tensor.matmul(m1[:, 2 * NE:3 * NE], onesb[:], hotb[:, 0], start=True, stop=False)
                nc.tensor.matmul(m1[:, 2 * NE:3 * NE], onesb[:], hotb[:, 1], start=False, stop=True
                                 ).then_inc(rk_filled, 1)

            first = Step(0, 0, 0, 0, 0)
            for n in range(tiles):
                maximum(first, n)
            turn_maxima(first)
            for n in range(ahead):
                maximum(Step(1, 1, 0, 1, 1), n)

            def step(st):
                nxt = Step(st.s + 1, 1 - st.par, st.half + st.par, st.low + 1, st.high + 1)
                n = 0

                def then(piece, *args):
                    piece(*args)
                    more_maxima()

                def weigh_between(st, g):
                    for c in range(chunks):
                        weigh(st, g, c)
                        if c < 2:
                            more_maxima()

                def more_maxima():
                    nonlocal n
                    following_maximum(maximum, st, n)
                    n += 1

                for pair in range(H // 2):
                    if pair == 6 and not cross and st.before(B - 1):
                        turn_maxima(nxt)
                    then(scores, st, 2 * pair)
                    then(scores, st, 2 * pair + 1)
                    if cross:
                        scores_context(st, pair)
                    if pair == 0:
                        for t in range(TT):
                            for a in range(PAIRS):
                                tail(project, st, t, a)
                                if cross:
                                    more_maxima()
                                    if a == 0:
                                        more_maxima()
                    if pair == 2:
                        weigh_between(st, 0)
                    if pair == 4:
                        then(tail, turn_x, st)
                        weigh_between(st, 1)
                        then(tail, logits if cross else project_q, st)
                    if pair == 5 and not cross:
                        tail(project_k, st)
                    if pair == 6 and not cross:
                        for c in range(chunks):
                            weigh(st, 2, c)
                if cross:
                    if st.before(B - 1):
                        turn_maxima(nxt)
                    tail(ranks, st)
                    weigh_between(st, 2)
                    weigh_between(st, 3)
                else:
                    tail(project_v, st)
                    for c in range(chunks):
                        weigh(st, 3, c)

            steps(pe, step)
            last = Step(B - 1, 1, B // 2 - 1, B - 1, B - 1)
            for t in range(TT):
                for a in range(PAIRS):
                    project(last, t, a)
            turn_x(last)
            if cross:
                logits(last)
                ranks(last)
            else:
                project_q(last)
                project_k(last)
                project_v(last)

        @block.scalar
        def _(act):
            chain = Chain(act, act_seq)
            nc.scalar.preload_act_table_set("natural_log_exp_and_others")

            def probabilities(st, pair):
                g = pair // 2
                if pair % 2 == 0 and (st.since(1) or g >= 2):
                    act.wait_ge(pv_filled, st.s * UNITS + (g - 1))
                for e in range(2):
                    h = pair * 2 + e
                    act.wait_ge(st_filled, st.s * H + (h + 1))
                    nc.scalar.activation(pm[:, g % 2, h % HU], st_bank[e][:, 0:wide], ACT.Exp,
                                         scale=SCALE).then_inc(st_drained, 1)
                if cross:
                    act.wait_ge(tl_filled, st.s * (H // 2) + (pair + 1))
                    nc.scalar.activation(pt[:, g % 2, pair % 2 * 2:pair % 2 * 2 + 2], tl_bank[0:NCTX].rearrange(
                        "p (e t) -> p e t", e=2), ACT.Exp, scale=SCALE).then_inc(tl_drained, 1)

            def drain_maxima(st):
                act.wait_ge(nm_filled, st.s + 1)
                if st.since(2):
                    act.wait_ge(nm_loaded[st.par], st.half * 48)
                nc.scalar.copy(nmT[:, st.par], mx_bank[0:3 * H, 0:N // 2].bitcast(bf16)).then_inc(nm_drained, 1)

            def drain_x(st):
                act.wait_ge(tr_filled, st.s + 1)
                if st.since(1):
                    act.wait_ge(lg_filled if cross else v_filled, st.s)
                nc.scalar.copy(xnT[:].rearrange("p k t -> p (k t)"), m1[:]).then_inc(tr_drained, 1)

            def high_q(st):
                if st.since(1):
                    act.wait_ge(p_stored, st.s * 48)
                act.wait_ge(q_filled, st.s + 1)
                nc.scalar.copy(planes[:, 0, kept_at(0, 0)], m0[:]).then_inc(high_ready, 1)

            def high_k(st):
                act.wait_ge(k_filled, st.s + 1)
                nc.scalar.copy(planes[:, 1, kept_at(1, 0)], m1[:]).then_inc(high_ready, 1)

            def drain_v(st):
                if not st.since(1):
                    act.wait_ge(ones_set, 1)
                act.wait_ge(v_filled, st.s + 1)
                nc.scalar.copy(vo[:, :, :, 0:D], m0[:].rearrange("p (t h d) -> p t h d", t=TT, h=H)
                               ).then_inc(v_drained, 1)

            def gates(st):
                act.wait_ge(gap_ready, st.s + 1)
                nc.scalar.activation(egap[:], gap[:], ACT.Exp).then_inc(egap_ready, 1)

            def spread(st):
                act.wait_ge(stats_ready, st.s + 1)
                chain.link(nc.scalar.activation(lnv[:, st.par], mv[:, st.par, :, 1], ACT.Ln, bias=eps[:]))
                nc.scalar.activation(rstd[:, st.par], lnv[:, st.par], ACT.Exp, scale=-0.5).then_inc(rstd_ready, 1)

            def norm(st):
                act.wait_ge(shift_ready, st.s + 1)
                if st.since(2):
                    act.wait_ge(x_stored[st.par], st.half * 16)
                    if cross:
                        act.wait_ge(scattered[st.par], st.half * 64)
                for t in range(TT):
                    last = nc.scalar.activation(xn[:, st.par, t], m0[:, t * C:(t + 1) * C], ACT.Identity,
                                                bias=shift[:, st.par, t:t + 1], scale=newton[:, st.par, t:t + 1])
                last.then_inc(xn_ready, 1)

            drain_maxima(Step(0, 0, 0, 0, 0))

            def step(st):
                for pair in range(H // 2):
                    if pair == 6 and not cross and st.before(B - 1):
                        drain_maxima(Step(st.s + 1, 1 - st.par, st.half + st.par, st.low + 1, st.high + 1))
                    if pair == 6 and not cross:
                        tail(high_k, st)
                    probabilities(st, pair)
                    if pair == 1:
                        tail(spread, st)
                    if pair == 3:
                        tail(norm, st)
                    if pair == 4:
                        tail(drain_x, st)
                    if pair == (6 if cross else 4):
                        tail(gates if cross else high_q, st)
                    if pair == 7 and not cross:
                        tail(drain_v, st)
                if cross and st.before(B - 1):
                    drain_maxima(Step(st.s + 1, 1 - st.par, st.half + st.par, st.low + 1, st.high + 1))

            steps(act, step, chain=chain, per_pair=2)
            last = Step(B - 1, 1, B // 2 - 1, B - 1, B - 1)
            spread(last)
            norm(last)
            drain_x(last)
            if cross:
                gates(last)
            else:
                high_q(last)
                high_k(last)
                drain_v(last)

        @block.vector
        def _(dve):
            chain = Chain(dve, dve_seq)
            if not cross:
                nc.vector.memset(vo[:, :, :, D:], 1.0).then_inc(ones_set, 1)

            def maximum(st, n):
                if n == 0 and st.since(2):
                    dve.wait_ge(nmp_ready, st.s - 1)
                dve.wait_ge(sm_filled, st.s * tiles + (n + 1))
                if cross:
                    nc.vector.reduce_max(nm[:, st.par, n // TT, n % TT:n % TT + 1], sm_bank[n % 2][:, 0:NK], AX.X,
                                         negate=True).then_inc(sm_drained, 1)
                else:
                    nc.vector.reduce_max(nm[:, st.par, n], sm_bank[n % 2][:, 0:TT * WIN].rearrange(
                        "p (t n) -> p t n", t=TT), AX.X, negate=True).then_inc(sm_drained, 1)

            def turn_out(st, g):
                dve.wait_ge(pv_filled, st.s * UNITS + (g + 1))
                nc.vector.transpose(turned[:, g % 2], pv_bank[:, 0:N]).then_inc(pv_drained, 1)

            def blocks(a):
                return a.rearrange("p (b r) -> p b r", r=32)

            def invert(st, g):
                dve.wait_ge(pv_drained, st.s * UNITS + (g + 1))
                chain.mark(nc.vector.reciprocal(rden[:, g % 2], blocks(turned[:, g % 2])[:, :, D:D + 1]))

            def divide(st, g):
                chain.wait()
                at = g % 2 * D
                chain.mark(nc.vector.tensor_tensor(blocks(joined[:])[:, :, at:at + D],
                                                   blocks(turned[:, g % 2])[:, :, 0:D], rden[:, g % 2].to_broadcast([P, N // 32, D]), ALU.mult))

            def turn_back(st, g):
                chain.wait(apart=True)
                if g == 1 and st.since(1):
                    dve.wait_ge(op_filled, st.s)
                    alone(dve)
                nc.vector.transpose(on[:, g // 2], joined[:]).then_inc(on_ready, 1)

            def statistics(st):
                dve.wait_ge(op_filled, st.s + 1)
                alone(dve)
                for t in range(TT):
                    last = nc.vector.bn_stats(stats[:, t], m0[:, t * C:(t + 1) * C])
                chain.mark(last)

            def collect(st):
                chain.wait(apart=True)
                for t in range(TT):
                    last = nc.vector.bn_aggr(mv[:, st.par, t], stats[:, t])
                last.then_inc(stats_ready, 1)

            def refine(st, n):
                r, t1, mean, var = rstd[:, st.par], newton[:, st.par], mv[:, st.par, :, 0], mv[:, st.par, :, 1]
                if n == 0:
                    dve.wait_ge(rstd_ready, st.s + 1)
                    if st.since(2):
                        dve.wait_ge(xn_ready, st.s - 1)
                    chain.mark(nc.vector.tensor_tensor(t1, r, r, ALU.mult))
                    return
                chain.wait()
                if n == 1:
                    chain.mark(nc.vector.scalar_tensor_tensor(t1, var, EPS, t1, ALU.add, ALU.mult))
                elif n == 2:
                    chain.mark(nc.vector.tensor_scalar(t1, t1, -0.5, 1.5, ALU.mult, ALU.add))
                elif n == 3:
                    chain.mark(nc.vector.tensor_tensor(t1, t1, r, ALU.mult))
                else:
                    nc.vector.scalar_tensor_tensor(shift[:, st.par], mean, -1.0, t1, ALU.mult, ALU.mult
                                                   ).then_inc(shift_ready, 1)

            def residue(st, b, out):
                dve.wait_ge(high_ready, st.s * 2 + (b + 1))
                if st.since(1):
                    dve.wait_ge(planes_ready, st.s * 2)
                nc.vector.tensor_tensor(res[:, b], out[:], planes[:, b, kept_at(b, 0)], ALU.subtract
                                        ).then_inc(res_ready, 1)

            def residue_q(st):
                residue(st, 0, m0)

            def residue_k(st):
                residue(st, 1, m1)

            def choose(st, n):
                if n == 0:
                    dve.wait_ge(lg_filled, st.s + 1)
                    nc.vector.tensor_tensor(logit[:].rearrange("p t e -> p (t e)"), m0[:, 0:TT * NE],
                                            rb[:].rearrange("p t e -> p (t e)"), ALU.add).then_inc(lg_drained, 1)
                elif n == 1:
                    dve.wait_ge(lg_drained, st.s + 1)
                    alone(dve)
                    for t in range(TT):
                        last = nc.vector.max(top[:, t], logit[:, t])
                    chain.mark(last)
                elif n == 2:
                    chain.wait(apart=True)
                    for t in range(TT):
                        last = nc.vector.max_index(topi[:, t], top[:, t], logit[:, t])
                    chain.mark(last)
                elif n == 3:
                    chain.wait()
                    nc.vector.tensor_tensor(gap[:], top[:, :, 1], top[:, :, 0], ALU.subtract).then_inc(gap_ready, 1)
                    chain.mark(nc.vector.tensor_copy(idxf[:], topi[:, :, 0:2]))
                elif n == 4:
                    chain.wait()
                    chain.mark(nc.vector.tensor_tensor(
                        hot[:], iota4[:], idxf[:].rearrange("p t k -> p (t k)").unsqueeze(2).to_broadcast(
                            [P, 2 * TT, NE]), ALU.is_equal))
                else:
                    chain.wait()
                    hv = hot[:].rearrange("p (t k) e -> p t k e", t=TT)
                    nc.vector.tensor_tensor(hotb[:], hv[:, :, 0], hv[:, :, 1], ALU.add).then_inc(hot_ready, 1)

            def weights(st, n):
                if n == 0:
                    dve.wait_ge(egap_ready, st.s + 1)
                    chain.mark(nc.vector.tensor_scalar(oneg[:], egap[:], 1.0, None, ALU.add))
                elif n == 1:
                    chain.wait()
                    chain.mark(nc.vector.reciprocal(gate[:, 0], oneg[:]))
                else:
                    chain.wait()
                    chain.link(nc.vector.tensor_tensor(gate[:, 1], egap[:], gate[:, 0], ALU.mult))
                    nc.vector.tensor_copy(kept["gate"][:, bass.ds(st.s * 2 * TT, 2 * TT)],
                                          gate[:].rearrange("p k t -> p (k t)"))

            def assign(st, n):
                if n == 0:
                    dve.wait_ge(rk_filled, st.s + 1)
                    if st.since(1):
                        dve.wait_ge(rk_drained, st.s)
                    chain.mark(nc.vector.tensor_tensor(
                        place[:], m1[:, 0:TT * NE].rearrange("p (t e) -> p t e", t=TT),
                        base[:].unsqueeze(1).to_broadcast([P, TT, NE]), ALU.add))
                elif n == 1:
                    chain.wait()
                    nc.vector.tensor_tensor(base[:], m1[:, TT * NE:(TT + 1) * NE], base[:], ALU.add
                                            ).then_inc(rk_drained, 1)
                    chain.mark(nc.vector.tensor_tensor(
                        place[:], place[:], const[:, REGION:REGION + NE].unsqueeze(1).to_broadcast([P, TT, NE]),
                        ALU.add))
                elif n == 2:
                    chain.wait()
                    for t in range(TT):
                        last = nc.vector.tensor_tensor(pick[:, 2 * t:2 * t + 2], hot[:, 2 * t:2 * t + 2],
                                                       place[:, t:t + 1].to_broadcast([P, 2, NE]), ALU.mult)
                    chain.mark(last)
                elif n == 3:
                    chain.wait()
                    chain.mark(nc.vector.reduce_sum(slotf[:], pick[:], AX.X))
                else:
                    chain.wait()
                    if st.since(2):
                        dve.wait_ge(scattered[st.par], st.half * 64)
                    nc.vector.tensor_copy(kept["slot"][:, bass.ds(st.s * 2 * TT, 2 * TT)], slotf[:])
                    nc.vector.tensor_copy(slot[:, st.par], slotf[:]).then_inc(slot_ready, 1)

            first = Step(0, 0, 0, 0, 0)
            for n in range(tiles):
                maximum(first, n)
            for n in range(ahead):
                maximum(Step(1, 1, 0, 1, 1), n)

            def step(st):
                if cross:
                    due = [(8, tail, statistics, st), (9, tail, collect, st),
                           (11, tail, refine, st, 0), (12, tail, refine, st, 1), (13, tail, refine, st, 2),
                           (14, tail, refine, st, 3), (14, tail, refine, st, 4),
                           (15, turn_out, st, 0), (16, invert, st, 0), (17, divide, st, 0),
                           (22, tail, choose, st, 0), (23, tail, choose, st, 1), (24, tail, choose, st, 2),
                           (25, tail, choose, st, 3), (26, tail, choose, st, 4), (26, tail, choose, st, 5),
                           (26, turn_out, st, 1), (27, invert, st, 1), (28, divide, st, 1), (28, turn_back, st, 1),
                           (30, turn_out, st, 2), (30, tail, assign, st, 0), (30, invert, st, 2),
                           (30, tail, assign, st, 1), (31, divide, st, 2), (31, tail, assign, st, 2),
                           (32, tail, assign, st, 3), (32, tail, weights, st, 0), (32, tail, assign, st, 4),
                           (32, tail, weights, st, 1), (32, tail, weights, st, 2)]
                else:
                    due = [(2, tail, statistics, st), (3, tail, collect, st),
                           (6, tail, refine, st, 0), (7, tail, refine, st, 1), (8, tail, refine, st, 2),
                           (8, tail, refine, st, 3), (8, tail, refine, st, 4),
                           (10, turn_out, st, 0), (11, invert, st, 0), (12, divide, st, 0),
                           (16, turn_out, st, 1), (16, tail, residue_q, st), (16, invert, st, 1),
                           (16, divide, st, 1), (16, turn_back, st, 1), (16, tail, residue_k, st),
                           (16, turn_out, st, 2), (16, invert, st, 2), (16, divide, st, 2)]
                if cross:
                    due = [(0, tail, turn_out, st, 3), (1, tail, invert, st, 3), (2, tail, divide, st, 3),
                           (2, tail, turn_back, st, 3)] + due
                else:
                    due += [(16, piece, st, 3) for piece in (turn_out, invert, divide, turn_back)]
                n = 0
                for at, what, *args in due:
                    while n < at:
                        following_maximum(maximum, st, n)
                        n += 1
                    what(*args)

            steps(dve, step, chain=chain, per_pair=2 * (8 + 1 + 4 + (4 + 3 + 4 if cross else 0)))
            last = Step(B - 1, 1, B // 2 - 1, B - 1, B - 1)
            if cross:
                for piece in (turn_out, invert, divide, turn_back):
                    piece(last, UNITS - 1)
            statistics(last)
            collect(last)
            for n in range(5):
                refine(last, n)
            if cross:
                for n in range(6):
                    choose(last, n)
                for n in range(3):
                    weights(last, n)
                for n in range(5):
                    assign(last, n)
            else:
                residue_q(last)
                residue_k(last)

        @block.gpsimd
        def _(pool):
            chain = Chain(pool, pool_seq)

            def split_maxima(st):
                pool.wait_ge(sm_drained, st.s * tiles + tiles)
                if st.since(2):
                    pool.wait_ge(nm_filled, st.s - 1)
                alone(pool)
                v = nm[:, st.par].rearrange("p h t -> p t h")
                chain.link(nc.gpsimd.tensor_copy(nmp[:, st.par, :, 0], v))
                chain.link(nc.gpsimd.tensor_tensor(nmr[:, st.par], v, nmp[:, st.par, :, 0], ALU.subtract), apart=True)
                chain.link(nc.gpsimd.tensor_copy(nmp[:, st.par, :, 1], nmr[:, st.par]))
                nc.gpsimd.tensor_tensor(nmp[:, st.par, :, 2], nmr[:, st.par], nmp[:, st.par, :, 1],
                                        ALU.subtract).then_inc(nmp_ready, 1)

            def low(st):
                for b in range(2):
                    pool.wait_ge(res_ready, st.s * 2 + (b + 1))
                    if st.since(1) and b == 0:
                        pool.wait_ge(p_stored, st.s * 48)
                    alone(pool)
                    chain.link(nc.gpsimd.tensor_copy(planes[:, b, kept_at(b, 1)], res[:, b]))
                    nc.gpsimd.tensor_tensor(planes[:, b, kept_at(b, 2)], res[:, b], planes[:, b, kept_at(b, 1)],
                                            ALU.subtract
                                            ).then_inc(planes_ready, 1)

            def scatter(st):
                pool.wait_ge(slot_ready, st.s + 1)
                alone(pool)
                for t in range(TT):
                    for k in range(2):
                        pool.indirect_dma_start(
                            out=hbm["xs"], out_offset=bass.IndirectOffsetOnAxis(
                                ap=slot[:, st.par, 2 * t + k:2 * t + k + 1], axis=0),
                            in_=xn[:, st.par, t], in_offset=None).then_inc(scattered[st.par], 16)

            def add_bias(st):
                pool.wait_ge(rest_loaded[st.par], (st.half + 1) * (3 if cross else 2) * 16)
                alone(pool)
                nc.gpsimd.tensor_tensor(resid[:, st.par], resid[:, st.par], bias[:], ALU.add).then_inc(resid_ready, 1)

            split_maxima(Step(0, 0, 0, 0, 0))

            def step(st):
                add_bias(st)
                if st.before(B - 1):
                    split_maxima(Step(st.s + 1, 1 - st.par, st.half + st.par, st.low + 1, st.high + 1))
                tail(scatter if cross else low, st)

            steps(pool, step, chain=chain, per_pair=6 if cross else 10)
            last = Step(B - 1, 1, B // 2 - 1, B - 1, B - 1)
            if cross:
                scatter(last)
                for par in range(2):
                    pool.wait_ge(scattered[par], 64 * B // 2)
            else:
                low(last)


def experts(nc, hbm, kept):
    fp32, fp32r, i32 = mybir.dt.float32, mybir.dt.float32r, mybir.dt.int32
    ALU, ACT, AX = mybir.AluOpType, mybir.ActivationFunctionType, mybir.AxisListType
    ctx = ExitStack()
    with ctx:
        def sb(name, shape, dt=fp32):
            return ctx.enter_context(nc.sbuf_tensor("e_" + name, shape, dt))

        def sem(name):
            return ctx.enter_context(nc.semaphore("e_" + name))

        def bank(name):
            return ctx.enter_context(nc.psum_tensor("e_" + name, [P, 512], fp32))

        const = kept["const"]
        zeros = sb("zeros", [P, TMT, C])
        gu_raw, wd_raw = kept["gu_raw"], kept["wd_raw"]
        gu_hi = sb("gu_hi", [P, 2, KT, F], fp32r)
        gu_lo = sb("gu_lo", [P, 2, KT, F], fp32r)
        wd = sb("wd", [P, 2, FM, 2, C], fp32r)
        xs = sb("xs", [P, 2, TMT, C])
        x_hi, x_lo = sb("x_hi", [P, KT, TM], fp32r), sb("x_lo", [P, KT, TM], fp32r)
        silu = sb("silu", [P, 2, TM])
        h = sb("h", [P, 2, TM])
        h_hi, h_lo = sb("h_hi", [P, FM, TM], fp32r), sb("h_lo", [P, FM, TM], fp32r)
        cross = sb("cross", [P, 2, C])
        y = sb("y", [P, 2, TMT, C])
        over = sb("over", [P, NE, LEVELS])
        tiles = sb("tiles", [P, NE])
        below = sb("below", [P, NE, NE])
        ends = sb("ends", [P, NE])
        skip = sb("skip", [P, NE])
        n = B * TT * 2
        behind = sb("behind", [P, n, NE - 1])
        gaps = sb("gaps", [P, n])
        past = sb("past", [1, NTILE, NE])
        past2 = sb("past2", [1, NTILE, NE])
        expf = sb("expf", [1, NTILE])
        rowf = sb("rowf", [1, NTILE])
        expert_of = sb("expert_of", [1, NTILE], i32)
        row_of = sb("row_of", [1, NTILE], i32)
        tail_of = sb("tail_of", [1, NE], i32)
        tailf = sb("tailf", [1, NE])
        g_bank = [bank(f"g{i}") for i in range(2)]
        u_bank = [bank(f"u{i}") for i in range(2)]
        y_bank = [bank(f"y{i}") for i in range(2)]
        t_bank = [bank(f"t{i}") for i in range(2)]
        map_ready, first_padded, padded = sem("map_ready"), sem("first_padded"), sem("padded")
        zeros_set, tail_ready = sem("zeros_set"), sem("tail_ready")
        gu_loaded, wd_loaded = kept["gu_loaded"], kept["wd_loaded"]
        xs_loaded = [sem(f"xs_loaded{i}") for i in range(2)]
        gu_high, gu_split = sem("gu_high"), sem("gu_split")
        wd_high, wd_split = sem("wd_high"), sem("wd_split")
        x_filled, x_high, x_split = sem("x_filled"), sem("x_high"), sem("x_split")
        gu_filled, silu_ready = sem("gu_filled"), sem("silu_ready")
        h_ready, h_high, h_split = sem("h_ready"), sem("h_high"), sem("h_split")
        y_filled, cross_ready, y_ready = sem("y_filled"), sem("cross_ready"), sem("y_ready")
        y_stored = [sem(f"y_stored{i}") for i in range(2)]
        dve_seq = sem("dve_seq")
        block = ctx.enter_context(nc.Block())
        DM = FM // WDQ

        def slots(name, row):
            return hbm[name][bass.ds(row, TM)].rearrange("(t p) n -> p t n", p=P)

        def following(st):
            return Step(st.s + 1, 1 - st.par, st.half + st.par, st.low + 1, st.high + 1)

        def y_place(st, t):
            return (t + st.par * TMT) % 2

        @block.sync
        def _(sp):
            sp.wait_ge(zeros_set, 1)
            sp.wait_ge(tail_ready, 1)

            def pad(experts, padded):
                for e in experts:
                    row = sp.value_load(tail_of[0:1, e:e + 1], min_val=0, max_val=SPARE - TM)
                    sp.dma_start(slots("xs", row), zeros[:]).then_inc(padded, 16)

            pad(range(1), first_padded)
            pad(range(1, 2), padded)
            sp.wait_ge(first_padded, 16)
            sp.dma_start(xs[:, 0], slots("xs", 0)).then_inc(xs_loaded[0], 16)
            sp.wait_ge(map_ready, 1)

            def store(st):
                sp.wait_ge(y_ready, st.s * TMT + TMT)
                alone(sp)
                sp.dma_start(slots("ys", st.s * TM), y[:, st.par]).then_inc(y_stored[st.par], 16)

            def load(st):
                if st.high < 1:
                    return
                e = sp.value_load(expert_of[0:1, bass.ds(st.s, 1)], min_val=0, max_val=NE - 1)
                if st.since(2):
                    sp.wait_ge(gu_split, st.s * FM - FM)
                for i, name in enumerate(("wg", "wu")):
                    sp.dma_start(gu_raw[:, st.par, i].rearrange("p k n -> p (k n)"), hbm[name][bass.ds(e, 1)].rearrange(
                        "a p n -> p (a n)")).then_inc(gu_loaded[st.par], 16)
                if st.high < 2:
                    sp.dma_start(slots("xs", SPARE), zeros[:]).then_inc(padded, 16)
                    pad(range(2, NE), padded)
                    sp.wait_ge(padded, NE * 16)
                if st.since(2):
                    sp.wait_ge(x_filled, st.s - 1)
                    alone(sp)
                row = sp.value_load(row_of[0:1, bass.ds(st.s, 1)], min_val=0, max_val=NSLOT - TM)
                sp.dma_start(xs[:, st.par], slots("xs", row)).then_inc(xs_loaded[st.par], 16)
                if st.since(1):
                    sp.wait_ge(wd_split, st.s * WDQ)
                sp.dma_start(wd_raw[:].rearrange("p k n -> p (k n)"), hbm["wd"][bass.ds(e, 1)].rearrange(
                    "a p n -> p (a n)")).then_inc(wd_loaded, 16)
                if st.since(2):
                    store(Step(st.s - 2, st.par, st.half - 1, st.low - 2, st.high - 2))

            steps(sp, load, total=NTILE, front=2, back=1)
            for s in range(NTILE - 2, NTILE):
                store(Step(s, s % 2, s // 2, s, s))
            for par in range(2):
                sp.wait_ge(y_stored[par], ((NTILE + 1 - par) // 2) * 16)

        @block.tensor
        def _(pe):
            def turn(st):
                pe.wait_ge(xs_loaded[st.par], st.half * 16 + 16)
                for k in range(KT):
                    for t in range(TMT):
                        last = nc.tensor.transpose(t_bank[k][:, t * P:(t + 1) * P],
                                                   xs[:, st.par, t, k * P:(k + 1) * P], const[:, IDENT:IDENT + P])
                last.then_inc(x_filled, 1)

            turn(Step(0, 0, 0, 0, 0))

            def tile(st):
                pe.wait_ge(x_split, st.s + 1)
                for m in range(FM):
                    if st.since(1) or m >= 2:
                        pe.wait_ge(h_ready, st.s * FM + (m - 1))
                    pe.wait_ge(gu_split, st.s * FM + (m + 1))
                    for i, out in enumerate((g_bank, u_bank)):
                        for k in range(KT):
                            hi, lo = (a[:, i, k, m * P:(m + 1) * P] for a in (gu_hi, gu_lo))
                            nc.tensor.matmul(out[m % 2][:, 0:TM], hi, x_hi[:, k], start=(k == 0), stop=False)
                            nc.tensor.matmul(out[m % 2][:, 0:TM], hi, x_lo[:, k], start=False, stop=False)
                            last = nc.tensor.matmul(out[m % 2][:, 0:TM], lo, x_hi[:, k], start=False,
                                                    stop=(k == KT - 1))
                    last.then_inc(gu_filled, 1)
                if st.before(NTILE - 1):
                    turn(following(st))
                pe.wait_ge(wd_split, st.s * WDQ + WDQ)
                for t in range(TMT):
                    if st.since(1) or t >= 2:
                        pe.wait_ge(y_ready, st.s * TMT + (t - 1))
                    out = y_bank[y_place(st, t)]
                    for m in range(FM):
                        if t == 0:
                            pe.wait_ge(h_split, st.s * FM + (m + 1))
                        hi, lo = (a[:, m, t * P:(t + 1) * P] for a in (h_hi, h_lo))
                        for high in (True, False) if m < FM - 1 else (False, True):
                            if high:
                                last = nc.tensor.matmul(out[:], hi, wd[:, st.par, m].rearrange("p a n -> p (a n)"),
                                                        start=(m == 0), stop=(m == FM - 1))
                            else:
                                nc.tensor.matmul(out[:, 0:C], lo, wd[:, st.par, m, 0], start=False, stop=False)
                    last.then_inc(y_filled, 1)

            steps(pe, tile, total=NTILE, front=2, back=1)

        @block.scalar
        def _(act):
            def gu_part(st, m):
                if m == 0:
                    act.wait_ge(gu_loaded[st.par], st.half * 32 + 32)
                for i in range(2):
                    last = nc.scalar.copy(gu_hi[:, i, :, m * P:(m + 1) * P], gu_raw[:, st.par, i, :, m * P:(m + 1) * P])
                last.then_inc(gu_high, 1)

            def wd_part(st, q):
                if q == 0:
                    act.wait_ge(wd_loaded, st.s * 16 + 16)
                nc.scalar.copy(wd[:, st.par, q * DM:(q + 1) * DM, 0], wd_raw[:, q * DM:(q + 1) * DM]
                               ).then_inc(wd_high, 1)

            def x_part(st):
                act.wait_ge(x_filled, st.s + 1)
                for k in range(KT):
                    last = nc.scalar.copy(x_hi[:, k], t_bank[k][:, 0:TM])
                last.then_inc(x_high, 1)

            first = Step(0, 0, 0, 0, 0)
            for m in range(FM):
                gu_part(first, m)
            x_part(first)
            for q in range(WDQ):
                wd_part(first, q)

            def tile(st):
                for m in range(FM):
                    act.wait_ge(gu_filled, st.s * FM + (m + 1))
                    if st.since(1) or m >= 2:
                        act.wait_ge(h_ready, st.s * FM + (m - 1))
                    nc.scalar.activation(silu[:, m % 2], g_bank[m % 2][:, 0:TM], ACT.Silu).then_inc(silu_ready, 1)
                    if st.before(NTILE - 1):
                        gu_part(following(st), m)
                    act.wait_ge(h_ready, st.s * FM + (m + 1))
                    nc.scalar.copy(h_hi[:, m], h[:, m % 2]).then_inc(h_high, 1)
                if st.before(NTILE - 1):
                    x_part(following(st))
                    for q in range(WDQ):
                        wd_part(following(st), q)
                for t in range(TMT):
                    act.wait_ge(y_filled, st.s * TMT + (t + 1))
                    nc.scalar.copy(cross[:, y_place(st, t)], y_bank[y_place(st, t)][:, C:]).then_inc(cross_ready, 1)

            steps(act, tile, total=NTILE, front=2, back=1)

        @block.vector
        def _(dve):
            chain = Chain(dve, dve_seq)
            count = kept["count"][:]
            nc.vector.memset(zeros[:], 0.0).then_inc(zeros_set, 1)

            def table(at, *shape):
                n = 1
                for x in shape:
                    n *= x
                v = const[:, at:at + n]
                return v.rearrange("p (a b) -> p a b", b=shape[-1]) if len(shape) == 2 else v

            chain.link(nc.vector.tensor_tensor(tailf[:], kept["count"][0:1], table(REGION, NE)[0:1], ALU.add))
            nc.vector.tensor_copy(tail_of[:], tailf[:]).then_inc(tail_ready, 1)
            chain.link(nc.vector.tensor_tensor(over[:], count.unsqueeze(2).to_broadcast([P, NE, LEVELS]),
                                               table(LEVEL, NE, LEVELS), ALU.is_gt))
            chain.link(nc.vector.reduce_sum(tiles[:], over[:], AX.X))
            chain.link(nc.vector.tensor_tensor(below[:], tiles[:].unsqueeze(1).to_broadcast([P, NE, NE]),
                                               table(LOWER, NE, NE), ALU.mult))
            chain.link(nc.vector.reduce_sum(ends[:], below[:], AX.X))
            chain.link(nc.vector.tensor_scalar(skip[:], tiles[:], -float(TM), float(CAP), ALU.mult, ALU.add))
            chain.link(nc.vector.tensor_tensor(past[:], table(TILE, NTILE, NE)[0:1],
                                               ends[0:1].unsqueeze(1).to_broadcast([1, NTILE, NE]), ALU.is_ge))
            chain.link(nc.vector.reduce_sum(expf[:], past[:], AX.X))
            chain.link(nc.vector.tensor_tensor(past2[:], past[:],
                                               skip[0:1].unsqueeze(1).to_broadcast([1, NTILE, NE]), ALU.mult))
            chain.link(nc.vector.reduce_sum(rowf[:], past2[:], AX.X))
            chain.link(nc.vector.tensor_scalar(expf[:], expf[:], float(NE - 1), None, ALU.min))
            chain.link(nc.vector.tensor_copy(expert_of[:], expf[:]))
            chain.link(nc.vector.scalar_tensor_tensor(rowf[:], table(TILE, NTILE, NE)[0:1, :, 0], float(TM), rowf[:],
                                                      ALU.mult, ALU.add))
            chain.link(nc.vector.tensor_scalar(rowf[:], rowf[:], float(SPARE), None, ALU.min))
            nc.vector.tensor_copy(row_of[:], rowf[:]).then_inc(map_ready, 1)

            def gu_part(st, m):
                dve.wait_ge(gu_high, st.s * FM + (m + 1))
                for i in range(2):
                    cut = slice(m * P, (m + 1) * P)
                    last = nc.vector.tensor_tensor(gu_lo[:, i, :, cut], gu_raw[:, st.par, i, :, cut],
                                                   gu_hi[:, i, :, cut], ALU.subtract)
                last.then_inc(gu_split, 1)

            def wd_part(st, q):
                dve.wait_ge(wd_high, st.s * WDQ + (q + 1))
                cut = slice(q * DM, (q + 1) * DM)
                nc.vector.tensor_tensor(wd[:, st.par, cut, 1], wd_raw[:, cut], wd[:, st.par, cut, 0], ALU.subtract
                                        ).then_inc(wd_split, 1)

            def x_part(st):
                dve.wait_ge(x_high, st.s + 1)
                for k in range(KT):
                    last = nc.vector.tensor_tensor(x_lo[:, k], t_bank[k][:, 0:TM], x_hi[:, k], ALU.subtract)
                last.then_inc(x_split, 1)

            first = Step(0, 0, 0, 0, 0)
            for m in range(FM):
                gu_part(first, m)
            x_part(first)
            for q in range(WDQ):
                wd_part(first, q)

            region = table(REGION, NE)
            chain.link(nc.vector.tensor_tensor(
                behind[:], kept["slot"][:].unsqueeze(2).to_broadcast([P, n, NE - 1]),
                region[:, 1:].unsqueeze(1).to_broadcast([P, n, NE - 1]), ALU.is_ge))
            chain.link(nc.vector.tensor_tensor(
                behind[:], behind[:], skip[:, 0:NE - 1].unsqueeze(1).to_broadcast([P, n, NE - 1]), ALU.mult))
            chain.link(nc.vector.reduce_sum(gaps[:], behind[:], AX.X))
            nc.vector.tensor_tensor(kept["slot"][:], kept["slot"][:], gaps[:], ALU.subtract)

            def tile(st):
                for m in range(FM):
                    dve.wait_ge(silu_ready, st.s * FM + (m + 1))
                    if st.since(1) or m >= 2:
                        dve.wait_ge(h_split, st.s * FM + (m - 1))
                    nc.vector.tensor_tensor(h[:, m % 2], u_bank[m % 2][:, 0:TM], silu[:, m % 2], ALU.mult
                                            ).then_inc(h_ready, 1)
                    if st.before(NTILE - 1):
                        gu_part(following(st), m)
                    dve.wait_ge(h_high, st.s * FM + (m + 1))
                    nc.vector.tensor_tensor(h_lo[:, m], h[:, m % 2], h_hi[:, m], ALU.subtract).then_inc(h_split, 1)
                if st.before(NTILE - 1):
                    x_part(following(st))
                    for q in range(WDQ):
                        wd_part(following(st), q)
                if st.since(2):
                    dve.wait_ge(y_stored[st.par], st.half * 16)
                for t in range(TMT):
                    dve.wait_ge(cross_ready, st.s * TMT + (t + 1))
                    nc.vector.tensor_tensor(y[:, st.par, t], y_bank[y_place(st, t)][:, 0:C],
                                            cross[:, y_place(st, t)], ALU.add).then_inc(y_ready, 1)

            steps(dve, tile, total=NTILE, front=2, back=1)


def combine(nc, hbm, kept):
    fp32, u32 = mybir.dt.float32, mybir.dt.uint32
    ALU, ACT = mybir.AluOpType, mybir.ActivationFunctionType
    ctx = ExitStack()
    with ctx:
        def sb(name, shape, dt=fp32):
            return ctx.enter_context(nc.sbuf_tensor("o_" + name, shape, dt))

        def sem(name):
            return ctx.enter_context(nc.semaphore("o_" + name))

        x = sb("x", [P, LANES, TT, C])
        picked = sb("picked", [P, LANES, TT, 2, C])
        slot = sb("slot", [P, LANES, TT * 2], u32)
        gate = sb("gate", [P, LANES, 2, TT])
        y = sb("y", [P, LANES, TT, C])
        out = sb("out", [P, LANES, TT, C])
        stats = sb("stats", [P, TT, 6])
        mv = sb("mv", [P, LANES, TT, 2])
        lnv = sb("lnv", [P, LANES, TT])
        rstd = sb("rstd", [P, LANES, TT])
        newton = sb("newton", [P, LANES, TT])
        shift = sb("shift", [P, LANES, TT])
        eps = sb("eps", [P, 1])
        eps_set = sem("eps_set")
        x_loaded = [sem(f"x_loaded{i}") for i in range(LANES)]
        gathered = [sem(f"gathered{i}") for i in range(LANES)]
        slot_ready, sum_ready, stats_ready = sem("slot_ready"), sem("sum_ready"), sem("stats_ready")
        rstd_ready, shift_ready, out_ready = sem("rstd_ready"), sem("shift_ready"), sem("out_ready")
        stored = [sem(f"stored{i}") for i in range(LANES)]
        dve_seq, act_seq = sem("dve_seq"), sem("act_seq")
        block = ctx.enter_context(nc.Block())

        def rows(name, st):
            return hbm[name][bass.ds(st.s, 1)].rearrange("a (t p) n -> p (a t) n", p=P)

        turns = {"front": LANES, "back": LANES, "lanes": LANES}

        def earlier(st, n):
            return Step(st.s - n, (st.par - n) % LANES, st.half - (1 if st.par < n else 0), st.low - n, st.high - n)

        @block.sync
        def _(sp):
            def step(st):
                if st.since(LANES):
                    sp.wait_ge(sum_ready, st.s - (LANES - 1))
                sp.dma_start(x[:, st.par], rows("x2", st)).then_inc(x_loaded[st.par], 16)
                if st.since(2):
                    store(earlier(st, 2))

            def store(st):
                sp.wait_ge(out_ready, st.s + 1)
                sp.dma_start(rows("out", st), out[:, st.par]).then_inc(stored[st.par], 16)

            steps(sp, step, **turns)
            for s in range(B - 2, B):
                store(Step(s, s % LANES, s // LANES, s, s))
            for par in range(LANES):
                sp.wait_ge(stored[par], 16 * B // LANES)

        @block.gpsimd
        def _(pool):
            def gather(st):
                pool.wait_ge(slot_ready, st.s + 1)
                if st.since(LANES):
                    pool.wait_ge(sum_ready, st.s - (LANES - 1))
                alone(pool)
                for t in range(TT):
                    for k in range(2):
                        pool.indirect_dma_start(
                            out=picked[:, st.par, t, k], out_offset=None, in_=hbm["ys"],
                            in_offset=bass.IndirectOffsetOnAxis(ap=slot[:, st.par, 2 * t + k:2 * t + k + 1], axis=0),
                        ).then_inc(gathered[st.par], 16)

            steps(pool, gather, **turns)

        @block.scalar
        def _(act):
            chain = Chain(act, act_seq)
            nc.scalar.preload_act_table_set("natural_log_exp_and_others")
            act.wait_ge(eps_set, 1)

            def spread(st):
                act.wait_ge(stats_ready, st.s + 1)
                chain.link(nc.scalar.activation(lnv[:, st.par], mv[:, st.par, :, 1], ACT.Ln, bias=eps[:]))
                nc.scalar.activation(rstd[:, st.par], lnv[:, st.par], ACT.Exp, scale=-0.5).then_inc(rstd_ready, 1)

            def norm(st):
                act.wait_ge(shift_ready, st.s + 1)
                if st.since(LANES):
                    act.wait_ge(stored[st.par], st.half * 16)
                for t in range(TT):
                    last = nc.scalar.activation(out[:, st.par, t], y[:, st.par, t], ACT.Identity,
                                                bias=shift[:, st.par, t:t + 1], scale=newton[:, st.par, t:t + 1])
                last.then_inc(out_ready, 1)

            def step(st):
                spread(st)
                if st.since(1):
                    norm(earlier(st, 1))

            steps(act, step, chain=chain, per_pair=LANES, **turns)
            norm(Step(B - 1, LANES - 1, B // LANES - 1, B - 1, B - 1))

        @block.vector
        def _(dve):
            chain = Chain(dve, dve_seq)
            nc.vector.memset(eps[:], EPS).then_inc(eps_set, 1)
            def address(st):
                nc.vector.tensor_copy(gate[:, st.par].rearrange("p k t -> p (k t)"),
                                      kept["gate"][:, bass.ds(st.s * 2 * TT, 2 * TT)])
                if st.since(LANES):
                    dve.wait_ge(gathered[st.par], st.half * 64)
                nc.vector.tensor_copy(slot[:, st.par], kept["slot"][:, bass.ds(st.s * 2 * TT, 2 * TT)]
                                      ).then_inc(slot_ready, 1)

            def add(st):
                dve.wait_ge(x_loaded[st.par], st.half * 16 + 16)
                dve.wait_ge(gathered[st.par], st.half * 64 + 64)
                dve.wait_ge(slot_ready, st.s + 1)
                if st.since(LANES):
                    dve.wait_ge(out_ready, st.s - (LANES - 1))
                for t in range(TT):
                    last = nc.vector.scalar_tensor_tensor(y[:, st.par, t], picked[:, st.par, t, 0],
                                                          gate[:, st.par, 0, t:t + 1], x[:, st.par, t],
                                                          ALU.mult, ALU.add)
                chain.link(last)
                for t in range(TT):
                    last = nc.vector.scalar_tensor_tensor(y[:, st.par, t], picked[:, st.par, t, 1],
                                                          gate[:, st.par, 1, t:t + 1], y[:, st.par, t],
                                                          ALU.mult, ALU.add)
                last.then_inc(sum_ready, 1)
                dve.wait_ge(sum_ready, st.s + 1)
                for t in range(TT):
                    last = nc.vector.bn_stats(stats[:, t], y[:, st.par, t])
                chain.link(last, apart=True)
                for t in range(TT):
                    last = nc.vector.bn_aggr(mv[:, st.par, t], stats[:, t])
                last.then_inc(stats_ready, 1)

            def refine(st):
                dve.wait_ge(rstd_ready, st.s + 1)
                r, t1, var = rstd[:, st.par], newton[:, st.par], mv[:, st.par, :, 1]
                chain.link(nc.vector.tensor_tensor(t1, r, r, ALU.mult))
                chain.link(nc.vector.scalar_tensor_tensor(t1, var, EPS, t1, ALU.add, ALU.mult))
                chain.link(nc.vector.tensor_scalar(t1, t1, -0.5, 1.5, ALU.mult, ALU.add))
                chain.link(nc.vector.tensor_tensor(t1, t1, r, ALU.mult))
                nc.vector.scalar_tensor_tensor(shift[:, st.par], mv[:, st.par, :, 0], -1.0, t1, ALU.mult, ALU.mult
                                               ).then_inc(shift_ready, 1)

            for s in range(2):
                address(Step(s, s, 0, s, s))

            def step(st):
                if st.before(B - 2):
                    address(Step(st.s + 2, (st.par + 2) % LANES, st.half + (st.par + 2) // LANES,
                                 st.low + 2, st.high + 2))
                add(st)
                if st.since(1):
                    refine(earlier(st, 1))

            steps(dve, step, chain=chain, per_pair=LANES * 6, **turns)
            refine(Step(B - 1, LANES - 1, B // LANES - 1, B - 1, B - 1))


def program(nc, hbm):
    fp32, bf16 = mybir.dt.float32, mybir.dt.bfloat16

    def scratch(name, shape, dt=fp32):
        hbm[name] = nc.dram_tensor("scratch_" + name, shape, dt, kind="Internal").ap()

    scratch("q1", [B, 3, C, N], bf16)
    scratch("k1", [B, 3, C, N], bf16)
    scratch("v1", [B, N, H * 2 * D])
    scratch("q2", [B, 3, C, N], bf16)
    scratch("k2", [B, 3, C, NK], bf16)
    scratch("v2", [B, N, H * 2 * D])
    scratch("x1", [B, N, C])
    scratch("x2", [B, N, C])
    scratch("xs", [NSLOT, C])
    scratch("ys", [NTILE * TM, C])
    with ExitStack() as ctx:
        routed = {name: ctx.enter_context(nc.sbuf_tensor(name + "s", [P, n], fp32))
                  for name, n in (("slot", B * TT * 2), ("gate", B * TT * 2), ("count", NE), ("const", NCONST))}
        routed.update(
            gu_raw=ctx.enter_context(nc.sbuf_tensor("gu_raw", [P, 2, 2, KT, F], fp32)),
            wd_raw=ctx.enter_context(nc.sbuf_tensor("wd_raw", [P, FM, C], fp32)),
            gu_loaded=[ctx.enter_context(nc.semaphore(f"gu_loaded{i}")) for i in range(2)],
            wd_loaded=ctx.enter_context(nc.semaphore("wd_loaded")))
        first = ctx.enter_context(ExitStack())

        def keep(name, shape, dt=fp32):
            return first.enter_context(nc.sbuf_tensor(name, shape, dt))

        kept = {
            "qs": keep("qs", [ROWS + 3, 2, H, N], bf16),
            "ks": keep("ks", [ROWS + 3, 2, H, NK], bf16),
            "va": keep("va", [P, 2, TT + 1, H, 2 * D]),
            "resid": keep("resid", [P, 2, TT, C]),
            "wp1": keep("wp1", [P, PAIRS, C]), "wp2": keep("wp2", [P, PAIRS, C]),
            "bp1": keep("bp1", [P, TT, C]), "bp2": keep("bp2", [P, TT, C]),
            "wx": keep("wx", [P, KT, 3 * C]),
            "identb": keep("identb", [P, P], bf16),
            "maskb": keep("maskb", [P, TT, WIN], bf16), "eps": keep("eps", [P, 1]),
            "rw": keep("rw", [P, KT, NE]), "rb": keep("rb", [P, TT, NE]),
            "trib": keep("trib", [P, P], bf16), "onesb": keep("onesb", [P, P], bf16),
            "iota4": keep("iota4", [P, 2 * TT, NE]), "loads": 2 + 2 * TT + 3 + TT,
        }
        kept.update(routed)
        for which in "12":
            kept["qk_loaded" + which] = [[ctx.enter_context(nc.semaphore(f"qk{which}_loaded{a}{b}"))
                                          for b in range(HALVES)] for a in range(2)]
            kept["rest_loaded" + which] = [ctx.enter_context(nc.semaphore(f"rest{which}_loaded{a}")) for a in range(2)]
        project_first(nc, hbm, kept)
        attention(nc, hbm, kept, cross=False)
        attention(nc, hbm, kept, cross=True)
        first.close()
        experts(nc, hbm, kept)
        combine(nc, hbm, kept)


def constants():
    import numpy as np
    p = np.arange(P)[:, None]
    out = np.zeros((P, NCONST), np.float32)
    out[:, IDENT:IDENT + P] = p == np.arange(P)
    out[:, UPPER:UPPER + P] = p < np.arange(P)
    for t in range(TT):
        apart = np.abs(t * P + p - (W0[t] + np.arange(WIN)))
        out[:, MASK + t * WIN:MASK + (t + 1) * WIN] = np.where(apart <= BAND, 0.0, MASKED)
    out[:, EXPERT:EXPERT + NE] = np.arange(NE)
    out[:, LEVEL:LEVEL + NE * LEVELS] = np.tile(np.arange(LEVELS) * TM, NE)
    out[:, LEVEL] = -1
    out[:, LOWER:LOWER + NE * NE] = (np.arange(NE)[:, None] >= np.arange(NE)).reshape(-1)
    out[:, TILE:TILE + NTILE * NE] = np.repeat(np.arange(NTILE), NE)
    out[:, REGION:REGION + NE] = np.arange(NE) * CAP
    return out


def kernel(x, ctx_2048, L0_attn_Wqkv, L0_attn_Wproj, L0_attn_bproj, L0_xattn_w_qkv, L0_xattn_w_proj,
           L0_xattn_b_proj, L0_ffn_router_w, L0_ffn_router_b, L0_ffn_gate_w, L0_ffn_up_w, L0_ffn_down_w):
    import numpy as np
    import concourse.bacc as bacc
    from concourse.bass_utils import run_bass_kernel_spmd

    def lay(a, *order):
        return np.ascontiguousarray(np.transpose(np.asarray(a), order))

    def heads_last(a, axis):
        shape = a.shape
        a = a.reshape(*shape[:axis], H, D, *shape[axis + 1:])
        return np.ascontiguousarray(np.swapaxes(a, axis, axis + 1)).reshape(shape)

    def qkv(a):
        return np.concatenate([heads_last(a[:, :C], 1), heads_last(a[:, C:2 * C], 1), a[:, 2 * C:]], axis=1)

    def project(a):
        return np.ascontiguousarray(a.reshape(PAIRS, 2, HU, D, C).transpose(2, 1, 3, 0, 4).reshape(P, PAIRS, C))

    def up(a):
        a = np.asarray(a).reshape(NE, F, KT, P)
        return np.ascontiguousarray(a.transpose(0, 3, 2, 1).reshape(NE, P, KT * F))

    def down(a):
        a = np.asarray(a).reshape(NE, C, FM, P)
        return np.ascontiguousarray(a.transpose(0, 3, 2, 1).reshape(NE, P, FM * C))

    arrays = {
        "x": np.ascontiguousarray(x), "xT": lay(x, 0, 2, 1),
        "ctx": np.ascontiguousarray(ctx_2048), "ckT": heads_last(np.transpose(np.asarray(ctx_2048)[:, :, :C], (0, 2, 1)), 1),
        "wqkv": qkv(np.asarray(L0_attn_Wqkv)), "wp1": project(np.asarray(L0_attn_Wproj)),
        "bp1": np.asarray(L0_attn_bproj).reshape(1, C),
        "wx": qkv(np.transpose(np.asarray(L0_xattn_w_qkv), (1, 0))), "wp2": project(lay(L0_xattn_w_proj, 1, 0)),
        "bp2": np.asarray(L0_xattn_b_proj).reshape(1, C),
        "rw": lay(L0_ffn_router_w, 1, 0), "rb": np.asarray(L0_ffn_router_b).reshape(1, NE),
        "wg": up(L0_ffn_gate_w), "wu": up(L0_ffn_up_w), "wd": down(L0_ffn_down_w),
        "const": constants(),
    }
    nc = bacc.Bacc("TRN2", target_bir_lowering=False, num_devices=1)
    hbm = {n: nc.dram_tensor("in_" + n, a.shape, mybir.dt.from_np(a.dtype), kind="ExternalInput").ap()
           for n, a in arrays.items()}
    hbm["out"] = nc.dram_tensor("out_x", [B, N, C], mybir.dt.float32, kind="ExternalOutput").ap()
    program(nc, hbm)
    r = run_bass_kernel_spmd(nc, [{"in_" + n: a for n, a in arrays.items()}], core_ids=[0])
    return r.results[0]["out_x"]
```
